# Optimizing a Trainium2 kernel written in Bass

```python
import numpy as np
import jax
import jax.numpy as jnp

def _softmax(x, axis=-1):
    return jax.nn.softmax(x, axis=axis)

def _gelu(x):
    return jax.nn.gelu(x, approximate=True)

def _silu(x):
    return jax.nn.silu(x)

def _sigmoid(x):
    return jax.nn.sigmoid(x)

def _layernorm(x, axis=-1, eps=1e-05):
    m = jnp.mean(x, axis=axis, keepdims=True)
    v = jnp.var(x, axis=axis, keepdims=True)
    return (x - m) / jnp.sqrt(v + eps)

def _scatter_add(tgt, idx, src, axis=0):
    return tgt.at[idx].add(src)

def _segment_sum(src, seg, n):
    return jax.ops.segment_sum(src, seg, n)
kernel_name = 'mk_decoder_postln_d1_seqx_r4_e5bc86'

def setup_inputs(seed: int=0):
    np.random.seed(seed)
    _w = jnp.asarray

    def _rec_inputs():
        import jax
        import jax.numpy as jnp
        _rk = jax.random.key(seed)
        x = 4.136e-05 + 0.9999 * jax.random.normal(jax.random.fold_in(_rk, 1), (4, 512, 512), jnp.float32)
        _lenS = 512 - jax.random.randint(jax.random.fold_in(_rk, 7), (4,), 0, max(1, 512 // 4) + 1, jnp.int32)
        _lenS2 = 512 - jax.random.randint(jax.random.fold_in(_rk, 8), (4,), 0, max(1, 512 // 4) + 1, jnp.int32)
        _ctx_1024P = jax.random.normal(jax.random.fold_in(_rk, 11), (4, 16, 256), jnp.float32)
        _ctx_1024c = jax.random.dirichlet(jax.random.fold_in(_rk, 511), 0.3 * jnp.ones((16,), jnp.float32), (4, 512))
        _ctx_1024t = jnp.einsum('bsk,bkd->bsd', _ctx_1024c, _ctx_1024P)
        _ctx_1024t = _ctx_1024t * jax.lax.rsqrt(jnp.mean(jnp.square(_ctx_1024t)) + 1e-12) * 0.953939
        ctx_1024 = -0.000292821 + 1.00034 * (_ctx_1024t + 0.3 * jax.random.normal(jax.random.fold_in(_rk, 611), (4, 512, 256), jnp.float32))
        return (x, ctx_1024)
    x, ctx_1024 = _rec_inputs()

    def _L0_attn_setup():
        import jax, jax.numpy as jnp
        import numpy as np
        H, DK, DV = (16, 128, 128)
        BINS = 64
        EPS = 1e-06
        NORM_EPS = 1e-05

        def silu(x):
            return x * jax.nn.sigmoid(x)

        def short_conv(x, w):
            C = x.shape[-1]
            K = w.shape[1]
            lhs = jnp.swapaxes(x, 1, 2)
            rhs = w[:, None, :]
            out = jax.lax.conv_general_dilated(lhs, rhs, window_strides=(1,), padding=[(K - 1, 0)], dimension_numbers=('NCH', 'OIH', 'NCH'), feature_group_count=C)
            return silu(jnp.swapaxes(out, 1, 2))

        def delta_rule(q, k, v, beta, decay):
            B = q.shape[0]

            def step(S, inp):
                qt, kt, vt, bt, gt = inp
                Sd = S * gt[..., None]
                v_pred = jnp.einsum('bhk,bhkv->bhv', kt, Sd)
                S_new = Sd + jnp.einsum('bhk,bhv->bhkv', kt * bt[..., None], vt - v_pred)
                ot = jnp.einsum('bhk,bhkv->bhv', qt, S_new)
                return (S_new, ot)
            tm = lambda a: jnp.swapaxes(a, 0, 1)
            S0 = jnp.zeros((B, H, DK, DV), q.dtype)
            _, o = jax.lax.scan(step, S0, (tm(q), tm(k), tm(v), tm(beta), tm(decay)))
            return jnp.swapaxes(o, 0, 1)

        def _forward(hidden_states, wq, wk, wv, conv_q_w, conv_k_w, conv_v_w, A_log, dt_bias, proxy_w, unc_w, head_embed, mlp_w1, mlp_b1, mlp_w2, mlp_b2, bb_w, bb_b, bd_w, bd_b, lam_w, lam_b, ab_w, ab_b, ad_w, ad_b, g1_w, g2_w, g2_b, onorm_w, wo):
            x = hidden_states
            B, T, _ = x.shape
            q = short_conv(x @ wq, conv_q_w).reshape(B, T, H, DK)
            k = short_conv(x @ wk, conv_k_w).reshape(B, T, H, DK)
            v = short_conv(x @ wv, conv_v_w).reshape(B, T, H, DV)
            logp = jax.nn.log_softmax(x @ unc_w, axis=-1)
            entropy = -jnp.sum(jnp.exp(logp) * logp, axis=-1)
            ent_norm = entropy / jnp.log(jnp.asarray(BINS, x.dtype))
            k_unit = k / (jnp.linalg.norm(k, axis=-1, keepdims=True) + EPS)
            v_hat = jnp.einsum('bthk,kv->bthv', k, proxy_w)
            err = v - v_hat
            err_n = jnp.linalg.norm(err, axis=-1)
            v_n = jnp.linalg.norm(v, axis=-1)
            vh_n = jnp.linalg.norm(v_hat, axis=-1)
            rel_err = err_n / (v_n + EPS)
            cos = jnp.sum(v * v_hat, axis=-1) / (v_n * vh_n + EPS)
            feats = jnp.stack([jnp.broadcast_to(ent_norm[..., None], err_n.shape), rel_err, cos, jnp.log1p(err_n)], axis=-1)
            he = jnp.broadcast_to(head_embed[None, None], (B, T, H, head_embed.shape[-1]))
            feats = jnp.concatenate([feats, he], axis=-1)
            hf = silu(silu(feats @ mlp_w1 + mlp_b1) @ mlp_w2 + mlp_b2)
            beta_base = hf @ bb_w + bb_b[0]
            beta_delta = hf @ bd_w + bd_b[0]
            beta_fast = jax.nn.sigmoid(beta_base + beta_delta)
            beta_slow = jax.nn.sigmoid(beta_base - beta_delta)
            lam = jax.nn.sigmoid(hf @ lam_w + lam_b[0])
            amp_base = hf @ ab_w + ab_b[0]
            amp_delta = hf @ ad_w + ad_b[0]
            amp_fast = jax.nn.sigmoid(amp_base + amp_delta)
            amp_slow = jax.nn.sigmoid(amp_base - amp_delta)
            g_chan = -jnp.exp(A_log)[:, None] * jax.nn.softplus(dt_bias).reshape(H, DK)
            decay_fast = jnp.exp(g_chan[None, None] * amp_fast[..., None])
            decay_slow = jnp.exp(g_chan[None, None] * amp_slow[..., None])
            qs = q * DK ** (-0.5)
            o_fast = delta_rule(qs, k_unit, v, beta_fast, decay_fast)
            o_slow = delta_rule(qs, k_unit, v, beta_slow, decay_slow)
            o = lam[..., None] * o_fast + (1.0 - lam[..., None]) * o_slow
            g = (x @ g1_w @ g2_w + g2_b).reshape(B, T, H, DV)
            rms = jnp.sqrt(jnp.mean(o * o, axis=-1, keepdims=True) + NORM_EPS)
            o = o / rms * onorm_w * jax.nn.sigmoid(g)
            return o.reshape(B, T, H * DV) @ wo
        key = jax.random.key(seed)
        ks = jax.random.split(key, 40)
        B, T, D = (2, 64, 512)

        def w(k, shape, fan_in):
            return jax.random.normal(k, shape, jnp.float32) * fan_in ** (-0.5)
        return {'hidden_states': jax.random.normal(ks[0], (B, T, D), jnp.float32), 'wq': w(ks[1], (D, H * DK), D), 'wk': w(ks[2], (D, H * DK), D), 'wv': w(ks[3], (D, H * DV), D), 'conv_q_w': w(ks[4], (H * DK, 4), 4), 'conv_k_w': w(ks[5], (H * DK, 4), 4), 'conv_v_w': w(ks[6], (H * DV, 4), 4), 'A_log': jnp.log(jax.random.uniform(ks[7], (H,), jnp.float32, 1.0, 16.0)), 'dt_bias': jnp.zeros((H * DK,), jnp.float32), 'proxy_w': w(ks[8], (DK, DV), DK), 'unc_w': w(ks[9], (D, BINS), D), 'head_embed': jax.random.normal(ks[10], (H, 4), jnp.float32), 'mlp_w1': w(ks[11], (8, 32), 8), 'mlp_b1': jnp.zeros((32,), jnp.float32), 'mlp_w2': w(ks[12], (32, 32), 32), 'mlp_b2': jnp.zeros((32,), jnp.float32), 'bb_w': w(ks[13], (32,), 32), 'bb_b': jnp.zeros((1,), jnp.float32), 'bd_w': w(ks[14], (32,), 32), 'bd_b': jnp.zeros((1,), jnp.float32), 'lam_w': w(ks[15], (32,), 32), 'lam_b': jnp.zeros((1,), jnp.float32), 'ab_w': w(ks[16], (32,), 32), 'ab_b': jnp.zeros((1,), jnp.float32), 'ad_w': w(ks[17], (32,), 32), 'ad_b': jnp.zeros((1,), jnp.float32), 'g1_w': w(ks[18], (D, DV), D), 'g2_w': w(ks[19], (DV, H * DV), DV), 'g2_b': jnp.zeros((H * DV,), jnp.float32), 'onorm_w': jnp.ones((DV,), jnp.float32), 'wo': w(ks[20], (H * DV, D), H * DV)}
    _L0_attn_all = _L0_attn_setup()
    _L0_attn_in = {k: v for k, v in _L0_attn_all.items() if k in ('wq', 'wk', 'wv', 'conv_q_w', 'conv_k_w', 'conv_v_w', 'A_log', 'dt_bias', 'proxy_w', 'unc_w', 'head_embed', 'mlp_w1', 'mlp_b1', 'mlp_w2', 'mlp_b2', 'bb_w', 'bb_b', 'bd_w', 'bd_b', 'lam_w', 'lam_b', 'ab_w', 'ab_b', 'ad_w', 'ad_b', 'g1_w', 'g2_w', 'g2_b', 'onorm_w', 'wo')}
    del _L0_attn_all

    def _L0_xattn_setup():
        import jax, jax.numpy as jnp
        import numpy as np
        import math
        B, L, DM = (2, 512, 256)
        DS, DC, EXP = (16, 4, 2)
        DI = EXP * DM
        DR = math.ceil(DM / 16)
        DT_MIN, DT_MAX, DT_FLOOR = (0.001, 0.1, 0.0001)

        def _ssm_forward(hidden_states, z, in_proj_w, conv_w, conv_b, x_proj_w, dt_proj_w, dt_proj_b, A_log, D):
            b = hidden_states.shape[0]
            x = jnp.einsum('ed,bld->bel', in_proj_w, hidden_states)
            xp = jnp.pad(x, ((0, 0), (0, 0), (DC - 1, 0)))
            xc = jax.lax.conv_general_dilated(xp, conv_w[:, None, :], window_strides=(1,), padding='VALID', dimension_numbers=('NCH', 'OIH', 'NCH'), feature_group_count=DI)
            u = jax.nn.silu(xc + conv_b[None, :, None])
            x_dbl = jnp.einsum('ke,bel->bkl', x_proj_w, u)
            dt_lo = x_dbl[:, :DR]
            Bm = x_dbl[:, DR:DR + DS]
            Cm = x_dbl[:, DR + DS:]
            delta = jax.nn.softplus(jnp.einsum('er,brl->bel', dt_proj_w, dt_lo) + dt_proj_b[None, :, None])
            A = -jnp.exp(A_log)

            def step(state, xs):
                d_t, B_t, C_t, u_t = xs
                dA = jnp.exp(d_t[..., None] * A)
                state = state * dA + (d_t * u_t)[..., None] * B_t[:, None, :]
                y_t = jnp.einsum('ben,bn->be', state, C_t)
                return (state, y_t)
            xs = (jnp.moveaxis(delta, -1, 0), jnp.moveaxis(Bm, -1, 0), jnp.moveaxis(Cm, -1, 0), jnp.moveaxis(u, -1, 0))
            state0 = jnp.zeros((b, DI, DS), delta.dtype)
            _, ys = jax.lax.scan(step, state0, xs)
            y = jnp.moveaxis(ys, 0, -1)
            y = y + D[None, :, None] * u
            y = y * jax.nn.silu(z)
            return jnp.swapaxes(y, 1, 2)
        key = jax.random.key(seed)
        ks = jax.random.split(key, 8)
        hidden_states = jax.random.normal(ks[0], (B, L, DM), jnp.float32)
        z = jax.random.normal(ks[1], (B, DI, L), jnp.float32)
        in_proj_w = jax.random.normal(ks[2], (DI, DM), jnp.float32) * DM ** (-0.5)
        conv_w = jax.random.normal(ks[3], (DI, DC), jnp.float32) * DC ** (-0.5)
        conv_b = jnp.zeros((DI,), jnp.float32)
        x_proj_w = jax.random.normal(ks[4], (DR + 2 * DS, DI), jnp.float32) * DI ** (-0.5)
        dt_std = DR ** (-0.5)
        dt_proj_w = jax.random.uniform(ks[5], (DI, DR), jnp.float32, -dt_std, dt_std)
        dt = jnp.exp(jax.random.uniform(ks[6], (DI,), jnp.float32) * (math.log(DT_MAX) - math.log(DT_MIN)) + math.log(DT_MIN))
        dt = jnp.clip(dt, DT_FLOOR)
        dt_proj_b = dt + jnp.log(-jnp.expm1(-dt))
        A_log = jnp.log(jnp.broadcast_to(jnp.arange(1, DS + 1, dtype=jnp.float32), (DI, DS)))
        D = jnp.ones((DI,), jnp.float32)
        return dict(hidden_states=hidden_states, z=z, in_proj_w=in_proj_w, conv_w=conv_w, conv_b=conv_b, x_proj_w=x_proj_w, dt_proj_w=dt_proj_w, dt_proj_b=dt_proj_b, A_log=A_log, D=D)
    _L0_xattn_all = _L0_xattn_setup()
    _L0_xattn_in = {k: v for k, v in _L0_xattn_all.items() if k in ('in_proj_w', 'conv_w', 'conv_b', 'x_proj_w', 'dt_proj_w', 'dt_proj_b', 'A_log', 'D')}
    del _L0_xattn_all

    def _L0_ffn_setup():
        import jax, jax.numpy as jnp
        import numpy as np
        B, S, D = (4, 512, 512)
        DFF = 1408
        E, K, R = (8, 2, 16)
        SCALING = 32.0 / 16.0
        key = jax.random.key(seed)
        ks = jax.random.split(key, 12)
        s = lambda k, shape, scale: jax.random.normal(k, shape, dtype=jnp.float32) * scale
        return {'x': s(ks[0], (B, S, D), 1.0), 'Wg': s(ks[1], (DFF, D), 0.02), 'Wu': s(ks[2], (DFF, D), 0.02), 'Wd': s(ks[3], (D, DFF), 0.02), 'Wr': s(ks[4], (E, D), 0.02), 'Ag': s(ks[5], (E, R, D), 0.02), 'Bg': s(ks[6], (E, DFF, R), 0.02), 'Au': s(ks[7], (E, R, D), 0.02), 'Bu': s(ks[8], (E, DFF, R), 0.02), 'Ad': s(ks[9], (E, R, DFF), 0.02), 'Bd': s(ks[10], (E, D, R), 0.02)}
    _L0_ffn_all = _L0_ffn_setup()
    _L0_ffn_in = {k: v for k, v in _L0_ffn_all.items() if k in ('Wg', 'Wu', 'Wd', 'Wr', 'Ag', 'Bg', 'Au', 'Bu', 'Ad', 'Bd')}
    del _L0_ffn_all
    return {'x': x, 'ctx_1024': ctx_1024, 'L0_attn_wq': _L0_attn_in['wq'], 'L0_attn_wk': _L0_attn_in['wk'], 'L0_attn_wv': _L0_attn_in['wv'], 'L0_attn_conv_q_w': _L0_attn_in['conv_q_w'], 'L0_attn_conv_k_w': _L0_attn_in['conv_k_w'], 'L0_attn_conv_v_w': _L0_attn_in['conv_v_w'], 'L0_attn_A_log': _L0_attn_in['A_log'], 'L0_attn_dt_bias': _L0_attn_in['dt_bias'], 'L0_attn_proxy_w': _L0_attn_in['proxy_w'], 'L0_attn_unc_w': _L0_attn_in['unc_w'], 'L0_attn_head_embed': _L0_attn_in['head_embed'], 'L0_attn_mlp_w1': _L0_attn_in['mlp_w1'], 'L0_attn_mlp_b1': _L0_attn_in['mlp_b1'], 'L0_attn_mlp_w2': _L0_attn_in['mlp_w2'], 'L0_attn_mlp_b2': _L0_attn_in['mlp_b2'], 'L0_attn_bb_w': _L0_attn_in['bb_w'], 'L0_attn_bb_b': _L0_attn_in['bb_b'], 'L0_attn_bd_w': _L0_attn_in['bd_w'], 'L0_attn_bd_b': _L0_attn_in['bd_b'], 'L0_attn_lam_w': _L0_attn_in['lam_w'], 'L0_attn_lam_b': _L0_attn_in['lam_b'], 'L0_attn_ab_w': _L0_attn_in['ab_w'], 'L0_attn_ab_b': _L0_attn_in['ab_b'], 'L0_attn_ad_w': _L0_attn_in['ad_w'], 'L0_attn_ad_b': _L0_attn_in['ad_b'], 'L0_attn_g1_w': _L0_attn_in['g1_w'], 'L0_attn_g2_w': _L0_attn_in['g2_w'], 'L0_attn_g2_b': _L0_attn_in['g2_b'], 'L0_attn_onorm_w': _L0_attn_in['onorm_w'], 'L0_attn_wo': _L0_attn_in['wo'], 'L0_xattn_in_proj_w': _L0_xattn_in['in_proj_w'], 'L0_xattn_conv_w': _L0_xattn_in['conv_w'], 'L0_xattn_conv_b': _L0_xattn_in['conv_b'], 'L0_xattn_x_proj_w': _L0_xattn_in['x_proj_w'], 'L0_xattn_dt_proj_w': _L0_xattn_in['dt_proj_w'], 'L0_xattn_dt_proj_b': _L0_xattn_in['dt_proj_b'], 'L0_xattn_A_log': _L0_xattn_in['A_log'], 'L0_xattn_D': _L0_xattn_in['D'], 'L0_ffn_Wg': _L0_ffn_in['Wg'], 'L0_ffn_Wu': _L0_ffn_in['Wu'], 'L0_ffn_Wd': _L0_ffn_in['Wd'], 'L0_ffn_Wr': _L0_ffn_in['Wr'], 'L0_ffn_Ag': _L0_ffn_in['Ag'], 'L0_ffn_Bg': _L0_ffn_in['Bg'], 'L0_ffn_Au': _L0_ffn_in['Au'], 'L0_ffn_Bu': _L0_ffn_in['Bu'], 'L0_ffn_Ad': _L0_ffn_in['Ad'], 'L0_ffn_Bd': _L0_ffn_in['Bd']}

def reference(x, ctx_1024, L0_attn_wq, L0_attn_wk, L0_attn_wv, L0_attn_conv_q_w, L0_attn_conv_k_w, L0_attn_conv_v_w, L0_attn_A_log, L0_attn_dt_bias, L0_attn_proxy_w, L0_attn_unc_w, L0_attn_head_embed, L0_attn_mlp_w1, L0_attn_mlp_b1, L0_attn_mlp_w2, L0_attn_mlp_b2, L0_attn_bb_w, L0_attn_bb_b, L0_attn_bd_w, L0_attn_bd_b, L0_attn_lam_w, L0_attn_lam_b, L0_attn_ab_w, L0_attn_ab_b, L0_attn_ad_w, L0_attn_ad_b, L0_attn_g1_w, L0_attn_g2_w, L0_attn_g2_b, L0_attn_onorm_w, L0_attn_wo, L0_xattn_in_proj_w, L0_xattn_conv_w, L0_xattn_conv_b, L0_xattn_x_proj_w, L0_xattn_dt_proj_w, L0_xattn_dt_proj_b, L0_xattn_A_log, L0_xattn_D, L0_ffn_Wg, L0_ffn_Wu, L0_ffn_Wd, L0_ffn_Wr, L0_ffn_Ag, L0_ffn_Bg, L0_ffn_Au, L0_ffn_Bu, L0_ffn_Ad, L0_ffn_Bd):
    import jax
    import jax.numpy as jnp

    def _L0_attn_ref(hidden_states, wq, wk, wv, conv_q_w, conv_k_w, conv_v_w, A_log, dt_bias, proxy_w, unc_w, head_embed, mlp_w1, mlp_b1, mlp_w2, mlp_b2, bb_w, bb_b, bd_w, bd_b, lam_w, lam_b, ab_w, ab_b, ad_w, ad_b, g1_w, g2_w, g2_b, onorm_w, wo):
        import jax, jax.numpy as jnp
        import numpy as np
        H, DK, DV = (16, 128, 128)
        BINS = 64
        EPS = 1e-06
        NORM_EPS = 1e-05

        def silu(x):
            return x * jax.nn.sigmoid(x)

        def short_conv(x, w):
            C = x.shape[-1]
            K = w.shape[1]
            lhs = jnp.swapaxes(x, 1, 2)
            rhs = w[:, None, :]
            out = jax.lax.conv_general_dilated(lhs, rhs, window_strides=(1,), padding=[(K - 1, 0)], dimension_numbers=('NCH', 'OIH', 'NCH'), feature_group_count=C)
            return silu(jnp.swapaxes(out, 1, 2))

        def delta_rule(q, k, v, beta, decay):
            B = q.shape[0]

            def step(S, inp):
                qt, kt, vt, bt, gt = inp
                Sd = S * gt[..., None]
                v_pred = jnp.einsum('bhk,bhkv->bhv', kt, Sd)
                S_new = Sd + jnp.einsum('bhk,bhv->bhkv', kt * bt[..., None], vt - v_pred)
                ot = jnp.einsum('bhk,bhkv->bhv', qt, S_new)
                return (S_new, ot)
            tm = lambda a: jnp.swapaxes(a, 0, 1)
            S0 = jnp.zeros((B, H, DK, DV), q.dtype)
            _, o = jax.lax.scan(step, S0, (tm(q), tm(k), tm(v), tm(beta), tm(decay)))
            return jnp.swapaxes(o, 0, 1)

        def _forward(hidden_states, wq, wk, wv, conv_q_w, conv_k_w, conv_v_w, A_log, dt_bias, proxy_w, unc_w, head_embed, mlp_w1, mlp_b1, mlp_w2, mlp_b2, bb_w, bb_b, bd_w, bd_b, lam_w, lam_b, ab_w, ab_b, ad_w, ad_b, g1_w, g2_w, g2_b, onorm_w, wo):
            x = hidden_states
            B, T, _ = x.shape
            q = short_conv(x @ wq, conv_q_w).reshape(B, T, H, DK)
            k = short_conv(x @ wk, conv_k_w).reshape(B, T, H, DK)
            v = short_conv(x @ wv, conv_v_w).reshape(B, T, H, DV)
            logp = jax.nn.log_softmax(x @ unc_w, axis=-1)
            entropy = -jnp.sum(jnp.exp(logp) * logp, axis=-1)
            ent_norm = entropy / jnp.log(jnp.asarray(BINS, x.dtype))
            k_unit = k / (jnp.linalg.norm(k, axis=-1, keepdims=True) + EPS)
            v_hat = jnp.einsum('bthk,kv->bthv', k, proxy_w)
            err = v - v_hat
            err_n = jnp.linalg.norm(err, axis=-1)
            v_n = jnp.linalg.norm(v, axis=-1)
            vh_n = jnp.linalg.norm(v_hat, axis=-1)
            rel_err = err_n / (v_n + EPS)
            cos = jnp.sum(v * v_hat, axis=-1) / (v_n * vh_n + EPS)
            feats = jnp.stack([jnp.broadcast_to(ent_norm[..., None], err_n.shape), rel_err, cos, jnp.log1p(err_n)], axis=-1)
            he = jnp.broadcast_to(head_embed[None, None], (B, T, H, head_embed.shape[-1]))
            feats = jnp.concatenate([feats, he], axis=-1)
            hf = silu(silu(feats @ mlp_w1 + mlp_b1) @ mlp_w2 + mlp_b2)
            beta_base = hf @ bb_w + bb_b[0]
            beta_delta = hf @ bd_w + bd_b[0]
            beta_fast = jax.nn.sigmoid(beta_base + beta_delta)
            beta_slow = jax.nn.sigmoid(beta_base - beta_delta)
            lam = jax.nn.sigmoid(hf @ lam_w + lam_b[0])
            amp_base = hf @ ab_w + ab_b[0]
            amp_delta = hf @ ad_w + ad_b[0]
            amp_fast = jax.nn.sigmoid(amp_base + amp_delta)
            amp_slow = jax.nn.sigmoid(amp_base - amp_delta)
            g_chan = -jnp.exp(A_log)[:, None] * jax.nn.softplus(dt_bias).reshape(H, DK)
            decay_fast = jnp.exp(g_chan[None, None] * amp_fast[..., None])
            decay_slow = jnp.exp(g_chan[None, None] * amp_slow[..., None])
            qs = q * DK ** (-0.5)
            o_fast = delta_rule(qs, k_unit, v, beta_fast, decay_fast)
            o_slow = delta_rule(qs, k_unit, v, beta_slow, decay_slow)
            o = lam[..., None] * o_fast + (1.0 - lam[..., None]) * o_slow
            g = (x @ g1_w @ g2_w + g2_b).reshape(B, T, H, DV)
            rms = jnp.sqrt(jnp.mean(o * o, axis=-1, keepdims=True) + NORM_EPS)
            o = o / rms * onorm_w * jax.nn.sigmoid(g)
            return o.reshape(B, T, H * DV) @ wo
        return _forward(hidden_states, wq, wk, wv, conv_q_w, conv_k_w, conv_v_w, A_log, dt_bias, proxy_w, unc_w, head_embed, mlp_w1, mlp_b1, mlp_w2, mlp_b2, bb_w, bb_b, bd_w, bd_b, lam_w, lam_b, ab_w, ab_b, ad_w, ad_b, g1_w, g2_w, g2_b, onorm_w, wo)

    def _L0_xattn_ref(hidden_states, z, in_proj_w, conv_w, conv_b, x_proj_w, dt_proj_w, dt_proj_b, A_log, D):
        import jax, jax.numpy as jnp
        import numpy as np
        import math
        B, L, DM = (2, 512, 256)
        DS, DC, EXP = (16, 4, 2)
        DI = EXP * DM
        DR = math.ceil(DM / 16)
        DT_MIN, DT_MAX, DT_FLOOR = (0.001, 0.1, 0.0001)

        def _ssm_forward(hidden_states, z, in_proj_w, conv_w, conv_b, x_proj_w, dt_proj_w, dt_proj_b, A_log, D):
            b = hidden_states.shape[0]
            x = jnp.einsum('ed,bld->bel', in_proj_w, hidden_states)
            xp = jnp.pad(x, ((0, 0), (0, 0), (DC - 1, 0)))
            xc = jax.lax.conv_general_dilated(xp, conv_w[:, None, :], window_strides=(1,), padding='VALID', dimension_numbers=('NCH', 'OIH', 'NCH'), feature_group_count=DI)
            u = jax.nn.silu(xc + conv_b[None, :, None])
            x_dbl = jnp.einsum('ke,bel->bkl', x_proj_w, u)
            dt_lo = x_dbl[:, :DR]
            Bm = x_dbl[:, DR:DR + DS]
            Cm = x_dbl[:, DR + DS:]
            delta = jax.nn.softplus(jnp.einsum('er,brl->bel', dt_proj_w, dt_lo) + dt_proj_b[None, :, None])
            A = -jnp.exp(A_log)

            def step(state, xs):
                d_t, B_t, C_t, u_t = xs
                dA = jnp.exp(d_t[..., None] * A)
                state = state * dA + (d_t * u_t)[..., None] * B_t[:, None, :]
                y_t = jnp.einsum('ben,bn->be', state, C_t)
                return (state, y_t)
            xs = (jnp.moveaxis(delta, -1, 0), jnp.moveaxis(Bm, -1, 0), jnp.moveaxis(Cm, -1, 0), jnp.moveaxis(u, -1, 0))
            state0 = jnp.zeros((b, DI, DS), delta.dtype)
            _, ys = jax.lax.scan(step, state0, xs)
            y = jnp.moveaxis(ys, 0, -1)
            y = y + D[None, :, None] * u
            y = y * jax.nn.silu(z)
            return jnp.swapaxes(y, 1, 2)
        return _ssm_forward(hidden_states, z, in_proj_w, conv_w, conv_b, x_proj_w, dt_proj_w, dt_proj_b, A_log, D)

    def _L0_ffn_ref(x, Wg, Wu, Wd, Wr, Ag, Bg, Au, Bu, Ad, Bd):
        import jax, jax.numpy as jnp
        import numpy as np
        B, S, D = (4, 512, 512)
        DFF = 1408
        E, K, R = (8, 2, 16)
        SCALING = 32.0 / 16.0
        b, s, d = x.shape
        xf = x.reshape(-1, d)
        gate_base = xf @ Wg.T
        up_base = xf @ Wu.T
        base_out = jax.nn.silu(gate_base) * up_base @ Wd.T
        router_logits = xf @ Wr.T
        probs = jax.nn.softmax(router_logits.astype(jnp.float32), axis=-1)
        topw, topi = jax.lax.top_k(probs, K)
        topw = topw.astype(x.dtype)
        expert_w = jnp.sum(jax.nn.one_hot(topi, E, dtype=x.dtype) * topw[..., None], axis=1)

        def expert_step(acc, params):
            Ag_e, Bg_e, Au_e, Bu_e, Ad_e, Bd_e, we = params
            g_lora = xf @ Ag_e.T @ Bg_e.T * SCALING
            u_lora = xf @ Au_e.T @ Bu_e.T * SCALING
            h = jax.nn.silu(gate_base + g_lora) * (up_base + u_lora)
            d_delta = h @ Ad_e.T @ Bd_e.T * SCALING
            return (acc + d_delta * we[:, None], None)
        acc0 = jnp.zeros_like(base_out)
        acc, _ = jax.lax.scan(expert_step, acc0, (Ag, Bg, Au, Bu, Ad, Bd, expert_w.T))
        return (base_out + acc).reshape(b, s, d)
    x = _layernorm(x + _L0_attn_ref(x, L0_attn_wq, L0_attn_wk, L0_attn_wv, L0_attn_conv_q_w, L0_attn_conv_k_w, L0_attn_conv_v_w, L0_attn_A_log, L0_attn_dt_bias, L0_attn_proxy_w, L0_attn_unc_w, L0_attn_head_embed, L0_attn_mlp_w1, L0_attn_mlp_b1, L0_attn_mlp_w2, L0_attn_mlp_b2, L0_attn_bb_w, L0_attn_bb_b, L0_attn_bd_w, L0_attn_bd_b, L0_attn_lam_w, L0_attn_lam_b, L0_attn_ab_w, L0_attn_ab_b, L0_attn_ad_w, L0_attn_ad_b, L0_attn_g1_w, L0_attn_g2_w, L0_attn_g2_b, L0_attn_onorm_w, L0_attn_wo), axis=-1)
    x = _layernorm(x + _L0_xattn_ref(ctx_1024, x, L0_xattn_in_proj_w, L0_xattn_conv_w, L0_xattn_conv_b, L0_xattn_x_proj_w, L0_xattn_dt_proj_w, L0_xattn_dt_proj_b, L0_xattn_A_log, L0_xattn_D), axis=-1)
    x = _layernorm(x + _L0_ffn_ref(x, L0_ffn_Wg, L0_ffn_Wu, L0_ffn_Wd, L0_ffn_Wr, L0_ffn_Ag, L0_ffn_Bg, L0_ffn_Au, L0_ffn_Bu, L0_ffn_Ad, L0_ffn_Bd), axis=-1)
    return x

_drawn_inputs = setup_inputs


def setup_inputs(seed=0):
    import zlib

    import numpy as np

    out = dict(_drawn_inputs(seed))
    spreads = {'L0_attn_dt_bias': (0.0, 0.665),
     'L0_attn_mlp_b1': (0.0, 0.8),
     'L0_attn_mlp_b2': (0.0, 0.8),
     'L0_attn_g2_b': (0.0, 0.417),
     'L0_attn_onorm_w': (1.0, 0.2),
     'L0_xattn_conv_b': (0.0, 0.1),
     'L0_xattn_D': (1.0, 0.2)}
    factors = {'L0_attn_proxy_w': 8.0,
     'L0_attn_unc_w': 8.0,
     'L0_attn_bb_w': 8.0,
     'L0_attn_bd_w': 5.931,
     'L0_attn_lam_w': 8.0,
     'L0_attn_ad_w': 3.884,
     'L0_xattn_dt_proj_w': 5.377,
     'L0_ffn_Wr': 8.0,
     'L0_ffn_Ag': 8.0,
     'L0_ffn_Bg': 8.0,
     'L0_ffn_Au': 8.0,
     'L0_ffn_Bu': 8.0,
     'L0_ffn_Ad': 8.0,
     'L0_ffn_Bd': 8.0,
     'L0_ffn_Wd': 39.452}
    for name, (base, spread) in spreads.items():
        noise = np.random.default_rng([zlib.crc32(name.encode()), seed]).standard_normal(out[name].shape)
        drawn = base * np.exp(spread * noise) if base else spread * noise
        out[name] = jnp.asarray(drawn.astype(out[name].dtype))
    for name, factor in factors.items():
        out[name] = (out[name] * factor).astype(out[name].dtype)
    return out
```

```python
import math
from contextlib import ExitStack

import concourse.bass as bass
from concourse import mybir

F32 = mybir.dt.float32
I32 = mybir.dt.int32
ALU = mybir.AluOpType
ACT = mybir.ActivationFunctionType
AX_X = mybir.AxisListType.X

P = 128
B, T, D = 4, 512, 512
DC = D // P
TT = T // P
H = 16
BINS = 64
HID = 32
EPS = 1e-6
NORM_EPS = 1e-5
LEVELS = 7
HALF = P // 2
DI, DS, DR, CTX = 512, 16, 16, 256
ET = DI // P
DFF, E, R = 1408, 8, 16
FC = DFF // P
LORA_SCALE = 2.0
Q_SCALE = float(P) ** -0.5
LN_BINS_INV = 1.0 / math.log(BINS)


def spread(ap, shape):
    return ap.broadcast_to(shape)


def ssm_stage(nc, io):
    NB = 4
    with ExitStack() as ctx:
        def sb(name, shape):
            return ctx.enter_context(nc.sbuf_tensor("m_" + name, shape, F32))

        def ps(name, shape=(P, 512)):
            return ctx.enter_context(nc.psum_tensor("m_" + name, list(shape), F32))

        def sem(name):
            return ctx.enter_context(nc.semaphore("m_" + name))

        ident = sb("ident", [P, P])
        w_in = sb("w_in", [P, 2, DI])
        w_x = sb("w_x", [P, ET, DR + 2 * DS])
        w_dt = sb("w_dt", [DR, DI])
        cols = sb("cols", [P, ET, 4 + 1 + 1 + 1 + DS])
        neg_a = sb("neg_a", [P, ET, DS])
        ctx_t = sb("ctx_t", [P, 2, T])
        tap = sb("tap", [P, 2, T])
        u = sb("u", [P, ET, T])
        x_dbl = sb("x_dbl", [DR + 2 * DS, T])
        soft = sb("soft", [P, 2, T])
        delta = sb("delta", [P, ET, T])
        b_rows = sb("b_rows", [P, DS, T])
        c_rows = sb("c_rows", [P, DS, T])
        du = sb("du", [P, 2, T])
        da = sb("da", [P, NB, T])
        dbu = sb("dbu", [P, NB, T])
        state = sb("state", [P, NB, T])
        cs = sb("cs", [P, NB, T])
        y_out = sb("y_out", [P, 2, T])
        p_x = ps("p_x", (P, 2, T))
        p_d = ps("p_d")
        p_b = ps("p_b", (P, 2, T))
        p_y = ps("p_y", (P, 2, T))

        weights = sem("weights")
        ctx_in = sem("ctx_in")
        neg_a_ready = sem("neg_a_ready")
        projected = sem("projected")
        tapped = sem("tapped")
        convolved = sem("convolved")
        u_ready = sem("u_ready")
        dbl_sum = sem("dbl_sum")
        dbl_ready = sem("dbl_ready")
        dt_sum = sem("dt_sum")
        soft_ready = sem("soft_ready")
        delta_ready = sem("delta_ready")
        row_sum = sem("row_sum")
        b_ready = sem("b_ready")
        c_ready = sem("c_ready")
        du_ready = sem("du_ready")
        da_ready = sem("da_ready")
        dbu_ready = sem("dbu_ready")
        scanned = sem("scanned")
        cs_ready = sem("cs_ready")
        summed = sem("summed")
        y_ready = sem("y_ready")
        y_stored = [sem(f"y_stored{i}") for i in range(2)]
        rounds = sem("rounds")
        passed = sem("passed")

        with nc.Block() as block:

            @block.sync
            def _(sp):
                sp.dma_start(ident[:], io["ident"]).then_inc(weights, 16)
                sp.dma_start(w_in[:], io["ssm_in_w"]).then_inc(weights, 16)
                sp.dma_start(w_x[:], io["ssm_x_w"]).then_inc(weights, 16)
                sp.dma_start(w_dt[:], io["ssm_dt_w"]).then_inc(weights, 16)
                sp.dma_start(cols[:], io["ssm_cols"]).then_inc(weights, 16)
                for stored in y_stored:
                    sp.sem_inc(stored, 1)
                sp.sem_inc(rounds, 1)
                with sp.Fori(0, B) as b:
                    sp.wait_ge(rounds, 4 * b + 1)
                    sp.dma_start(ctx_t[:], io["ctx_t"][b]).then_inc(ctx_in, 16)
                    for et in range(ET):
                        sp.wait_ge(y_ready, b * ET + et + 1)
                        sp.dma_start(io["y_ssm"][b, et], y_out[:, et % 2]).then_inc(y_stored[et % 2], 16)
                for stored in y_stored:
                    sp.wait_ge(stored, 16 * B * ET // 2 + 1)

            @block.tensor
            def _(pe):
                pe.wait_ge(weights, 80)
                with pe.Fori(0, B) as b:
                    pe.wait_ge(rounds, 4 * b + 1)
                    pe.wait_ge(ctx_in, 16 * (b + 1))
                    for et in range(ET):
                        if et >= 2:
                            pe.wait_ge(convolved, b * ET + et - 1)
                        for k in range(2):
                            mm = nc.tensor.matmul(p_x[:, et % 2], w_in[:, k, et * P:(et + 1) * P], ctx_t[:, k],
                                                  start=(k == 0), stop=(k == 1))
                        mm.then_inc(projected, 1)
                    for et in range(ET):
                        pe.wait_ge(u_ready, b * ET + et + 1)
                        mm = nc.tensor.matmul(p_d[0:DR + 2 * DS, :], w_x[:, et], u[:, et],
                                              start=(et == 0), stop=(et == ET - 1))
                    mm.then_inc(dbl_sum, 1)
                    pe.wait_ge(dbl_ready, b + 1)
                    for et in range(ET):
                        if et >= 2:
                            pe.wait_ge(soft_ready, b * ET + et - 1)
                        nc.tensor.matmul(p_x[:, et % 2], w_dt[:, et * P:(et + 1) * P], x_dbl[0:DR, :],
                                                      start=True, stop=True).then_inc(dt_sum, 1)
                    for n in range(2 * DS):
                        if n >= 2:
                            pe.wait_ge(b_ready if n % 2 == 0 else c_ready, b * DS + n // 2)
                        k = DR + (n // 2) + DS * (n % 2)
                        nc.tensor.matmul(
                            p_b[:, n % 2], spread(ident[0:DR + 2 * DS, k:k + 1], [DR + 2 * DS, P]),
                            x_dbl[:, :], start=True, stop=True).then_inc(row_sum, 1)
                    for et in range(ET):
                        if et >= 2:
                            pe.wait_ge(y_ready, b * ET + et - 1)
                        for n in range(DS):
                            i = et * DS + n
                            pe.wait_ge(cs_ready, b * ET * DS + i + 1)
                            nc.tensor.matmul(p_y[:, et % 2], ident[:], cs[:, i % NB],
                                                          start=(n == 0), stop=(n == DS - 1)).then_inc(summed, 1)
                    pe.drain().then_inc(rounds, 1)

            @block.scalar
            def _(act):
                act.wait_ge(weights, 80)
                nc.scalar.activation(neg_a[:], cols[:, :, 7:], ACT.Exp)
                act.drain()
                nc.scalar.activation(neg_a[:], neg_a[:], ACT.Copy, scale=-1.0).then_inc(neg_a_ready, 1)
                act.wait_ge(neg_a_ready, 1)
                with act.Fori(0, B) as b:
                    act.wait_ge(rounds, 4 * b + 1)

                    def silu(et):
                        act.wait_ge(convolved, b * ET + et + 1)
                        nc.scalar.activation(u[:, et], tap[:, et % 2], ACT.Silu, bias=cols[:, et, 4:5]).then_inc(u_ready, 1)

                    for et in range(ET):
                        act.wait_ge(projected, b * ET + et + 1)
                        if et >= 2:
                            act.wait_ge(u_ready, b * ET + et - 1)
                        nc.scalar.activation(tap[:, et % 2], p_x[:, et % 2], ACT.Copy,
                                                          scale=cols[:, et, 3:4]).then_inc(tapped, 1)
                        if et >= 1:
                            silu(et - 1)
                    silu(ET - 1)
                    act.wait_ge(dbl_sum, b + 1)
                    nc.scalar.copy(x_dbl[:], p_d[0:DR + 2 * DS, :]).then_inc(dbl_ready, 1)
                    for et in range(ET):
                        act.wait_ge(dt_sum, b * ET + et + 1)
                        if et >= 1:
                            act.wait_ge(delta_ready, b * ET + et)
                        bias = cols[:, et, 5:6]
                        nc.scalar.activation(soft[:, 0], p_x[:, et % 2], ACT.Abs, bias=bias)
                        nc.scalar.activation(soft[:, 1], p_x[:, et % 2], ACT.Relu, bias=bias)
                        act.drain()
                        nc.scalar.activation(soft[:, 0], soft[:, 0], ACT.Exp, scale=-1.0)
                        act.drain()
                        nc.scalar.activation(soft[:, 0], soft[:, 0], ACT.Ln, bias=1.0).then_inc(soft_ready, 1)
                    for n in range(DS):
                        act.wait_ge(row_sum, b * 2 * DS + 2 * n + 1)
                        nc.scalar.copy(b_rows[:, n], p_b[:, 0]).then_inc(b_ready, 1)
                    for et in range(ET):
                        act.wait_ge(delta_ready, b * ET + et + 1)
                        for n in range(DS):
                            i = et * DS + n
                            if i >= NB:
                                act.wait_ge(scanned, b * ET * DS + i - NB + 1)
                            nc.scalar.activation(da[:, i % NB], delta[:, et], ACT.Exp,
                                                                scale=neg_a[:, et, n:n + 1]).then_inc(da_ready, 1)
                    act.drain().then_inc(rounds, 1)

            @block.vector
            def _(dve):
                dve.wait_ge(weights, 80)
                with dve.Fori(0, B) as b:
                    dve.wait_ge(rounds, 4 * b + 1)
                    for et in range(ET):
                        dve.wait_ge(tapped, b * ET + et + 1)
                        for s in range(1, 4):
                            last = nc.vector.scalar_tensor_tensor(
                                tap[:, et % 2, s:T], p_x[:, et % 2, 0:T - s], cols[:, et, 3 - s:4 - s],
                                tap[:, et % 2, s:T], ALU.mult, ALU.add)
                            if s < 3:
                                dve.drain()
                        last.then_inc(convolved, 1)
                    for et in range(ET):
                        dve.wait_ge(soft_ready, b * ET + et + 1)
                        nc.vector.tensor_tensor(delta[:, et], soft[:, 0], soft[:, 1], ALU.add).then_inc(delta_ready, 1)
                    for n in range(DS):
                        dve.wait_ge(row_sum, b * 2 * DS + 2 * n + 2)
                        nc.vector.tensor_copy(c_rows[:, n], p_b[:, 1]).then_inc(c_ready, 1)

                    def times_c(i):
                        dve.wait_ge(scanned, b * ET * DS + i + 1)
                        if i >= NB:
                            dve.wait_ge(summed, b * ET * DS + i - NB + 1)
                        nc.vector.tensor_tensor(cs[:, i % NB], state[:, i % NB],
                                                               c_rows[:, i % DS], ALU.mult).then_inc(cs_ready, 1)

                    for et in range(ET):
                        for n in range(DS):
                            i = et * DS + n
                            dve.wait_ge(da_ready, b * ET * DS + i + 1)
                            dve.wait_ge(dbu_ready, b * ET * DS + i + 1)
                            if i >= NB:
                                dve.wait_ge(cs_ready, b * ET * DS + i - NB + 1)
                            nc.vector.tensor_tensor_scan(state[:, i % NB], da[:, i % NB],
                                                                       dbu[:, i % NB], 0.0, ALU.mult, ALU.add).then_inc(scanned, 1)
                            if i >= 1:
                                times_c(i - 1)
                        if et == ET - 1:
                            times_c(ET * DS - 1)
                        for done in ([et - 1] if et >= 1 else []) + ([et] if et == ET - 1 else []):
                            dve.wait_ge(summed, b * ET * DS + (done + 1) * DS)
                            dve.wait_ge(y_stored[done % 2], 16 * (b * (ET // 2) + done // 2) + 1)
                            nc.vector.scalar_tensor_tensor(
                                y_out[:, done % 2], u[:, done], cols[:, done, 6:7], p_y[:, done % 2],
                                ALU.mult, ALU.add).then_inc(y_ready, 1)
                    dve.drain().then_inc(rounds, 1)

            @block.gpsimd
            def _(pool):
                with pool.Fori(0, B) as b:
                    pool.wait_ge(rounds, 4 * b + 1)
                    for et in range(ET):
                        pool.wait_ge(delta_ready, b * ET + et + 1)
                        pool.wait_ge(u_ready, b * ET + et + 1)
                        if et >= 2:
                            pool.wait_ge(dbu_ready, b * ET * DS + (et - 1) * DS)
                        nc.gpsimd.tensor_tensor(du[:, et % 2], delta[:, et], u[:, et], ALU.mult).then_inc(du_ready, 1)
                        pool.wait_ge(du_ready, b * ET + et + 1)
                        for n in range(DS):
                            i = et * DS + n
                            pool.wait_ge(b_ready, b * DS + n + 1)
                            if i >= NB:
                                pool.wait_ge(scanned, b * ET * DS + i - NB + 1)
                            nc.gpsimd.tensor_tensor(dbu[:, i % NB], du[:, et % 2],
                                                                    b_rows[:, n], ALU.mult).then_inc(dbu_ready, 1)
                    pool.drain().then_inc(rounds, 1)


P_NORM, P_BETA_SLOW, P_BETA_FAST, P_LAMBDA, P_AMP_SLOW, P_AMP_FAST = range(6)
SLOW, FAST = 0, 1
NEG_K, QUERY = 0, 1
PAIRS = 2 * TT
C_G2B, C_BIAS1, C_DECAY = 12, 13, 14


def left(ap, h):
    return ap.rearrange("p x (s two h) -> p x s two h", two=2, h=h)[:, :, :, 0, :]


def right(ap, h):
    return ap.rearrange("p x (s two h) -> p x s two h", two=2, h=h)[:, :, :, 1, :]


def compact(ap, h):
    return ap.rearrange("p x (s h) -> p x s h", h=h)


def attn_stage(nc, io):
    with ExitStack() as ctx:
        def sb(name, shape, dt=F32):
            return ctx.enter_context(nc.sbuf_tensor("a_" + name, shape, dt))

        def sem(name):
            return ctx.enter_context(nc.semaphore("a_" + name))

        pb = ctx.enter_context(nc.psum_tensor("a_pb", [P, 8, 512], F32))
        ident = sb("ident", [P, P])
        ones = sb("ones", [P, HID])
        mean_w = sb("mean_w", [P, HID])
        eps_col = sb("eps_col", [P, 1])
        mask_u = sb("mask_u", [P, LEVELS, HALF], I32)
        mask_l = sb("mask_l", [P, LEVELS, HALF], I32)
        sel = sb("sel", [P, P])
        small = sb("small", [P, 49])
        x_t = sb("x_t", [P, DC, B * T])
        g_t = sb("g_t", [P, B * T])
        head_cols = sb("head_cols", [P, H, 15])
        w_out = sb("w_out", [P, 5, P])
        b_out = sb("b_out", [P, 5])
        w2_diag = sb("w2_diag", [P, P])
        ent_w = sb("ent_w", [P, T])
        work = sb("work", [P, 12, T])
        proxy = sb("proxy", [P, P])

        with ExitStack() as once:
            def sb1(name, shape):
                return once.enter_context(nc.sbuf_tensor("a1_" + name, shape, F32))

            def sem1(name):
                return once.enter_context(nc.semaphore("a1_" + name))

            g1 = sb1("g1", [P, DC, P])
            unc = sb1("unc", [P, DC, BINS])
            w1_embed = sb1("w1_embed", [4, P])
            embed_t = sb1("embed_t", [4, H])
            cols = sb1("cols", [P, 12, B * TT])
            loaded = sem1("loaded")
            zeroed = sem1("zeroed")
            placed = sem1("placed")
            logits = sem1("logits")
            shifted = sem1("shifted")
            exped = sem1("exped")
            summed = sem1("summed")
            logged = sem1("logged")
            ent_rows = sem1("ent_rows")
            ent_sum = sem1("ent_sum")
            g1_sum = sem1("g1_sum")
            bias_sum = sem1("bias_sum")
            soft = sem1("soft")
            LOADS = 12
            with nc.Block() as block:

                @block.sync
                def _(sp):
                    for dst, src in ((ident, "ident"), (mask_u, "mask_u"), (mask_l, "mask_l"), (sel, "sel"),
                                     (small, "small"), (proxy, "proxy"), (x_t, "x_t"), (g1, "g1"), (unc, "unc"),
                                     (w1_embed, "w1_embed"), (embed_t, "embed_t")):
                        sp.dma_start(dst[:], io[src]).then_inc(loaded, 16)
                    sp.dma_start(head_cols[:, :, 0:13], io["head_cols"]).then_inc(loaded, 16)
                    sp.wait_ge(zeroed, 1)
                    for q in range(4):
                        sp.dma_start(w2_diag[32 * q:32 * q + 32, 32 * q:32 * q + 32], io["mlp_w2"]).then_inc(placed, 16)
                    sp.wait_ge(placed, 64)
                    sp.wait_ge(loaded, 16 * LOADS)

                @block.gpsimd
                def _(pool):
                    nc.gpsimd.memset(w2_diag[:], 0.0).then_inc(zeroed, 1)
                    nc.gpsimd.memset(ones[:], 1.0)
                    nc.gpsimd.memset(mean_w[:], 1.0 / P)
                    nc.gpsimd.memset(eps_col[:], NORM_EPS)

                @block.tensor
                def _(pe):
                    pe.wait_ge(loaded, 16 * LOADS)
                    lg = pb[:, 0:2].rearrange("p k (i n) -> p (k i) n", n=BINS)
                    for i in range(B * TT):
                        for k in range(DC):
                            mm = nc.tensor.matmul(lg[:, i], x_t[:, k, i * P:(i + 1) * P], unc[:, k],
                                                  start=(k == 0), stop=(k == DC - 1))
                    mm.then_inc(logits, 1)
                    for b in range(B):
                        for k in range(DC):
                            mm = nc.tensor.matmul(pb[:, 3 + b], g1[:, k], x_t[:, k, b * T:(b + 1) * T],
                                                  start=(k == 0), stop=(k == DC - 1))
                    mm.then_inc(g1_sum, 1)
                    nc.tensor.matmul(pb[:, 7, 0:H], w1_embed[:], embed_t[:], start=True, stop=True).then_inc(bias_sum, 1)
                    pe.wait_ge(ent_rows, 1)
                    for tt in range(TT):
                        mm = nc.tensor.matmul(pb[:, 2, tt * P:(tt + 1) * P], work[:, 6, tt * P:(tt + 1) * P],
                                              ident[:], start=True, stop=True)
                    mm.then_inc(ent_sum, 1)

                @block.scalar
                def _(act):
                    act.wait_ge(loaded, 16 * LOADS)
                    nc.scalar.activation(cols[:, 8], small[:, 17:33], ACT.Exp)
                    nc.scalar.activation(cols[:, 9], small[:, 33:49], ACT.Relu)
                    nc.scalar.activation(cols[:, 10], small[:, 33:49], ACT.Abs)
                    act.drain()
                    nc.scalar.activation(cols[:, 10], cols[:, 10], ACT.Exp, scale=-1.0)
                    act.drain()
                    nc.scalar.activation(cols[:, 10], cols[:, 10], ACT.Ln, bias=1.0).then_inc(soft, 1)
                    act.wait_ge(bias_sum, 1)
                    nc.scalar.activation(head_cols[:, :, C_BIAS1], pb[:, 7, 0:H], ACT.Identity, bias=small[:, 4:5])
                    act.wait_ge(g1_sum, 1)
                    for b in range(B):
                        nc.scalar.copy(g_t[:, b * T:(b + 1) * T], pb[:, 3 + b])
                    act.wait_ge(shifted, 1)
                    nc.scalar.activation(work[:, 2:4], work[:, 0:2], ACT.Exp).then_inc(exped, 1)
                    act.wait_ge(summed, 1)
                    nc.scalar.activation(cols[:, 2], cols[:, 1], ACT.Ln).then_inc(logged, 1)

                @block.vector
                def _(dve):
                    dve.wait_ge(loaded, 16 * LOADS)
                    for src, dst in ((small[:, 6:11], cols[:, 5, 0:5]), (small[:, 11:16], b_out[:])):
                        for o, base, delta, op in ((0, 0, 1, ALU.subtract), (1, 0, 1, ALU.add),
                                                   (3, 3, 4, ALU.subtract), (4, 3, 4, ALU.add)):
                            nc.vector.tensor_tensor(dst[:, o:o + 1], src[:, base:base + 1], src[:, delta:delta + 1], op)
                        nc.vector.tensor_copy(dst[:, 2:3], src[:, 2:3])
                    dve.drain()
                    nc.vector.tensor_copy(w_out[:], spread(cols[:, 5, 0:5].unsqueeze(2), [P, 5, P]))
                    dve.wait_ge(soft, 1)
                    nc.vector.tensor_tensor(cols[:, 9], cols[:, 9], cols[:, 10], ALU.add)
                    dve.drain()
                    nc.vector.scalar_tensor_tensor(head_cols[:, :, C_DECAY], cols[:, 9], -1.0, cols[:, 8],
                                                   ALU.mult, ALU.mult)
                    lg = pb[:, 0:2].rearrange("p k (i n) -> p (k i) n", n=BINS)
                    z = work[:, 0:2].rearrange("p k (i n) -> p (k i) n", n=BINS)
                    ez = work[:, 2:4].rearrange("p k (i n) -> p (k i) n", n=BINS)
                    zez = work[:, 4:6].rearrange("p k (i n) -> p (k i) n", n=BINS)
                    dve.wait_ge(logits, 1)
                    nc.vector.tensor_reduce(cols[:, 0], lg, AX_X, ALU.max)
                    dve.drain()
                    nc.vector.tensor_tensor(
                        z, lg, spread(cols[:, 0].unsqueeze(2), [P, B * TT, BINS]), ALU.subtract).then_inc(shifted, 1)
                    dve.wait_ge(exped, 1)
                    nc.vector.tensor_reduce(cols[:, 1], ez, AX_X, ALU.add).then_inc(summed, 1)
                    nc.vector.tensor_tensor(zez, ez, z, ALU.mult)
                    dve.drain()
                    nc.vector.tensor_reduce(cols[:, 3], zez, AX_X, ALU.add)
                    nc.vector.reciprocal(cols[:, 4], cols[:, 1])
                    dve.drain()
                    nc.vector.tensor_tensor(cols[:, 3], cols[:, 3], cols[:, 4], ALU.mult)
                    dve.drain()
                    dve.wait_ge(logged, 1)
                    nc.vector.tensor_tensor(cols[:, 3], cols[:, 2], cols[:, 3], ALU.subtract)
                    dve.drain()
                    ent = cols[:, 3].rearrange("p (b t) -> p t b", b=B).unsqueeze(3)
                    rows = work[:, 6].rearrange("p (t b m) -> p t b m", t=TT, b=B)
                    for tt in range(TT):
                        last = nc.vector.tensor_scalar(rows[:, tt], spread(ent[:, tt], [P, B, HID]),
                                                       LN_BINS_INV, None, ALU.mult)
                    last.then_inc(ent_rows, 1)
                    dve.wait_ge(ent_sum, 1)
                    nc.vector.tensor_scalar(ent_w[:], pb[:, 2], small[:, 0:1], None, ALU.mult)

        w_qkv = sb("w_qkv", [P, 3, DC, P])
        g2 = sb("g2", [P, P])
        cur = sb("cur", [P, 15])
        nq = sb("nq", [P, B, 2, 2, T])
        ks = sb("ks", [P, B, 2, T])
        bv = sb("bv", [P, B, 2, T])
        e1 = sb("e1", [P, 2, 2, T])
        tot = sb("tot", [P, 2 * T])
        tot_chunk = sb("tot_chunk", [P, B, PAIRS])
        x_inv = sb("x_inv", [P, PAIRS, P])
        y_inv = sb("y_inv", [P, 2, PAIRS, P])
        w_sb = sb("w_sb", [P, PAIRS, P])
        state = sb("state", [P, 2, P])
        r_sb = sb("r_sb", [P, 2, P])
        u_sb = sb("u_sb", [P, 2, P])
        kt_sb = sb("kt_sb", [P, 2, P])
        o_t = sb("o_t", [P, B, T])
        gates = sb("gates", [P, 3, T])
        hf = sb("hf", [P, T])
        rnorm = sb("rnorm", [P, T])
        apt = work[:].rearrange("p (r k) t -> p r (k t)", r=3).rearrange("p r (i w t) -> p r i w t", i=PAIRS, w=2)
        ERR, V_VH, V2, VH2, K2, CONV = 0, 2, 4, 6, 8, 10
        EN, L1P, RV, VN, VHN, RVV, KN, FEAT, HID1 = 0, 1, 5, 4, 6, 7, 8, 9, 10
        G, BANK_W, BANK_X, BANK_Y, BANK_RU, BANK_S, BANK_N = 0, 2, 3, 4, 5, 6, 7
        products = pb[:, G:G + 2]

        def tot_of(b, level):
            if level == 0:
                return e1[:, b % 2].rearrange("p r t -> p (r t)")
            if level == LEVELS:
                return tot_chunk[:, b]
            at = sum(2 * (T >> k) for k in range(1, level))
            return tot[:, at:at + 2 * (T >> level)]

        TILES = 3 * B
        PS, IS = LEVELS + 1, LEVELS
        w_in = sem("w_in")
        g2_in = sem("g2_in")
        cur_ready = sem("cur_ready")
        projected = sem("projected")
        tapped = sem("tapped")
        convolved = sem("convolved")
        silued = sem("silued")
        vhat = sem("vhat")
        vh_squared = sem("vh_squared")
        err_ready = sem("err_ready")
        squared = sem("squared")
        stats = sem("stats")
        rooted = sem("rooted")
        l1p_ready = sem("l1p_ready")
        feat_ready = sem("feat_ready")
        hid1_ready = sem("hid1_ready")
        hid2_sum = sem("hid2_sum")
        hf_ready = sem("hf_ready")
        piece_sum = sem("piece_sum")
        piece_used = sem("piece_used")
        k_copied = sem("k_copied")
        nq_ready = sem("nq_ready")
        bv_ready = sem("bv_ready")
        e1_ready = sem("e1_ready")
        apt_zeroed = sem("apt_zeroed")
        product = sem("product")
        kept = sem("kept")
        nq_decayed = sem("nq_decayed")
        ks_decayed = sem("ks_decayed")
        xy_ready = sem("xy_ready")
        w_sum = sem("w_sum")
        w_ready = sem("w_ready")
        xy_sum = sem("xy_sum")
        xy_grown = sem("xy_grown")
        kt_sum = sem("kt_sum")
        kt_ready = sem("kt_ready")
        r_sum = sem("r_sum")
        r_ready = sem("r_ready")
        u_sum = sem("u_sum")
        u_ready = sem("u_ready")
        o_sum = sem("o_sum")
        o_kept = sem("o_kept")
        s_sum = sem("s_sum")
        state_ready = sem("state_ready")
        o_squared = sem("o_squared")
        o_mean = sem("o_mean")
        o_root = sem("o_root")
        o_rroot = sem("o_rroot")
        gate_sum = sem("gate_sum")
        gate_ready = sem("gate_ready")
        rroot_rows = sem("rroot_rows")
        o_ready = sem("o_ready")
        o_stored = sem("o_stored")
        cleared = sem("cleared")
        rounds = sem("rounds")
        passed = sem("passed")

        def slots():
            def batch(b):
                return b if 0 <= b < B else None
            for s in range(-1, B + 2):
                for step in range(PS):
                    yield batch(s + 1), batch(s), batch(s - 1), batch(s - 2), step

        with nc.Block() as block:

            @block.sync
            def _(sp):
                sp.sem_inc(o_stored, 1)
                sp.sem_inc(rounds, 1)
                sp.dma_start(w_qkv[:], io["w_qkv"][0]).then_inc(w_in, 16)
                with sp.Fori(0, H) as h:
                    sp.wait_ge(rounds, 5 * h + 1)
                    sp.dma_start(g2[:], io["g2"][h]).then_inc(g2_in, 16)
                    sp.wait_ge(projected, h * TILES + TILES)
                    sp.dma_start(w_qkv[:], io["w_qkv"][h + 1]).then_inc(w_in, 16)
                    sp.wait_ge(o_ready, h * B + B)
                    sp.dma_start(io["attn_o"][h], o_t[:].rearrange("p b t -> p (b t)")).then_inc(o_stored, 16)
                    sp.drain().then_inc(rounds, 1)
                sp.wait_ge(o_stored, 16 * ((H - 1) + 1) + 1)
                sp.wait_ge(w_in, 16 * (H + 1))

            @block.tensor
            def _(pe):
                with pe.Fori(0, H) as h:
                    pe.wait_ge(rounds, 5 * h + 1)
                    pe.wait_ge(w_in, 16 * (h + 1))
                    for t in range(TILES):
                        b, i = divmod(t, 3)
                        if t >= 8:
                            pe.wait_ge(convolved, h * TILES + t - 7)
                        for k in range(DC):
                            mm = nc.tensor.matmul(pb[:, t % 8], w_qkv[:, i, k], x_t[:, k, b * T:(b + 1) * T],
                                                  start=(k == 0), stop=(k == DC - 1))
                        mm.then_inc(projected, 1)
                    pe.wait_ge(convolved, h * TILES + TILES)
                    for b in range(B + 1):
                        if b < B:
                            pe.wait_ge(silued, h * TILES + 3 * b + 2)
                            if b >= 2:
                                pe.wait_ge(squared, h * B + b - 1)
                            nc.tensor.matmul(pb[:, b % 2], proxy[:], ks[:, b, 0], start=True, stop=True).then_inc(vhat, 1)
                        if b >= 1:
                            c = b - 1
                            pe.wait_ge(squared, h * B + c + 1)
                            for n, src in enumerate((ERR, V2, VH2, K2, V_VH)):
                                mm = nc.tensor.matmul(pb[32 * c:32 * c + 32, 2 + n], ones[:], work[:, src + c % 2],
                                                      start=True, stop=True)
                            mm.then_inc(stats, 1)
                    pe.wait_ge(hid1_ready, h + 1)
                    nc.tensor.matmul(pb[:, 7], w2_diag[:], work[:, HID1], start=True, stop=True).then_inc(hid2_sum, 1)
                    pe.wait_ge(hf_ready, h + 1)

                    for bn, bp, bi, bs, step in slots():
                        if bn is not None and step < 6:
                            if bn or step:
                                pe.wait_ge(piece_used, h * 6 * B + 6 * bn + step)
                            if bs is not None and step % 2:
                                pe.wait_ge(kt_ready, h * TT * B + TT * bs + step // 2 + 1)
                            elif bs is not None and TT * bs + step // 2:
                                pe.wait_ge(o_kept, h * TT * B + TT * bs + step // 2)
                            q = slice(32 * bn, 32 * bn + 32)
                            w, rows = (sel[q, :], rnorm[q, :]) if step == P_NORM else (w_out[q, step - 1], hf[q, :])
                            nc.tensor.matmul(pb[:, BANK_N], w, rows, start=True, stop=True).then_inc(piece_sum, 1)
                        if bp is not None:
                            if step == 0:
                                pe.wait_ge(nq_ready, h * B + bp + 1)
                                pe.wait_ge(k_copied, h * B + bp + 1)
                            else:
                                pe.wait_ge(nq_decayed, h * PS * B + PS * bp + step)
                            if step >= 2:
                                pe.wait_ge(ks_decayed, h * LEVELS * B + LEVELS * bp + step - 1)
                            if bp or step:
                                pe.wait_ge(kept, h * PS * B + PS * bp + step)
                            for i in range(PAIRS):
                                rate, c = divmod(i, TT)
                                chunk = slice(c * P, (c + 1) * P)
                                out = products[:, rate, c * P:(c + 1) * P]
                                rhs = nq[:, bp, rate, QUERY, chunk]
                                if step:
                                    rhs = right(nq[:, bp, rate, :, chunk], 1 << (step - 1))
                                    out = out.rearrange("p (w s h) -> p w s h", w=2, h=1 << (step - 1))
                                mm = nc.tensor.matmul(out, ks[:, bp, rate, chunk], rhs, start=True, stop=True)
                            mm.then_inc(product, 1)
                        if bi is not None and step < IS:
                            hs = 1 << step
                            if step == 0:
                                pe.wait_ge(xy_ready, h * B + bi + 1)
                                pe.wait_ge(kept, h * PS * B + PS * bi + PS)
                            else:
                                pe.wait_ge(xy_grown, h * IS * B + IS * bi + step)
                            for i in range(PAIRS):
                                mm = nc.tensor.matmul(
                                    compact(pb[:, BANK_W:BANK_W + 1, i * HALF:(i + 1) * HALF], hs)[:, 0],
                                    apt[:, bi % 3, i, NEG_K], left(x_inv[:, i:i + 1], hs)[:, 0], start=True, stop=True)
                            mm.then_inc(w_sum, 1)
                        if bs is not None:
                            c = step // 2
                            n = TT * bs + c
                            chunk = slice(c * P, (c + 1) * P)
                            if step % 2 == 0:
                                if c == 0:
                                    pe.wait_ge(nq_decayed, h * PS * B + PS * (bs + 1))
                                    pe.wait_ge(ks_decayed, h * LEVELS * B + LEVELS * (bs + 1))
                                if n:
                                    pe.wait_ge(u_ready, h * TT * B + n)
                                    pe.wait_ge(o_kept, h * TT * B + n)
                                pe.wait_ge(piece_used, h * 6 * B + (6 * B if bn is None else 6 * bn + min(step + 1, 6)))
                                for rate in (SLOW, FAST):
                                    mm = nc.tensor.transpose(pb[:, BANK_N, rate * P:(rate + 1) * P],
                                                             ks[:, bs, rate, chunk], ident[:])
                                mm.then_inc(kt_sum, 1)
                                if c:
                                    pe.wait_ge(state_ready, h * ((TT - 1) * B) + (TT - 1) * bs + c)
                                else:
                                    pe.wait_ge(bv_ready, h * B + bs + 1)
                                for rate in (SLOW, FAST):
                                    out = pb[:, BANK_RU, rate * P:(rate + 1) * P]
                                    mm = nc.tensor.matmul(out, bv[:, bs, rate, chunk], ident[:], start=True, stop=(c == 0))
                                    if c:
                                        mm = nc.tensor.matmul(out, nq[:, bs, rate, NEG_K, chunk], state[:, rate],
                                                              start=False, stop=True)
                                mm.then_inc(r_sum, 1)
                            else:
                                pe.wait_ge(u_ready, h * TT * B + n + 1)
                                pe.wait_ge(kt_ready, h * TT * B + n + 1)
                                pe.wait_ge(piece_used, h * 6 * B + (6 * B if bn is None else 6 * bn + min(step + 1, 6)))
                                out = pb[:, BANK_N, 0:P]
                                for rate in (SLOW, FAST):
                                    mm = nc.tensor.matmul(out, u_sb[:, rate], apt[:, bs % 3, rate * TT + c, QUERY],
                                                          start=(rate == SLOW), stop=(rate == FAST and c == 0))
                                if c:
                                    for rate in (SLOW, FAST):
                                        mm = nc.tensor.matmul(out, state[:, rate], nq[:, bs, rate, QUERY, chunk],
                                                              start=False, stop=(rate == FAST))
                                mm.then_inc(o_sum, 1)
                                for rate in (SLOW, FAST):
                                    mm = nc.tensor.matmul(pb[:, BANK_S, rate * P:(rate + 1) * P], kt_sb[:, rate],
                                                          u_sb[:, rate], start=True, stop=True)
                                mm.then_inc(s_sum, 1)
                        if bi is not None and step < IS:
                            hs = 1 << step
                            pe.wait_ge(w_ready, h * IS * B + IS * bi + step + 1)
                            if step < IS - 1:
                                for i in range(PAIRS):
                                    nc.tensor.matmul(
                                        compact(pb[:, BANK_X:BANK_X + 1, i * HALF:(i + 1) * HALF], hs)[:, 0],
                                        y_inv[:, bi % 2, i], left(w_sb[:, i:i + 1], hs)[:, 0], start=True, stop=True)
                            for i in range(PAIRS):
                                mm = nc.tensor.matmul(
                                    compact(pb[:, BANK_Y:BANK_Y + 1, i * HALF:(i + 1) * HALF], hs)[:, 0],
                                    w_sb[:, i], right(y_inv[:, bi % 2, i:i + 1], hs)[:, 0], start=True, stop=True)
                            mm.then_inc(xy_sum, 1)
                        if bs is not None and step % 2 == 0:
                            c = step // 2
                            n = TT * bs + c
                            pe.wait_ge(r_ready, h * TT * B + n + 1)
                            if c == 0:
                                pe.wait_ge(xy_grown, h * IS * B + IS * (bs + 1))
                            for rate in (SLOW, FAST):
                                mm = nc.tensor.matmul(pb[:, BANK_RU, 256 + rate * P:256 + (rate + 1) * P],
                                                      y_inv[:, bs % 2, rate * TT + c], r_sb[:, rate],
                                                      start=True, stop=True)
                            mm.then_inc(u_sum, 1)

                    pe.wait_ge(g2_in, 16 * (h + 1))
                    pe.wait_ge(xy_grown, h * IS * B + IS * B)
                    pe.wait_ge(kept, h * PS * B + PS * B)
                    for b in range(B):
                        nc.tensor.matmul(pb[:, 1 + b], g2[:], g_t[:, b * T:(b + 1) * T],
                                                        start=True, stop=True).then_inc(gate_sum, 1)
                    for b in range(B):
                        pe.wait_ge(o_squared, h * B + b + 1)
                        mm = nc.tensor.matmul(pb[32 * b:32 * b + 32, 0], mean_w[:], work[:, b], start=True, stop=True)
                    mm.then_inc(o_mean, 1)
                    pe.wait_ge(o_rroot, h + 1)
                    for b in range(B):
                        q = slice(32 * b, 32 * b + 32)
                        nc.tensor.matmul(pb[:, (5 + b) % 8], sel[q, :], work[q, 5],
                                                          start=True, stop=True).then_inc(rroot_rows, 1)
                    pe.drain().then_inc(rounds, 1)

            @block.scalar
            def _(act):
                with act.Fori(0, H) as h:
                    act.wait_ge(rounds, 5 * h + 1)
                    act.wait_ge(cur_ready, h + 1)

                    def place(t):
                        b, i = divmod(t, 3)
                        return (ks[:, b, 0], bv[:, b, 0], nq[:, b, 0, QUERY])[i]

                    def silu(t):
                        act.wait_ge(convolved, h * TILES + t + 1)
                        nc.scalar.activation(place(t), work[:, CONV + t % 2], ACT.Silu).then_inc(silued, 1)

                    for t in range(TILES):
                        act.wait_ge(projected, h * TILES + t + 1)
                        if t >= 2:
                            act.wait_ge(silued, h * TILES + t - 1)
                        i = t % 3
                        nc.scalar.activation(work[:, CONV + t % 2], pb[:, t % 8], ACT.Copy,
                                                          scale=cur[:, 4 * i + 3:4 * i + 4]).then_inc(tapped, 1)
                        if t >= 1:
                            silu(t - 1)
                    silu(TILES - 1)
                    for b in range(B):
                        act.wait_ge(vhat, h * B + b + 1)
                        if b >= 2:
                            act.wait_ge(stats, h * B + b - 1)
                        nc.scalar.activation(work[:, VH2 + b % 2], pb[:, b % 2], ACT.Square).then_inc(vh_squared, 1)
                        act.wait_ge(silued, h * TILES + 3 * b + 3)
                        nc.scalar.activation(work[:, V2 + b % 2], bv[:, b, 0], ACT.Square)
                        nc.scalar.activation(work[:, K2 + b % 2], ks[:, b, 0], ACT.Square)
                        act.wait_ge(err_ready, h * B + b + 1)
                        nc.scalar.activation(work[:, ERR + b % 2], work[:, ERR + b % 2], ACT.Square).then_inc(squared, 1)
                    act.wait_ge(stats, h * B + B)
                    for n, dst in enumerate((EN, VN, VHN, KN)):
                        last = nc.scalar.activation(work[:, dst], pb[:, 2 + n], ACT.Sqrt)
                    last.then_inc(rooted, 1)
                    act.drain()
                    nc.scalar.activation(work[:, L1P], work[:, EN], ACT.Ln, bias=1.0).then_inc(l1p_ready, 1)
                    act.wait_ge(feat_ready, h + 1)
                    nc.scalar.activation(work[:, HID1], work[:, FEAT], ACT.Silu,
                                                          bias=cur[:, C_BIAS1:C_BIAS1 + 1]).then_inc(hid1_ready, 1)
                    act.wait_ge(hid2_sum, h + 1)
                    nc.scalar.activation(hf[:], pb[:, 7], ACT.Silu, bias=small[:, 5:6]).then_inc(hf_ready, 1)

                    for bn, bp, bi, bs, step in slots():
                        if bn is not None and 1 <= step <= 5:
                            act.wait_ge(piece_sum, h * 6 * B + 6 * bn + step + 1)
                            if step == P_BETA_SLOW and bn:
                                act.wait_ge(nq_ready, h * B + bn)
                                act.wait_ge(bv_ready, h * B + bn)
                            if step == P_AMP_SLOW and bn >= 2:
                                act.wait_ge(nq_decayed, h * PS * B + PS * (bn - 1))
                                act.wait_ge(ks_decayed, h * LEVELS * B + LEVELS * (bn - 1))
                            dst = gates[:, step - 1] if step <= P_LAMBDA else e1[:, bn % 2, step - P_AMP_SLOW]
                            nc.scalar.activation(dst, pb[:, BANK_N], ACT.Sigmoid,
                                                                  bias=b_out[:, step - 1:step]).then_inc(piece_used, 1)
                        if bn is not None and step == 6:
                            act.drain()
                            nc.scalar.activation(e1[:, bn % 2], e1[:, bn % 2], ACT.Exp,
                                                                scale=cur[:, C_DECAY:C_DECAY + 1]).then_inc(e1_ready, 1)
                        if bi is not None and step < IS:
                            act.wait_ge(w_sum, h * IS * B + IS * bi + step + 1)
                            if bi or step:
                                act.wait_ge(xy_sum, h * IS * B + IS * bi + step)
                            else:
                                act.wait_ge(cleared, 1)
                            nc.scalar.copy(left(w_sb[:], 1 << step),
                                                         compact(pb[:, BANK_W].rearrange("p (i t) -> p i t", i=PAIRS),
                                                                 1 << step)).then_inc(w_ready, 1)
                        if bs is not None:
                            c = step // 2
                            n = TT * bs + c
                            if step % 2 == 0:
                                act.wait_ge(kt_sum, h * TT * B + n + 1)
                                if n:
                                    act.wait_ge(s_sum, h * TT * B + n)
                                nc.scalar.copy(kt_sb[:], pb[:, BANK_N, 0:256].rearrange(
                                    "p (r t) -> p r t", r=2)).then_inc(kt_ready, 1)
                                act.wait_ge(r_sum, h * TT * B + n + 1)
                                nc.scalar.copy(r_sb[:], pb[:, BANK_RU, 0:256].rearrange(
                                    "p (r t) -> p r t", r=2)).then_inc(r_ready, 1)
                                act.wait_ge(u_sum, h * TT * B + n + 1)
                                nc.scalar.copy(u_sb[:], pb[:, BANK_RU, 256:512].rearrange(
                                    "p (r t) -> p r t", r=2)).then_inc(u_ready, 1)
                            else:
                                if n == 0:
                                    act.wait_ge(o_stored, 16 * h + 1)
                                act.wait_ge(o_sum, h * TT * B + n + 1)
                                nc.scalar.copy(o_t[:, bs, c * P:(c + 1) * P],
                                                            pb[:, BANK_N, 0:P]).then_inc(o_kept, 1)
                    act.wait_ge(s_sum, h * TT * B + TT * B)
                    act.sem_inc(passed, 1)
                    act.drain()
                    for b in range(B):
                        nc.scalar.activation(work[:, b], o_t[:, b], ACT.Square).then_inc(o_squared, 1)
                    for b in range(B):
                        act.wait_ge(gate_sum, h * B + b + 1)
                        nc.scalar.activation(work[:, 6 + b], pb[:, 1 + b], ACT.Sigmoid,
                                                              bias=cur[:, C_G2B:C_G2B + 1]).then_inc(gate_ready, 1)
                    act.wait_ge(o_mean, h + 1)
                    nc.scalar.activation(work[:, 4], pb[:, 0], ACT.Sqrt, bias=eps_col[:]).then_inc(o_root, 1)
                    act.drain().then_inc(rounds, 1)

            @block.vector
            def _(dve):
                nc.vector.memset(w_sb[:], 0.0)
                dve.drain().then_inc(cleared, 1)
                with dve.Fori(0, H) as h:
                    dve.wait_ge(rounds, 5 * h + 1)
                    nc.vector.tensor_copy(cur[:].unsqueeze(1), head_cols[:, bass.ds(h, 1), :]).then_inc(cur_ready, 1)
                    dve.drain()
                    for t in range(TILES):
                        i = t % 3
                        dve.wait_ge(tapped, h * TILES + t + 1)
                        acc = work[:, CONV + t % 2]
                        for s in range(1, 4):
                            last = nc.vector.scalar_tensor_tensor(
                                acc[:, s:T], pb[:, t % 8, 0:T - s], cur[:, 4 * i + 3 - s:4 * i + 4 - s],
                                acc[:, s:T], ALU.mult, ALU.add)
                            if s < 3:
                                dve.drain()
                        last.then_inc(convolved, 1)
                    for b in range(B):
                        dve.wait_ge(vh_squared, h * B + b + 1)
                        dve.wait_ge(silued, h * TILES + 3 * b + 2)
                        if b >= 2:
                            dve.wait_ge(stats, h * B + b - 1)
                        nc.vector.tensor_tensor(work[:, ERR + b % 2], bv[:, b, 0], pb[:, b % 2], ALU.subtract)
                        nc.vector.tensor_tensor(work[:, V_VH + b % 2], bv[:, b, 0], pb[:, b % 2], ALU.mult).then_inc(err_ready, 1)
                    dve.wait_ge(rooted, h + 1)
                    nc.vector.tensor_scalar(work[:, KN], work[:, KN], EPS, None, ALU.add)
                    nc.vector.tensor_scalar(work[:, RV], work[:, VN], EPS, None, ALU.add)
                    nc.vector.tensor_tensor(work[:, RVV], work[:, VN], work[:, VHN], ALU.mult)
                    dve.drain()
                    nc.vector.tensor_scalar(work[:, RVV], work[:, RVV], EPS, None, ALU.add)
                    nc.vector.reciprocal(work[:, RV], work[:, RV])
                    nc.vector.reciprocal(rnorm[:], work[:, KN])
                    dve.drain()
                    nc.vector.reciprocal(work[:, RVV], work[:, RVV])
                    nc.vector.tensor_tensor(work[:, RV], work[:, EN], work[:, RV], ALU.mult)
                    dve.drain()
                    nc.vector.tensor_tensor(work[:, RVV], pb[:, 6], work[:, RVV], ALU.mult)
                    nc.vector.scalar_tensor_tensor(work[:, FEAT], work[:, RV], small[:, 1:2], ent_w[:], ALU.mult, ALU.add)
                    dve.drain()
                    nc.vector.scalar_tensor_tensor(work[:, FEAT], work[:, RVV], small[:, 2:3], work[:, FEAT],
                                                   ALU.mult, ALU.add)
                    dve.drain()
                    dve.wait_ge(l1p_ready, h + 1)
                    nc.vector.scalar_tensor_tensor(
                        work[:, FEAT], work[:, L1P], small[:, 3:4], work[:, FEAT], ALU.mult, ALU.add).then_inc(feat_ready, 1)

                    for bn, bp, bi, bs, step in slots():
                        if bn is not None:
                            if step == P_NORM:
                                dve.wait_ge(piece_sum, h * 6 * B + 6 * bn + 1)
                                nc.vector.tensor_tensor(ks[:, bn, 0], ks[:, bn, 0],
                                                                         pb[:, BANK_N], ALU.mult).then_inc(piece_used, 1)
                            if step == 4:
                                dve.wait_ge(piece_used, h * 6 * B + 6 * bn + P_LAMBDA + 1)
                                query = nq[:, bn, SLOW, QUERY]
                                nc.vector.scalar_tensor_tensor(nq[:, bn, FAST, QUERY], query, Q_SCALE,
                                                               gates[:, P_LAMBDA - 1], ALU.mult, ALU.mult)
                                dve.drain()
                                nc.vector.scalar_tensor_tensor(query, query, Q_SCALE, nq[:, bn, FAST, QUERY],
                                                               ALU.mult, ALU.subtract)
                            if step == 5:
                                for rate in (SLOW, FAST):
                                    last = nc.vector.scalar_tensor_tensor(
                                        nq[:, bn, rate, NEG_K], ks[:, bn, 0], -1.0, gates[:, P_BETA_SLOW - 1 + rate],
                                        ALU.mult, ALU.mult)
                                last.then_inc(nq_ready, 1)
                        if bp is not None:
                            dve.drain()
                            dve.wait_ge(product, h * PS * B + PS * bp + step + 1)
                            if step == 0:
                                if bp >= 3:
                                    dve.wait_ge(o_sum, h * TT * B + TT * (bp - 2))
                                else:
                                    dve.wait_ge(hf_ready, h + 1)
                                nc.vector.tensor_tensor(
                                    apt[:, bp % 3, :, QUERY], products.rearrange("p r (c t) -> p (r c) t", c=TT),
                                    spread(ident[:].unsqueeze(1), [P, PAIRS, P]), ALU.mult).then_inc(kept, 1)
                                dve.wait_ge(e1_ready, h * B + bp + 1)
                                for rate in (SLOW, FAST):
                                    last = nc.vector.tensor_tensor(
                                        nq[:, bp, rate], nq[:, bp, rate],
                                        spread(e1[:, bp % 2, rate:rate + 1], [P, 2, T]), ALU.mult)
                                last.then_inc(nq_decayed, 1)
                            else:
                                level = step - 1
                                hs = 1 << level
                                if level == 0:
                                    dve.wait_ge(apt_zeroed, h * B + bp + 1)
                                dve.sem_inc(passed, 1)
                                nc.vector.copy_predicated(
                                    right(apt[:, bp % 3].rearrange("p i w t -> p (i w) t"), hs),
                                    spread(compact(mask_u[:, level:level + 1], hs), [P, 2 * PAIRS, HALF // hs, hs]),
                                    compact(products.rearrange("p r (c t) -> p (r c) t", t=HALF), hs)).then_inc(kept, 1)
                                blocks = tot_of(bp, level).rearrange("p (r s two) -> p r s two", r=2, two=2)
                                for rate in (SLOW, FAST):
                                    part = right(nq[:, bp, rate], hs)
                                    last = nc.vector.tensor_tensor(
                                        part, part, spread(blocks[:, rate:rate + 1, :, 0:1], [P, 2, T // (2 * hs), hs]),
                                        ALU.mult)
                                pairs = tot_of(bp, level).rearrange("p (s two) -> p s two", two=2)
                                nc.vector.tensor_tensor(tot_of(bp, level + 1), pairs[:, :, 0],
                                                                         pairs[:, :, 1], ALU.mult).then_inc(nq_decayed, 1)
                        if bs is not None and step % 2 == 1 and step < PS - 1:
                            c = step // 2
                            dve.wait_ge(s_sum, h * TT * B + TT * bs + c + 1)
                            for rate in (SLOW, FAST):
                                part = pb[:, BANK_S, rate * P:(rate + 1) * P]
                                if c == 0:
                                    last = nc.vector.tensor_copy(state[:, rate], part)
                                else:
                                    i = rate * TT + c
                                    last = nc.vector.scalar_tensor_tensor(
                                        state[:, rate], state[:, rate], tot_chunk[:, bs, i:i + 1], part,
                                        ALU.mult, ALU.add)
                            last.then_inc(state_ready, 1)
                        if bi is not None and step < IS:
                            hs = 1 << step
                            dve.wait_ge(xy_sum, h * IS * B + IS * bi + step + 1)
                            dve.sem_inc(passed, 1)
                            if step < IS - 1:
                                nc.vector.copy_predicated(
                                    left(x_inv[:], hs),
                                    spread(compact(mask_l[:, step:step + 1], hs), [P, PAIRS, HALF // hs, hs]),
                                    compact(pb[:, BANK_X].rearrange("p (i t) -> p i t", i=PAIRS), hs))
                            nc.vector.copy_predicated(
                                right(y_inv[:, bi % 2], hs),
                                spread(compact(mask_u[:, step:step + 1], hs), [P, PAIRS, HALF // hs, hs]),
                                compact(pb[:, BANK_Y].rearrange("p (i t) -> p i t", i=PAIRS), hs)).then_inc(xy_grown, 1)

                    dve.wait_ge(o_root, h + 1)
                    nc.vector.reciprocal(work[:, 5], work[:, 4]).then_inc(o_rroot, 1)
                    for b in range(B):
                        dve.wait_ge(rroot_rows, h * B + b + 1)
                        nc.vector.scalar_tensor_tensor(o_t[:, b], o_t[:, b], small[:, 16:17], pb[:, (5 + b) % 8],
                                                       ALU.mult, ALU.mult)
                        dve.drain()
                        dve.wait_ge(gate_ready, h * B + b + 1)
                        nc.vector.tensor_tensor(o_t[:, b], o_t[:, b], work[:, 6 + b], ALU.mult).then_inc(o_ready, 1)
                    dve.drain().then_inc(rounds, 1)

            @block.gpsimd
            def _(pool):
                with pool.Fori(0, H) as h:
                    pool.wait_ge(rounds, 5 * h + 1)
                    pool.wait_ge(hf_ready, h + 1)
                    for bn, bp, bi, bs, step in slots():
                        if bn is not None and step == 0:
                            pool.wait_ge(piece_used, h * 6 * B + 6 * bn + 1)
                            pool.sem_inc(passed, 1)
                            nc.gpsimd.tensor_copy(ks[:, bn, 1], ks[:, bn, 0]).then_inc(k_copied, 1)
                        if bp is not None and step == 0:
                            if bp >= 3:
                                pool.wait_ge(w_sum, h * IS * B + IS * (bp - 2))
                                pool.sem_inc(passed, 1)
                            nc.gpsimd.memset(apt[:, bp % 3, :, NEG_K], 0.0).then_inc(apt_zeroed, 1)
                        if bp is not None and step >= 1:
                            level = step - 1
                            hs = 1 << level
                            pool.wait_ge(product, h * PS * B + PS * bp + step + 1)
                            pool.wait_ge(nq_decayed, h * PS * B + PS * bp + step)
                            if level:
                                pool.wait_ge(ks_decayed, h * LEVELS * B + LEVELS * bp + level)
                            part = left(ks[:, bp].rearrange("p r t -> p (r t)").unsqueeze(1), hs)[:, 0]
                            blocks = tot_of(bp, level).rearrange("p (s two) -> p s two", two=2)[:, :, 1:2]
                            nc.gpsimd.tensor_tensor(part, part, spread(blocks, [P, T // hs, hs]),
                                                                     ALU.mult).then_inc(ks_decayed, 1)
                        if bn is not None and step == 4:
                            pool.wait_ge(piece_used, h * 6 * B + 6 * bn + P_BETA_FAST + 1)
                            nc.gpsimd.tensor_tensor(bv[:, bn, FAST], bv[:, bn, SLOW], gates[:, P_BETA_FAST - 1], ALU.mult)
                            pool.drain()
                            nc.gpsimd.tensor_tensor(bv[:, bn, SLOW], bv[:, bn, SLOW],
                                                                   gates[:, P_BETA_SLOW - 1], ALU.mult).then_inc(bv_ready, 1)
                        if bp is not None and step == PS - 1:
                            if bp >= 1:
                                pool.wait_ge(xy_grown, h * IS * B + IS * bp)
                            if bp >= 2:
                                pool.wait_ge(u_sum, h * TT * B + TT * (bp - 1))
                            pool.sem_inc(passed, 1)
                            every = spread(ident[:].unsqueeze(1), [P, PAIRS, P])
                            nc.gpsimd.tensor_copy(x_inv[:], every)
                            nc.gpsimd.tensor_copy(y_inv[:, bp % 2], every).then_inc(xy_ready, 1)
                    pool.drain().then_inc(rounds, 1)


def norm_deviation(act, stats, eps_col, var_ready, dev_ready, due):
    act.wait_ge(var_ready, due)
    act.activation(stats[:, :, 6:7], stats[:, :, 7:8], ACT.Sqrt, bias=eps_col[:]).then_inc(dev_ready, 1)


def norm_rows(dve, sums, stats, out, var_ready, dev_ready, due):
    dve.drain()
    for i in range(sums.shape[1]):
        dve.bn_stats(stats[:, i, 0:6], sums[:, i])
    dve.drain()
    for i in range(sums.shape[1]):
        dve.bn_aggr(stats[:, i, 8:10], stats[:, i, 0:6])
    dve.drain()
    dve.tensor_copy(stats[:, :, 7:8], stats[:, :, 9:10]).then_inc(var_ready, 1)
    dve.wait_ge(dev_ready, due)
    dve.reciprocal(stats[:, :, 6:7], stats[:, :, 6:7])
    dve.drain()
    for i in range(sums.shape[1]):
        last = dve.tensor_scalar(out[:, i], sums[:, i], stats[:, i, 8:9], stats[:, i, 6:7],
                                 ALU.subtract, ALU.mult)
    return last


def block_stage(nc, io):
    with ExitStack() as ctx:
        def sb(name, shape, dt=F32):
            return ctx.enter_context(nc.sbuf_tensor("b_" + name, shape, dt))

        def sem(name):
            return ctx.enter_context(nc.semaphore("b_" + name))

        pb = ctx.enter_context(nc.psum_tensor("b_pb", [P, 8, 512], F32))
        GROUPS, GH = 4, H // 4
        NORMS = 2
        ident = sb("ident", [P, P])
        eps_col = sb("eps_col", [P, 1])
        w_o = sb("w_o", [P, H, D])
        o_t = sb("o_t", [P, GROUPS, GH, T])
        x_in = sb("x_in", [P, TT, D])
        y_in = sb("y_in", [P, ET, T])
        sums = sb("sums", [P, TT, D])
        x1 = sb("x1", [P, TT, D])
        gated = sb("gated", [P, TT, D])
        x2 = sb("x2", [P, TT, D])
        x2_t = sb("x2_t", [P, DC, T])
        stats = sb("stats", [P, TT, 10])

        weights = sem("weights")
        o_in = [sem(f"o_in{g}") for g in range(GROUPS)]
        o_used = [sem(f"o_used{g}") for g in range(GROUPS)]
        x_loaded = sem("x_loaded")
        y_loaded = sem("y_loaded")
        x_used = sem("x_used")
        y_used = sem("y_used")
        eps_ready = sem("eps_ready")
        attn_sum = sem("attn_sum")
        var_ready = sem("var_ready")
        dev_ready = sem("dev_ready")
        x1_ready = sem("x1_ready")
        silu_ready = sem("silu_ready")
        gated_ready = sem("gated_ready")
        turned = sem("turned")
        x2_ready = sem("x2_ready")
        x2_turned = sem("x2_turned")
        x2_t_ready = sem("x2_t_ready")
        x2_stored = sem("x2_stored")
        x2_t_stored = sem("x2_t_stored")
        rounds = sem("rounds")
        passed = sem("passed")

        with nc.Block() as block:

            @block.sync
            def _(sp):
                sp.dma_start(ident[:], io["ident"]).then_inc(weights, 16)
                sp.dma_start(w_o[:], io["w_o"]).then_inc(weights, 16)
                for s in (*o_used, x_used, y_used, rounds):
                    sp.sem_inc(s, 1)
                with sp.Fori(0, B) as b:
                    for g in range(GROUPS):
                        sp.wait_ge(o_used[g], b + 1)
                        sp.dma_start(
                            o_t[:, g], io["attn_o"][g * GH:(g + 1) * GH, :, bass.ds(b * T, T)].rearrange("h p t -> p h t")).then_inc(o_in[g], 16)
                    sp.wait_ge(x_used, b + 1)
                    sp.dma_start(x_in[:], io["x_rows"][b]).then_inc(x_loaded, 16)
                    sp.wait_ge(y_used, b + 1)
                    sp.dma_start(y_in[:], io["y_ssm"][b].rearrange("e p t -> p e t")).then_inc(y_loaded, 16)

            @block.tensor
            def _(pe):
                pe.wait_ge(weights, 32)
                with pe.Fori(0, B) as b:
                    pe.wait_ge(rounds, 3 * b + 1)
                    for g in range(GROUPS):
                        pe.wait_ge(o_in[g], 16 * (b + 1))
                        for k in range(GH):
                            for tt in range(TT):
                                first, last = g + k == 0, g * GH + k == H - 1
                                mm = nc.tensor.matmul(pb[:, tt], o_t[:, g, k, tt * P:(tt + 1) * P],
                                                      w_o[:, g * GH + k], start=first, stop=last)
                        mm.then_inc(o_used[g], 1)
                    pe.drain().then_inc(attn_sum, 1)
                    pe.wait_ge(gated_ready, b + 1)
                    for lt in range(TT):
                        for et in range(ET):
                            mm = nc.tensor.transpose(pb[:, 4 + lt, et * P:(et + 1) * P],
                                                     gated[:, et, lt * P:(lt + 1) * P], ident[:])
                    mm.then_inc(turned, 1)
                    pe.wait_ge(x2_ready, b + 1)
                    for k in range(DC):
                        for lt in range(TT):
                            mm = nc.tensor.transpose(pb[:, k, lt * P:(lt + 1) * P],
                                                     x2[:, lt, k * P:(k + 1) * P], ident[:])
                    mm.then_inc(x2_turned, 1)
                    pe.drain().then_inc(rounds, 1)

            @block.scalar
            def _(act):
                act.wait_ge(eps_ready, 1)
                with act.Fori(0, B) as b:
                    act.wait_ge(rounds, 3 * b + 1)
                    norm_deviation(act, stats, eps_col, var_ready, dev_ready, NORMS * b + 1)
                    act.wait_ge(x1_ready, b + 1)
                    nc.scalar.activation(gated[:], x1[:], ACT.Silu).then_inc(silu_ready, 1)
                    norm_deviation(act, stats, eps_col, var_ready, dev_ready, NORMS * b + 2)
                    act.wait_ge(x2_ready, b + 1)
                    act.dma_start(io["x2_rows"][b], x2[:]).then_inc(x2_stored, 16)
                    act.wait_ge(x2_turned, b + 1)
                    nc.scalar.copy(x2_t[:], pb[:, 0:DC]).then_inc(x2_t_ready, 1)
                    act.wait_ge(x2_t_ready, b + 1)
                    act.dma_start(io["x2_t"][b], x2_t[:]).then_inc(x2_t_stored, 16)
                    act.wait_ge(x2_stored, 16 * (b + 1))
                    act.wait_ge(x2_t_stored, 16 * (b + 1))
                    act.sem_inc(passed, 1)
                    act.drain().then_inc(rounds, 1)

            @block.vector
            def _(dve):
                nc.vector.memset(eps_col[:], NORM_EPS).then_inc(eps_ready, 1)
                with dve.Fori(0, B) as b:
                    dve.wait_ge(rounds, 3 * b + 1)
                    dve.wait_ge(x_loaded, 16 * (b + 1))
                    dve.wait_ge(attn_sum, b + 1)
                    nc.vector.tensor_tensor(sums[:], x_in[:], pb[:, 0:TT], ALU.add).then_inc(x_used, 1)
                    norm_rows(dve, sums, stats, x1, var_ready, dev_ready, NORMS * b + 1).then_inc(x1_ready, 1)
                    dve.wait_ge(silu_ready, b + 1)
                    dve.wait_ge(y_loaded, 16 * (b + 1))
                    nc.vector.tensor_tensor(gated[:], y_in[:], gated[:], ALU.mult)
                    dve.drain().then_inc(y_used, 1)
                    dve.drain().then_inc(gated_ready, 1)
                    dve.wait_ge(turned, b + 1)
                    nc.vector.tensor_tensor(sums[:], x1[:], pb[:, 4:8], ALU.add)
                    norm_rows(dve, sums, stats, x2, var_ready, dev_ready, NORMS * b + 2).then_inc(x2_ready, 1)
                    dve.drain().then_inc(rounds, 1)


SECOND = (1, 2, 3, 4, 5, 6, 0)


def mlp_stage(nc, io):
    with ExitStack() as ctx:
        def sb(name, shape, dt=F32):
            return ctx.enter_context(nc.sbuf_tensor("f_" + name, shape, dt))

        def sem(name):
            return ctx.enter_context(nc.semaphore("f_" + name))

        pb = ctx.enter_context(nc.psum_tensor("f_pb", [P, 8, 512], F32))
        ident = sb("ident", [P, P])
        eps_col = sb("eps_col", [P, 1])
        signs = sb("signs", [P, 2])
        before = sb("before", [P, E, E])
        w_gu = sb("w_gu", [P, 2, DC, DFF])
        w_d = sb("w_d", [P, FC, D])
        w_r = sb("w_r", [P, DC, E])
        a_gu = sb("a_gu", [P, 2, 2, DC, P])
        b_gu = sb("b_gu", [P, 2, 2, DFF])
        a_d = sb("a_d", [P, FC, E, 2 * R])
        b_d = sb("b_d", [P, D])
        x2_t = sb("x2_t", [P, DC, T])
        rank_rows = sb("rank_rows", [P, 2, 2, T])
        probs = sb("probs", [P, 8, TT, E])
        compare = sb("compare", [P, 2, TT, E * E])
        e_w = sb("e_w", [P, TT, P])
        e_w_t = sb("e_w_t", [P, T])
        gate = sb("gate", [P, 3, T])
        h_base = sb("h_base", [P, FC, T])
        h_lora = sb("h_lora", [P, 4, T])
        sums = h_base[:, 0:4]
        x2 = h_base[:, 4:8]
        outs = h_base[:, 0:4]
        down = sb("down", [P, T])
        stats = sb("stats", [P, TT, 10])
        DOWN, SCORES = 6, 7
        NORMS = 1

        items = []
        for first in range(0, FC, 3):
            group = range(first, min(first + 3, FC))
            for e in range(-1, E):
                items += [(e, c, c - first) for c in group]
        number = {(e, c): n for n, (e, c, _) in enumerate(items)}
        last_in = {}
        held = {}
        for n, (e, c, j) in enumerate(items):
            last_in[n] = held.get(j)
            held[j] = n
        lora_items = [n for n, (e, c, j) in enumerate(items) if e >= 0]
        NI, NL, LAG, RING = len(items), len(lora_items), 2, 4

        weights = sem("weights")
        x2_t_in = sem("x2_t_in")
        x2_in = sem("x2_in")
        x2_t_used = sem("x2_t_used")
        eps_ready = sem("eps_ready")
        scores = sem("scores")
        shifted = sem("shifted")
        exped = sem("exped")
        e_w_ready = sem("e_w_ready")
        e_w_turned = sem("e_w_turned")
        e_w_t_ready = sem("e_w_t_ready")
        rank_sum = sem("rank_sum")
        rank_ready = sem("rank_ready")
        item_sum = sem("item_sum")
        gate_ready = sem("gate_ready")
        h_ready = sem("h_ready")
        down_sum = sem("down_sum")
        down_ready = sem("down_ready")
        out_sum = sem("out_sum")
        var_ready = sem("var_ready")
        dev_ready = sem("dev_ready")
        out_ready = sem("out_ready")
        stored = sem("stored")
        rounds = sem("rounds")
        passed = sem("passed")
        LOADS = 10

        with nc.Block() as block:

            @block.sync
            def _(sp):
                for dst, src in ((w_r, "w_r"), (ident, "ident"), (a_gu, "a_gu"), (signs, "signs"), (before, "before"),
                                 (w_gu, "w_gu"), (b_gu, "b_gu"), (a_d, "a_d"), (w_d, "w_d"), (b_d, "b_d")):
                    sp.dma_start(dst[:], io[src]).then_inc(weights, 16)
                for s in (x2_t_used, rounds):
                    sp.sem_inc(s, 1)
                with sp.Fori(0, B) as b:
                    sp.wait_ge(x2_t_used, b + 1)
                    sp.dma_start(x2_t[:], io["x2_t"][b]).then_inc(x2_t_in, 16)

            @block.tensor
            def _(pe):
                pe.wait_ge(weights, 16 * LOADS)
                with pe.Fori(0, B) as b:
                    pe.wait_ge(rounds, 3 * b + 1)
                    pe.wait_ge(x2_t_in, 16 * (b + 1))
                    for tt in range(TT):
                        for k in range(DC):
                            mm = nc.tensor.matmul(pb[:, SCORES, tt * E:(tt + 1) * E], x2_t[:, k, tt * P:(tt + 1) * P],
                                                  w_r[:, k], start=(k == 0), stop=(k == DC - 1))
                    mm.then_inc(scores, 1)
                    for n in range(4):
                        for k in range(DC):
                            mm = nc.tensor.matmul(pb[:, n], a_gu[:, n // 2, n % 2, k], x2_t[:, k],
                                                  start=(k == 0), stop=(k == DC - 1))
                        mm.then_inc(rank_sum, 1)
                    pe.wait_ge(rank_ready, b * 4 + 4)

                    def down_project(m):
                        n = lora_items[m]
                        e, c, _ = items[n]
                        pe.wait_ge(h_ready, b * NI + n + 1)
                        q = slice(32 * (e // 2), 32 * (e // 2) + 32)
                        nc.tensor.matmul(
                            pb[q, DOWN], a_d[:, c, e], h_lora[:, m % RING],
                            start=(c == 0 and e % 2 == 0), stop=(c == FC - 1 and e % 2 == 1), skip_group_check=True).then_inc(down_sum, 1)

                    m = 0
                    for n, (e, c, j) in enumerate(items):
                        if last_in[n] is not None:
                            pe.wait_ge(h_ready, b * NI + last_in[n] + 1)
                        cols = slice(c * P, (c + 1) * P)
                        for side in range(2):
                            out = pb[:, 2 * j + side]
                            if e < 0:
                                for k in range(DC):
                                    mm = nc.tensor.matmul(out, w_gu[:, side, k, cols], x2_t[:, k],
                                                          start=(k == 0), stop=(k == DC - 1), skip_group_check=True)
                            else:
                                arr, q = (1, 3) if e == 0 else (0, e // 2) if e % 2 else (1, e // 2 - 1)
                                q = slice(32 * q, 32 * q + 32)
                                mm = nc.tensor.matmul(out, b_gu[q, side, arr, cols], rank_rows[q, side, arr],
                                                      start=False, stop=True, skip_group_check=True)
                        mm.then_inc(item_sum, 1)
                        if n >= LAG and items[n - LAG][0] >= 0:
                            down_project(m)
                            m += 1
                        if n == 6:
                            pe.wait_ge(e_w_ready, b + 1)
                            for tt in range(TT):
                                mm = nc.tensor.matmul(pb[:, SCORES, tt * P:(tt + 1) * P], e_w[:, tt], ident[:],
                                                      start=True, stop=True)
                            mm.then_inc(e_w_turned, 1)
                    pe.drain().then_inc(x2_t_used, 1)
                    while m < NL:
                        down_project(m)
                        m += 1
                    pe.wait_ge(h_ready, b * NI + NI)
                    for tt in range(TT):
                        for c in range(FC):
                            nc.tensor.matmul(pb[:, tt], h_base[:, c, tt * P:(tt + 1) * P], w_d[:, c],
                                             start=(c == 0), stop=False)
                        if tt == 0:
                            pe.wait_ge(down_ready, b + 1)
                        mm = nc.tensor.matmul(pb[:, tt], down[:, tt * P:(tt + 1) * P], b_d[:],
                                              start=False, stop=True)
                    mm.then_inc(out_sum, 1)
                    pe.drain().then_inc(rounds, 1)

            @block.scalar
            def _(act):
                act.wait_ge(weights, 16 * LOADS)
                act.wait_ge(eps_ready, 1)
                with act.Fori(0, B) as b:
                    act.wait_ge(rounds, 3 * b + 1)
                    for n in range(4):
                        act.wait_ge(rank_sum, b * 4 + n + 1)
                        nc.scalar.activation(rank_rows[:, n // 2, n % 2], pb[:, n], ACT.Copy,
                                                              scale=signs[:, n % 2:n % 2 + 1]).then_inc(rank_ready, 1)
                    act.wait_ge(shifted, b + 1)
                    nc.scalar.activation(probs[:, 1], probs[:, 0], ACT.Exp).then_inc(exped, 1)
                    for n, (e, c, j) in enumerate(items):
                        act.wait_ge(item_sum, b * NI + n + 1)
                        if n >= 3:
                            act.wait_ge(h_ready, b * NI + n - 2)
                        nc.scalar.activation(gate[:, n % 3], pb[:, 2 * j], ACT.Silu).then_inc(gate_ready, 1)
                        if n == 8:
                            act.wait_ge(e_w_turned, b + 1)
                            nc.scalar.activation(e_w_t[:], pb[:, SCORES], ACT.Copy, scale=LORA_SCALE).then_inc(e_w_t_ready, 1)
                    act.wait_ge(out_sum, b + 1)
                    act.dma_start(x2, io["x2_rows"][b]).then_inc(x2_in, 16)
                    norm_deviation(act, stats, eps_col, var_ready, dev_ready, NORMS * b + 1)
                    act.wait_ge(out_ready, b + 1)
                    act.dma_start(io["out"][b], outs).then_inc(stored, 16)
                    act.wait_ge(stored, 16 * (b + 1))
                    act.sem_inc(passed, 1)
                    act.drain().then_inc(rounds, 1)

            @block.vector
            def _(dve):
                nc.vector.memset(eps_col[:], NORM_EPS).then_inc(eps_ready, 1)
                dve.wait_ge(weights, 16 * LOADS)
                with dve.Fori(0, B) as b:
                    dve.wait_ge(rounds, 3 * b + 1)
                    dve.wait_ge(scores, b + 1)
                    s = pb[:, SCORES, 0:TT * E].rearrange("p (t e) -> p t e", e=E)
                    nc.vector.tensor_reduce(probs[:, 2, :, 0], s, AX_X, ALU.max)
                    dve.drain()
                    nc.vector.tensor_tensor(probs[:, 0], s, spread(probs[:, 2, :, 0:1], [P, TT, E]),
                                                          ALU.subtract).then_inc(shifted, 1)
                    dve.wait_ge(exped, b + 1)
                    nc.vector.tensor_reduce(probs[:, 3, :, 0], probs[:, 1], AX_X, ALU.add)
                    dve.drain()
                    nc.vector.reciprocal(probs[:, 4, :, 0], probs[:, 3, :, 0])
                    dve.drain()
                    nc.vector.tensor_tensor(probs[:, 5], probs[:, 1], spread(probs[:, 4, :, 0:1], [P, TT, E]), ALU.mult)
                    dve.drain()
                    other = spread(probs[:, 5].unsqueeze(2), [P, TT, E, E])
                    own = spread(probs[:, 5].unsqueeze(3), [P, TT, E, E])
                    more = compare[:, 0].rearrange("p t (a c) -> p t a c", a=E)
                    same = compare[:, 1].rearrange("p t (a c) -> p t a c", a=E)
                    nc.vector.tensor_tensor(more, other, own, ALU.is_gt)
                    nc.vector.tensor_tensor(same, other, own, ALU.is_equal)
                    dve.drain()
                    nc.vector.tensor_tensor(compare[:, 1], compare[:, 1],
                                            spread(before[:].rearrange("p a c -> p (a c)").unsqueeze(1), [P, TT, E * E]),
                                            ALU.mult)
                    dve.drain()
                    nc.vector.tensor_tensor(more, more, same, ALU.add)
                    dve.drain()
                    nc.vector.tensor_reduce(probs[:, 6], more, AX_X, ALU.add)
                    dve.drain()
                    nc.vector.tensor_scalar(probs[:, 6], probs[:, 6], 1.5, None, ALU.is_lt)
                    dve.drain()
                    nc.vector.tensor_tensor(probs[:, 7], probs[:, 5], probs[:, 6], ALU.mult)
                    dve.drain()
                    nc.vector.tensor_copy(e_w[:].rearrange("p t (e r) -> p t e r", r=R),
                                                          spread(probs[:, 7].unsqueeze(3), [P, TT, E, R])).then_inc(e_w_ready, 1)
                    m = 0
                    for n, (e, c, j) in enumerate(items):
                        dve.wait_ge(gate_ready, b * NI + n + 1)
                        dst = h_base[:, c]
                        if e >= 0:
                            dst = h_lora[:, m % RING]
                            if m >= RING:
                                dve.wait_ge(down_sum, b * NL + m - RING + 1)
                            m += 1
                        nc.vector.tensor_tensor(dst, gate[:, n % 3], pb[:, 2 * j + 1], ALU.mult).then_inc(h_ready, 1)
                    dve.wait_ge(down_sum, b * NL + NL)
                    dve.wait_ge(e_w_t_ready, b + 1)
                    nc.vector.tensor_tensor(down[:], e_w_t[:], pb[:, DOWN], ALU.mult).then_inc(down_ready, 1)
                    dve.wait_ge(out_sum, b + 1)
                    dve.wait_ge(x2_in, 16 * (b + 1))
                    nc.vector.tensor_tensor(sums, x2, pb[:, 0:TT], ALU.add)
                    norm_rows(dve, sums, stats, outs, var_ready, dev_ready, NORMS * b + 1).then_inc(out_ready, 1)
                    dve.drain().then_inc(rounds, 1)


def layouts(inputs, np):
    a = {k.replace("L0_", ""): np.asarray(v) for k, v in inputs.items()}

    def pack(x):
        return np.ascontiguousarray(x)

    def rows(x, n):
        return pack(x.reshape(n, P, -1).transpose(1, 0, 2))

    ident = np.eye(P, dtype=np.float32)
    out = {"ident": ident}
    out["ctx_t"] = pack(a["ctx_1024"].transpose(0, 2, 1).reshape(B, 2, P, T).transpose(0, 2, 1, 3))
    out["ssm_in_w"] = rows(a["xattn_in_proj_w"].T, 2)
    out["ssm_x_w"] = rows(a["xattn_x_proj_w"].T, ET)
    out["ssm_dt_w"] = pack(a["xattn_dt_proj_w"].T)
    out["ssm_cols"] = rows(np.concatenate([
        a["xattn_conv_w"], a["xattn_conv_b"][:, None], a["xattn_dt_proj_b"][:, None], a["xattn_D"][:, None],
        a["xattn_A_log"]], axis=1), ET)
    out["x_t"] = rows(a["x"].reshape(B * T, D).T, DC)
    out["g1"] = rows(a["attn_g1_w"], DC)
    out["unc"] = rows(a["attn_unc_w"], DC)
    out["proxy"] = pack(a["attn_proxy_w"])
    out["mlp_w2"] = pack(a["attn_mlp_w2"])
    out["w1_embed"] = pack(np.tile(a["attn_mlp_w1"][4:8], (1, B)))
    out["embed_t"] = pack(a["attn_head_embed"].T)
    out["small"] = pack(np.concatenate([
        np.tile(a["attn_mlp_w1"][0:4].T, (B, 1)),
        np.tile(np.stack([a["attn_mlp_b1"], a["attn_mlp_b2"]], 1), (B, 1)),
        np.tile(np.stack([a["attn_" + n + "_w"] for n in ("bb", "bd", "lam", "ab", "ad")], 1), (B, 1)),
        np.tile(np.stack([a["attn_" + n + "_b"] for n in ("bb", "bd", "lam", "ab", "ad")], 1), (P, 1)),
        a["attn_onorm_w"][:, None],
        np.tile(a["attn_A_log"][None, :], (P, 1)),
        a["attn_dt_bias"].reshape(H, P).T], axis=1))
    taps = [a["attn_conv_" + n + "_w"].reshape(H, P, 4) for n in "kvq"]
    out["head_cols"] = pack(np.concatenate(taps + [a["attn_g2_b"].reshape(H, P, 1)], axis=2).transpose(1, 0, 2))
    heads = np.stack([a["attn_w" + n].reshape(DC, P, H, P).transpose(2, 1, 0, 3) for n in "kvq"], axis=2)
    out["w_qkv"] = pack(np.concatenate([heads, np.zeros_like(heads[:1])]))
    out["g2"] = pack(a["attn_g2_w"].reshape(P, H, P).transpose(1, 0, 2))
    token = np.arange(P)[:, None]
    upper, lower = [], []
    for level in range(LEVELS):
        h = 1 << level
        block = (np.arange(HALF) // h)[None, :]
        upper.append((token // h == 2 * block).astype(np.int32))
        lower.append((token // h == 2 * block + 1).astype(np.int32))
    out["mask_u"] = pack(np.stack(upper, 1))
    out["mask_l"] = pack(np.stack(lower, 1))
    sel = np.zeros((P, P), np.float32)
    sel[::32] = 1.0
    out["sel"] = sel
    out["x_rows"] = pack(a["x"].reshape(B, TT, P, D).transpose(0, 2, 1, 3))
    out["w_o"] = rows(a["attn_wo"], H)
    out["w_gu"] = pack(np.stack([rows(a["ffn_W" + n].T, DC) for n in "gu"], 1))
    out["w_d"] = rows(a["ffn_Wd"].T, FC)
    out["w_r"] = rows(a["ffn_Wr"].T, DC)

    def second(x):
        return np.concatenate([x[list(SECOND)], np.zeros_like(x[:1])])

    def a_rows(x):
        return rows(x.reshape(E * R, D).T, DC)

    def b_rows(x):
        return x.transpose(0, 2, 1).reshape(E * R, -1)

    out["a_gu"] = pack(np.stack([np.stack([a_rows(a["ffn_A" + n]), a_rows(second(a["ffn_A" + n]))], 1)
                                 for n in "gu"], 1))
    out["b_gu"] = pack(np.stack([np.stack([b_rows(a["ffn_B" + n]), b_rows(second(a["ffn_B" + n]))], 1)
                                 for n in "gu"], 1))
    a_d = np.zeros((P, FC, E, 2, R), np.float32)
    for e in range(E):
        a_d[:, :, e, e % 2] = rows(a["ffn_Ad"][e].T, FC)
    out["a_d"] = pack(a_d.reshape(P, FC, E, 2 * R))
    out["b_d"] = pack(b_rows(a["ffn_Bd"]))
    signs = np.full((E, R, 2), LORA_SCALE, np.float32)
    signs[0::2, :, 0] = -LORA_SCALE
    signs[0:6:2, :, 1] = -LORA_SCALE
    out["signs"] = pack(signs.reshape(P, 2))
    out["before"] = pack(np.tile(np.tril(np.ones((E, E), np.float32), -1)[None], (P, 1, 1)))
    return out


def kernel(**inputs):
    import numpy as np
    import concourse.bacc as _bacc
    from concourse.bass_utils import run_bass_kernel_spmd as _run

    nc = _bacc.Bacc("TRN2", target_bir_lowering=False, num_devices=1)
    arrays = layouts(inputs, np)
    io = {n: nc.dram_tensor("in_" + n, a.shape, mybir.dt.from_np(a.dtype), kind="ExternalInput").ap()
          for n, a in arrays.items()}
    for name, shape in (("y_ssm", (B, ET, P, T)), ("attn_o", (H, P, B * T)), ("x2_rows", (B, P, TT, D)),
                        ("x2_t", (B, P, DC, T))):
        io[name] = nc.dram_tensor(name, shape, F32, kind="Internal").ap()
    io["out"] = nc.dram_tensor("out_0_dram", (B, P, TT, D), F32, kind="ExternalOutput").ap()
    ssm_stage(nc, io)
    attn_stage(nc, io)
    block_stage(nc, io)
    mlp_stage(nc, io)
    r = _run(nc, [{"in_" + n: a for n, a in arrays.items()}], core_ids=[0])
    out = r.results[0]["out_0_dram"]
    return np.ascontiguousarray(out.transpose(0, 2, 1, 3)).reshape(B, T, D)
```

```python
import math
from contextlib import ExitStack

import concourse.bass as bass
from concourse import mybir

F32 = mybir.dt.float32
I32 = mybir.dt.int32
ALU = mybir.AluOpType
ACT = mybir.ActivationFunctionType
AX_X = mybir.AxisListType.X

P = 128
B, T, D = 4, 512, 512
DC = D // P
TT = T // P
H = 16
BINS = 64
HID = 32
EPS = 1e-6
NORM_EPS = 1e-5
LEVELS = 7
HALF = P // 2
DI, DS, DR, CTX = 512, 16, 16, 256
ET = DI // P
DFF, E, R = 1408, 8, 16
FC = DFF // P
LORA_SCALE = 2.0
Q_SCALE = float(P) ** -0.5
LN_BINS_INV = 1.0 / math.log(BINS)


def spread(ap, shape):
    return ap.broadcast_to(shape)


def ssm_stage(nc, io):
    NB = 4
    with ExitStack() as ctx:
        def sb(name, shape):
            return ctx.enter_context(nc.sbuf_tensor("m_" + name, shape, F32))

        def ps(name, shape=(P, 512)):
            return ctx.enter_context(nc.psum_tensor("m_" + name, list(shape), F32))

        def sem(name):
            return ctx.enter_context(nc.semaphore("m_" + name))

        ident = sb("ident", [P, P])
        w_in = sb("w_in", [P, 2, DI])
        w_x = sb("w_x", [P, ET, DR + 2 * DS])
        w_dt = sb("w_dt", [DR, DI])
        cols = sb("cols", [P, ET, 4 + 1 + 1 + 1 + DS])
        neg_a = sb("neg_a", [P, ET, DS])
        ctx_t = sb("ctx_t", [P, 2, T])
        tap = sb("tap", [P, 2, T])
        u = sb("u", [P, ET, T])
        x_dbl = sb("x_dbl", [DR + 2 * DS, T])
        soft = sb("soft", [P, 2, T])
        delta = sb("delta", [P, ET, T])
        b_rows = sb("b_rows", [P, DS, T])
        c_rows = sb("c_rows", [P, DS, T])
        du = sb("du", [P, 2, T])
        da = sb("da", [P, NB, T])
        dbu = sb("dbu", [P, NB, T])
        state = sb("state", [P, NB, T])
        cs = sb("cs", [P, NB, T])
        y_out = sb("y_out", [P, 2, T])
        p_x = ps("p_x", (P, 2, T))
        p_d = ps("p_d")
        p_b = ps("p_b", (P, 2, T))
        p_y = ps("p_y", (P, 2, T))

        weights = sem("weights")
        ctx_in = sem("ctx_in")
        neg_a_ready = sem("neg_a_ready")
        projected = sem("projected")
        tapped = sem("tapped")
        convolved = sem("convolved")
        u_ready = sem("u_ready")
        dbl_sum = sem("dbl_sum")
        dbl_ready = sem("dbl_ready")
        dt_sum = sem("dt_sum")
        soft_ready = sem("soft_ready")
        delta_ready = sem("delta_ready")
        row_sum = sem("row_sum")
        b_ready = sem("b_ready")
        c_ready = sem("c_ready")
        du_ready = sem("du_ready")
        da_ready = sem("da_ready")
        dbu_ready = sem("dbu_ready")
        scanned = sem("scanned")
        cs_ready = sem("cs_ready")
        summed = sem("summed")
        y_ready = sem("y_ready")
        y_stored = [sem(f"y_stored{i}") for i in range(2)]
        rounds = sem("rounds")
        passed = sem("passed")

        with nc.Block() as block:

            @block.sync
            def _(sp):
                sp.dma_start(ident[:], io["ident"]).then_inc(weights, 16)
                sp.dma_start(w_in[:], io["ssm_in_w"]).then_inc(weights, 16)
                sp.dma_start(w_x[:], io["ssm_x_w"]).then_inc(weights, 16)
                sp.dma_start(w_dt[:], io["ssm_dt_w"]).then_inc(weights, 16)
                sp.dma_start(cols[:], io["ssm_cols"]).then_inc(weights, 16)
                for stored in y_stored:
                    sp.sem_inc(stored, 1)
                sp.sem_inc(rounds, 1)
                with sp.Fori(0, B) as b:
                    sp.wait_ge(rounds, 4 * b + 1)
                    sp.dma_start(ctx_t[:], io["ctx_t"][b]).then_inc(ctx_in, 16)
                    for et in range(ET):
                        sp.wait_ge(y_ready, b * ET + et + 1)
                        sp.dma_start(io["y_ssm"][b, et], y_out[:, et % 2]).then_inc(y_stored[et % 2], 16)
                for stored in y_stored:
                    sp.wait_ge(stored, 16 * B * ET // 2 + 1)

            @block.tensor
            def _(pe):
                pe.wait_ge(weights, 80)
                with pe.Fori(0, B) as b:
                    pe.wait_ge(rounds, 4 * b + 1)
                    pe.wait_ge(ctx_in, 16 * (b + 1))
                    for et in range(ET):
                        if et >= 2:
                            pe.wait_ge(convolved, b * ET + et - 1)
                        for k in range(2):
                            mm = nc.tensor.matmul(p_x[:, et % 2], w_in[:, k, et * P:(et + 1) * P], ctx_t[:, k],
                                                  start=(k == 0), stop=(k == 1))
                        mm.then_inc(projected, 1)
                    for et in range(ET):
                        pe.wait_ge(u_ready, b * ET + et + 1)
                        mm = nc.tensor.matmul(p_d[0:DR + 2 * DS, :], w_x[:, et], u[:, et],
                                              start=(et == 0), stop=(et == ET - 1))
                    mm.then_inc(dbl_sum, 1)
                    pe.wait_ge(dbl_ready, b + 1)
                    for et in range(ET):
                        if et >= 2:
                            pe.wait_ge(soft_ready, b * ET + et - 1)
                        nc.tensor.matmul(p_x[:, et % 2], w_dt[:, et * P:(et + 1) * P], x_dbl[0:DR, :],
                                                      start=True, stop=True).then_inc(dt_sum, 1)
                    for n in range(2 * DS):
                        if n >= 2:
                            pe.wait_ge(b_ready if n % 2 == 0 else c_ready, b * DS + n // 2)
                        k = DR + (n // 2) + DS * (n % 2)
                        nc.tensor.matmul(
                            p_b[:, n % 2], spread(ident[0:DR + 2 * DS, k:k + 1], [DR + 2 * DS, P]),
                            x_dbl[:, :], start=True, stop=True).then_inc(row_sum, 1)
                    for et in range(ET):
                        if et >= 2:
                            pe.wait_ge(y_ready, b * ET + et - 1)
                        for n in range(DS):
                            i = et * DS + n
                            pe.wait_ge(cs_ready, b * ET * DS + i + 1)
                            nc.tensor.matmul(p_y[:, et % 2], ident[:], cs[:, i % NB],
                                                          start=(n == 0), stop=(n == DS - 1)).then_inc(summed, 1)
                    pe.drain().then_inc(rounds, 1)

            @block.scalar
            def _(act):
                act.wait_ge(weights, 80)
                nc.scalar.activation(neg_a[:], cols[:, :, 7:], ACT.Exp)
                act.drain()
                nc.scalar.activation(neg_a[:], neg_a[:], ACT.Copy, scale=-1.0).then_inc(neg_a_ready, 1)
                act.wait_ge(neg_a_ready, 1)
                with act.Fori(0, B) as b:
                    act.wait_ge(rounds, 4 * b + 1)

                    def silu(et):
                        act.wait_ge(convolved, b * ET + et + 1)
                        nc.scalar.activation(u[:, et], tap[:, et % 2], ACT.Silu, bias=cols[:, et, 4:5]).then_inc(u_ready, 1)

                    for et in range(ET):
                        act.wait_ge(projected, b * ET + et + 1)
                        if et >= 2:
                            act.wait_ge(u_ready, b * ET + et - 1)
                        nc.scalar.activation(tap[:, et % 2], p_x[:, et % 2], ACT.Copy,
                                                          scale=cols[:, et, 3:4]).then_inc(tapped, 1)
                        if et >= 1:
                            silu(et - 1)
                    silu(ET - 1)
                    act.wait_ge(dbl_sum, b + 1)
                    nc.scalar.copy(x_dbl[:], p_d[0:DR + 2 * DS, :]).then_inc(dbl_ready, 1)
                    for et in range(ET):
                        act.wait_ge(dt_sum, b * ET + et + 1)
                        if et >= 1:
                            act.wait_ge(delta_ready, b * ET + et)
                        bias = cols[:, et, 5:6]
                        nc.scalar.activation(soft[:, 0], p_x[:, et % 2], ACT.Abs, bias=bias)
                        nc.scalar.activation(soft[:, 1], p_x[:, et % 2], ACT.Relu, bias=bias)
                        act.drain()
                        nc.scalar.activation(soft[:, 0], soft[:, 0], ACT.Exp, scale=-1.0)
                        act.drain()
                        nc.scalar.activation(soft[:, 0], soft[:, 0], ACT.Ln, bias=1.0).then_inc(soft_ready, 1)
                    for n in range(DS):
                        act.wait_ge(row_sum, b * 2 * DS + 2 * n + 1)
                        nc.scalar.copy(b_rows[:, n], p_b[:, 0]).then_inc(b_ready, 1)
                    for et in range(ET):
                        act.wait_ge(delta_ready, b * ET + et + 1)
                        for n in range(DS):
                            i = et * DS + n
                            if i >= NB:
                                act.wait_ge(scanned, b * ET * DS + i - NB + 1)
                            nc.scalar.activation(da[:, i % NB], delta[:, et], ACT.Exp,
                                                                scale=neg_a[:, et, n:n + 1]).then_inc(da_ready, 1)
                    act.drain().then_inc(rounds, 1)

            @block.vector
            def _(dve):
                dve.wait_ge(weights, 80)
                with dve.Fori(0, B) as b:
                    dve.wait_ge(rounds, 4 * b + 1)
                    for et in range(ET):
                        dve.wait_ge(tapped, b * ET + et + 1)
                        for s in range(1, 4):
                            last = nc.vector.scalar_tensor_tensor(
                                tap[:, et % 2, s:T], p_x[:, et % 2, 0:T - s], cols[:, et, 3 - s:4 - s],
                                tap[:, et % 2, s:T], ALU.mult, ALU.add)
                            if s < 3:
                                dve.drain()
                        last.then_inc(convolved, 1)
                    for et in range(ET):
                        dve.wait_ge(soft_ready, b * ET + et + 1)
                        nc.vector.tensor_tensor(delta[:, et], soft[:, 0], soft[:, 1], ALU.add).then_inc(delta_ready, 1)
                    for n in range(DS):
                        dve.wait_ge(row_sum, b * 2 * DS + 2 * n + 2)
                        nc.vector.tensor_copy(c_rows[:, n], p_b[:, 1]).then_inc(c_ready, 1)

                    def times_c(i):
                        dve.wait_ge(scanned, b * ET * DS + i + 1)
                        if i >= NB:
                            dve.wait_ge(summed, b * ET * DS + i - NB + 1)
                        nc.vector.tensor_tensor(cs[:, i % NB], state[:, i % NB],
                                                               c_rows[:, i % DS], ALU.mult).then_inc(cs_ready, 1)

                    for et in range(ET):
                        for n in range(DS):
                            i = et * DS + n
                            dve.wait_ge(da_ready, b * ET * DS + i + 1)
                            dve.wait_ge(dbu_ready, b * ET * DS + i + 1)
                            if i >= NB:
                                dve.wait_ge(cs_ready, b * ET * DS + i - NB + 1)
                            nc.vector.tensor_tensor_scan(state[:, i % NB], da[:, i % NB],
                                                                       dbu[:, i % NB], 0.0, ALU.mult, ALU.add).then_inc(scanned, 1)
                            if i >= 1:
                                times_c(i - 1)
                        if et == ET - 1:
                            times_c(ET * DS - 1)
                        for done in ([et - 1] if et >= 1 else []) + ([et] if et == ET - 1 else []):
                            dve.wait_ge(summed, b * ET * DS + (done + 1) * DS)
                            dve.wait_ge(y_stored[done % 2], 16 * (b * (ET // 2) + done // 2) + 1)
                            nc.vector.scalar_tensor_tensor(
                                y_out[:, done % 2], u[:, done], cols[:, done, 6:7], p_y[:, done % 2],
                                ALU.mult, ALU.add).then_inc(y_ready, 1)
                    dve.drain().then_inc(rounds, 1)

            @block.gpsimd
            def _(pool):
                with pool.Fori(0, B) as b:
                    pool.wait_ge(rounds, 4 * b + 1)
                    for et in range(ET):
                        pool.wait_ge(delta_ready, b * ET + et + 1)
                        pool.wait_ge(u_ready, b * ET + et + 1)
                        if et >= 2:
                            pool.wait_ge(dbu_ready, b * ET * DS + (et - 1) * DS)
                        nc.gpsimd.tensor_tensor(du[:, et % 2], delta[:, et], u[:, et], ALU.mult).then_inc(du_ready, 1)
                        pool.wait_ge(du_ready, b * ET + et + 1)
                        for n in range(DS):
                            i = et * DS + n
                            pool.wait_ge(b_ready, b * DS + n + 1)
                            if i >= NB:
                                pool.wait_ge(scanned, b * ET * DS + i - NB + 1)
                            nc.gpsimd.tensor_tensor(dbu[:, i % NB], du[:, et % 2],
                                                                    b_rows[:, n], ALU.mult).then_inc(dbu_ready, 1)
                    pool.drain().then_inc(rounds, 1)


P_NORM, P_BETA_SLOW, P_BETA_FAST, P_LAMBDA, P_AMP_SLOW, P_AMP_FAST = range(6)
SLOW, FAST = 0, 1
NEG_K, QUERY = 0, 1
PAIRS = 2 * TT
C_G2B, C_BIAS1, C_DECAY = 12, 13, 14


def left(ap, h):
    return ap.rearrange("p x (s two h) -> p x s two h", two=2, h=h)[:, :, :, 0, :]


def right(ap, h):
    return ap.rearrange("p x (s two h) -> p x s two h", two=2, h=h)[:, :, :, 1, :]


def compact(ap, h):
    return ap.rearrange("p x (s h) -> p x s h", h=h)


def halves(h):
    return [(slice(2 * h * n, 2 * h * n + h), slice(2 * h * n + h, 2 * h * (n + 1)), h * n)
            for n in range(P // (2 * h))]


def attn_stage(nc, io):
    with ExitStack() as ctx:
        def sb(name, shape, dt=F32):
            return ctx.enter_context(nc.sbuf_tensor("a_" + name, shape, dt))

        def sem(name):
            return ctx.enter_context(nc.semaphore("a_" + name))

        pb = ctx.enter_context(nc.psum_tensor("a_pb", [P, 8, 512], F32))
        ident = sb("ident", [P, P])
        ones = sb("ones", [P, HID])
        mean_w = sb("mean_w", [P, HID])
        eps_col = sb("eps_col", [P, 1])
        mask_u = sb("mask_u", [P, LEVELS, HALF], I32)
        mask_l = sb("mask_l", [P, LEVELS, HALF], I32)
        sel = sb("sel", [P, P])
        small = sb("small", [P, 49])
        x_t = sb("x_t", [P, DC, B * T])
        g_t = sb("g_t", [P, B * T])
        head_cols = sb("head_cols", [P, H + 1, 15])
        w_out = sb("w_out", [P, 5, P])
        b_out = sb("b_out", [P, 5])
        w2_diag = sb("w2_diag", [P, P])
        ent_w = sb("ent_w", [P, T])
        work = sb("work", [P, 12, T])
        proxy = sb("proxy", [P, P])

        with ExitStack() as once:
            def sb1(name, shape):
                return once.enter_context(nc.sbuf_tensor("a1_" + name, shape, F32))

            def sem1(name):
                return once.enter_context(nc.semaphore("a1_" + name))

            g1 = sb1("g1", [P, DC, P])
            unc = sb1("unc", [P, DC, BINS])
            w1_embed = sb1("w1_embed", [4, P])
            embed_t = sb1("embed_t", [4, H])
            cols = sb1("cols", [P, 12, B * TT])
            loaded = sem1("loaded")
            zeroed = sem1("zeroed")
            placed = sem1("placed")
            logits = sem1("logits")
            shifted = sem1("shifted")
            exped = sem1("exped")
            summed = sem1("summed")
            logged = sem1("logged")
            ent_rows = sem1("ent_rows")
            ent_sum = sem1("ent_sum")
            g1_sum = sem1("g1_sum")
            bias_sum = sem1("bias_sum")
            soft = sem1("soft")
            LOADS = 12
            with nc.Block() as block:

                @block.sync
                def _(sp):
                    for dst, src in ((ident, "ident"), (mask_u, "mask_u"), (mask_l, "mask_l"), (sel, "sel"),
                                     (small, "small"), (proxy, "proxy"), (x_t, "x_t"), (g1, "g1"), (unc, "unc"),
                                     (w1_embed, "w1_embed"), (embed_t, "embed_t")):
                        sp.dma_start(dst[:], io[src]).then_inc(loaded, 16)
                    sp.dma_start(head_cols[:, 0:H, 0:13], io["head_cols"]).then_inc(loaded, 16)
                    sp.wait_ge(zeroed, 1)
                    for q in range(4):
                        sp.dma_start(w2_diag[32 * q:32 * q + 32, 32 * q:32 * q + 32], io["mlp_w2"]).then_inc(placed, 16)
                    sp.wait_ge(placed, 64)
                    sp.wait_ge(loaded, 16 * LOADS)

                @block.gpsimd
                def _(pool):
                    nc.gpsimd.memset(w2_diag[:], 0.0).then_inc(zeroed, 1)
                    nc.gpsimd.memset(ones[:], 1.0)
                    nc.gpsimd.memset(head_cols[:, H], 0.0)
                    nc.gpsimd.memset(mean_w[:], 1.0 / P)
                    nc.gpsimd.memset(eps_col[:], NORM_EPS)

                @block.tensor
                def _(pe):
                    pe.wait_ge(loaded, 16 * LOADS)
                    lg = pb[:, 0:2].rearrange("p k (i n) -> p (k i) n", n=BINS)
                    for i in range(B * TT):
                        for k in range(DC):
                            mm = nc.tensor.matmul(lg[:, i], x_t[:, k, i * P:(i + 1) * P], unc[:, k],
                                                  start=(k == 0), stop=(k == DC - 1))
                    mm.then_inc(logits, 1)
                    for b in range(B):
                        for k in range(DC):
                            mm = nc.tensor.matmul(pb[:, 3 + b], g1[:, k], x_t[:, k, b * T:(b + 1) * T],
                                                  start=(k == 0), stop=(k == DC - 1))
                    mm.then_inc(g1_sum, 1)
                    nc.tensor.matmul(pb[:, 7, 0:H], w1_embed[:], embed_t[:], start=True, stop=True).then_inc(bias_sum, 1)
                    pe.wait_ge(ent_rows, 1)
                    for tt in range(TT):
                        mm = nc.tensor.matmul(pb[:, 2, tt * P:(tt + 1) * P], work[:, 6, tt * P:(tt + 1) * P],
                                              ident[:], start=True, stop=True)
                    mm.then_inc(ent_sum, 1)

                @block.scalar
                def _(act):
                    act.wait_ge(loaded, 16 * LOADS)
                    nc.scalar.activation(cols[:, 8], small[:, 17:33], ACT.Exp)
                    nc.scalar.activation(cols[:, 9], small[:, 33:49], ACT.Relu)
                    nc.scalar.activation(cols[:, 10], small[:, 33:49], ACT.Abs)
                    act.drain()
                    nc.scalar.activation(cols[:, 10], cols[:, 10], ACT.Exp, scale=-1.0)
                    act.drain()
                    nc.scalar.activation(cols[:, 10], cols[:, 10], ACT.Ln, bias=1.0).then_inc(soft, 1)
                    act.wait_ge(bias_sum, 1)
                    nc.scalar.activation(head_cols[:, 0:H, C_BIAS1], pb[:, 7, 0:H], ACT.Identity, bias=small[:, 4:5])
                    act.wait_ge(g1_sum, 1)
                    for b in range(B):
                        nc.scalar.copy(g_t[:, b * T:(b + 1) * T], pb[:, 3 + b])
                    act.wait_ge(shifted, 1)
                    nc.scalar.activation(work[:, 2:4], work[:, 0:2], ACT.Exp).then_inc(exped, 1)
                    act.wait_ge(summed, 1)
                    nc.scalar.activation(cols[:, 2], cols[:, 1], ACT.Ln).then_inc(logged, 1)

                @block.vector
                def _(dve):
                    dve.wait_ge(loaded, 16 * LOADS)
                    for src, dst in ((small[:, 6:11], cols[:, 5, 0:5]), (small[:, 11:16], b_out[:])):
                        for o, base, delta, op in ((0, 0, 1, ALU.subtract), (1, 0, 1, ALU.add),
                                                   (3, 3, 4, ALU.subtract), (4, 3, 4, ALU.add)):
                            nc.vector.tensor_tensor(dst[:, o:o + 1], src[:, base:base + 1], src[:, delta:delta + 1], op)
                        nc.vector.tensor_copy(dst[:, 2:3], src[:, 2:3])
                    dve.drain()
                    nc.vector.tensor_copy(w_out[:], spread(cols[:, 5, 0:5].unsqueeze(2), [P, 5, P]))
                    dve.wait_ge(soft, 1)
                    nc.vector.tensor_tensor(cols[:, 9], cols[:, 9], cols[:, 10], ALU.add)
                    dve.drain()
                    nc.vector.scalar_tensor_tensor(head_cols[:, 0:H, C_DECAY], cols[:, 9], -1.0, cols[:, 8],
                                                   ALU.mult, ALU.mult)
                    lg = pb[:, 0:2].rearrange("p k (i n) -> p (k i) n", n=BINS)
                    z = work[:, 0:2].rearrange("p k (i n) -> p (k i) n", n=BINS)
                    ez = work[:, 2:4].rearrange("p k (i n) -> p (k i) n", n=BINS)
                    zez = work[:, 4:6].rearrange("p k (i n) -> p (k i) n", n=BINS)
                    dve.wait_ge(logits, 1)
                    nc.vector.tensor_reduce(cols[:, 0], lg, AX_X, ALU.max)
                    dve.drain()
                    nc.vector.tensor_tensor(
                        z, lg, spread(cols[:, 0].unsqueeze(2), [P, B * TT, BINS]), ALU.subtract).then_inc(shifted, 1)
                    dve.wait_ge(exped, 1)
                    nc.vector.tensor_reduce(cols[:, 1], ez, AX_X, ALU.add).then_inc(summed, 1)
                    nc.vector.tensor_tensor(zez, ez, z, ALU.mult)
                    dve.drain()
                    nc.vector.tensor_reduce(cols[:, 3], zez, AX_X, ALU.add)
                    nc.vector.reciprocal(cols[:, 4], cols[:, 1])
                    dve.drain()
                    nc.vector.tensor_tensor(cols[:, 3], cols[:, 3], cols[:, 4], ALU.mult)
                    dve.drain()
                    dve.wait_ge(logged, 1)
                    nc.vector.tensor_tensor(cols[:, 3], cols[:, 2], cols[:, 3], ALU.subtract)
                    dve.drain()
                    ent = cols[:, 3].rearrange("p (b t) -> p t b", b=B).unsqueeze(3)
                    rows = work[:, 6].rearrange("p (t b m) -> p t b m", t=TT, b=B)
                    for tt in range(TT):
                        last = nc.vector.tensor_scalar(rows[:, tt], spread(ent[:, tt], [P, B, HID]),
                                                       LN_BINS_INV, None, ALU.mult)
                    last.then_inc(ent_rows, 1)
                    dve.wait_ge(ent_sum, 1)
                    nc.vector.tensor_scalar(ent_w[:], pb[:, 2], small[:, 0:1], None, ALU.mult)

        w_qkv = sb("w_qkv", [P, 3, DC, P])
        g2 = sb("g2", [P, P])
        cur = sb("cur", [P, 15])
        taps = sb("taps", [P, 12])
        nq = sb("nq", [P, B, 2, 2, T])
        ks = sb("ks", [P, B, 2, T])
        bv = sb("bv", [P, B, 2, T])
        e1 = sb("e1", [P, 2, 2, T])
        tot = sb("tot", [P, 2 * T])
        tot_chunk = sb("tot_chunk", [P, B, PAIRS])
        x_inv = sb("x_inv", [P, PAIRS, P])
        y_inv = sb("y_inv", [P, 2, PAIRS, P])
        w_sb = sb("w_sb", [P, PAIRS, P])
        state = sb("state", [P, 2, P])
        r_sb = sb("r_sb", [P, 2, P])
        u_sb = sb("u_sb", [P, 2, P])
        kt_sb = sb("kt_sb", [P, 2, P])
        o_t = sb("o_t", [P, B, T])
        gates = sb("gates", [P, 3, T])
        hf = sb("hf", [P, T])
        rnorm = sb("rnorm", [P, T])
        apt = work[:].rearrange("p (r k) t -> p r (k t)", r=3).rearrange("p r (i w t) -> p r i w t", i=PAIRS, w=2)
        ERR, V_VH, V2, VH2, K2, CONV = 0, 2, 4, 6, 8, 10
        EN, L1P, RV, VN, VHN, RVV, KN, FEAT, HID1 = 0, 1, 5, 4, 6, 7, 8, 9, 2
        G, BANK_W, BANK_X, BANK_Y, BANK_RU, BANK_S, BANK_N = 0, 2, 3, 4, 5, 6, 7
        def piece_bank(b, piece):
            return BANK_N if b else (BANK_N, 2, 3, 4, 5, 6)[piece]

        GATE_BANKS = (2, 4, 5, 6)
        ROW_BANKS = (7, 2, 4, 5)
        ORDER = [(b, i) for b in range(B) for i in (0, 1)] + [(b, 2) for b in range(B)]
        PROJ = (0, 1, 3, 0, 1, 3, 0, 1, 3, 0, 7, 0)
        products = pb[:, G:G + 2]

        def tot_of(b, level):
            if level == 0:
                return e1[:, b % 2].rearrange("p r t -> p (r t)")
            if level == LEVELS:
                return tot_chunk[:, b]
            at = sum(2 * (T >> k) for k in range(1, level))
            return tot[:, at:at + 2 * (T >> level)]

        TILES = 3 * B
        AHEAD = 10
        PS, IS, IW = LEVELS + 1, LEVELS, LEVELS - 1
        w_in = sem("w_in")
        g2_in = sem("g2_in")
        cur_ready = sem("cur_ready")
        taps_ready = sem("taps_ready")
        projected = sem("projected")
        tapped = sem("tapped")
        convolved = sem("convolved")
        silued = sem("silued")
        vhat = sem("vhat")
        vh_squared = sem("vh_squared")
        err_ready = sem("err_ready")
        squared = sem("squared")
        stats = sem("stats")
        rooted = sem("rooted")
        l1p_ready = sem("l1p_ready")
        feat_ready = sem("feat_ready")
        rnorm_ready = sem("rnorm_ready")
        hid1_ready = sem("hid1_ready")
        hid2_sum = sem("hid2_sum")
        hf_ready = sem("hf_ready")
        piece_sum = sem("piece_sum")
        piece_used = sem("piece_used")
        k_copied = sem("k_copied")
        nq_ready = sem("nq_ready")
        bv_ready = sem("bv_ready")
        e1_ready = sem("e1_ready")
        apt_zeroed = sem("apt_zeroed")
        product = sem("product")
        kept = sem("kept")
        nq_decayed = sem("nq_decayed")
        ks_decayed = sem("ks_decayed")
        xy_ready = sem("xy_ready")
        w_sum = sem("w_sum")
        w_ready = sem("w_ready")
        xy_sum = sem("xy_sum")
        xy_grown = sem("xy_grown")
        kt_sum = sem("kt_sum")
        kt_ready = sem("kt_ready")
        r_sum = sem("r_sum")
        r_ready = sem("r_ready")
        u_sum = sem("u_sum")
        u_ready = sem("u_ready")
        o_sum = sem("o_sum")
        o_kept = sem("o_kept")
        s_sum = sem("s_sum")
        state_ready = sem("state_ready")
        o_squared = sem("o_squared")
        o_mean = sem("o_mean")
        o_root = sem("o_root")
        o_rroot = sem("o_rroot")
        gate_sum = sem("gate_sum")
        gate_ready = sem("gate_ready")
        rroot_rows = sem("rroot_rows")
        o_ready = sem("o_ready")
        o_stored = sem("o_stored")
        cleared = sem("cleared")
        rounds = sem("rounds")
        passed = sem("passed")

        def slots():
            def batch(b):
                return b if 0 <= b < B else None
            for s in range(-1, B + 1):
                for step in range(PS):
                    bi, level = (batch(s), step - 2) if step >= 2 else (batch(s - 1) if step == 0 else None, LEVELS - 1)
                    yield batch(s + 1), batch(s), bi, level, batch(s - 1), step

        with nc.Block() as block:

            @block.sync
            def _(sp):
                sp.sem_inc(o_stored, 1)
                sp.dma_start(w_qkv[:], io["w_qkv"][0]).then_inc(w_in, 16)
                sp.sem_inc(rounds, 1)
                with sp.Fori(0, H) as h:
                    sp.wait_ge(rounds, 5 * h + 5)
                    sp.dma_start(g2[:], io["g2"][h]).then_inc(g2_in, 16)
                    sp.wait_ge(projected, h * TILES + TILES)
                    sp.dma_start(w_qkv[:], io["w_qkv"][h + 1]).then_inc(w_in, 16)
                    sp.wait_ge(o_ready, h * B + B)
                    sp.dma_start(io["attn_o"][h], o_t[:].rearrange("p b t -> p (b t)")).then_inc(o_stored, 16)
                    sp.drain().then_inc(rounds, 1)
                sp.wait_ge(o_stored, 16 * ((H - 1) + 1) + 1)
                sp.wait_ge(w_in, 16 * (H + 1))

            @block.tensor
            def _(pe):
                def project(g, t):
                    b, i = ORDER[t]
                    if t == 0:
                        pe.wait_ge(w_in, 16 * (g + 1))
                    if 3 <= t < AHEAD:
                        pe.wait_ge(convolved, g * TILES + t - 2)
                    for k in range(DC):
                        mm = nc.tensor.matmul(pb[:, PROJ[t]], w_qkv[:, i, k], x_t[:, k, b * T:(b + 1) * T],
                                              start=(k == 0), stop=(k == DC - 1))
                    mm.then_inc(projected, 1)

                for t in range(AHEAD):
                    project(0, t)
                pe.drain().then_inc(rounds, 1)
                with pe.Fori(0, H) as h:
                    pe.wait_ge(rounds, 5 * h + 5)
                    pe.wait_ge(convolved, h * TILES + AHEAD)
                    for b in range(B + 1):
                        if b < B:
                            pe.wait_ge(silued, h * TILES + 2 * b + 1)
                            if b >= 2:
                                pe.wait_ge(squared, h * B + b - 1)
                            nc.tensor.matmul(pb[:, b % 2], proxy[:], ks[:, b, 0], start=True, stop=True).then_inc(vhat, 1)
                        if b >= 1:
                            c = b - 1
                            pe.wait_ge(squared, h * B + c + 1)
                            for n, src in enumerate((ERR, V2, VH2, K2, V_VH)):
                                mm = nc.tensor.matmul(pb[32 * c:32 * c + 32, 2 + n], ones[:], work[:, src + c % 2],
                                                      start=True, stop=True)
                            mm.then_inc(stats, 1)
                    project(h, 10)
                    project(h, 11)
                    pe.wait_ge(hid1_ready, h + 1)
                    nc.tensor.matmul(pb[:, 1], w2_diag[:], work[:, HID1], start=True, stop=True).then_inc(hid2_sum, 1)
                    pe.wait_ge(hf_ready, h + 1)
                    pe.wait_ge(rnorm_ready, h + 1)
                    pe.wait_ge(convolved, h * TILES + TILES)

                    for bn, bp, bi, lv, bs, step in slots():
                        if bn is not None and step < 6:
                            if bn:
                                pe.wait_ge(piece_used, h * 6 * B + 6 * bn + step)
                            if bs is not None and step % 2:
                                pe.wait_ge(kt_ready, h * TT * B + TT * bs + step // 2 + 1)
                            elif bs is not None and TT * bs + step // 2:
                                pe.wait_ge(o_kept, h * TT * B + TT * bs + step // 2)
                            q = slice(32 * bn, 32 * bn + 32)
                            w, rows = (sel[q, :], rnorm[q, :]) if step == P_NORM else (w_out[q, step - 1], hf[q, :])
                            nc.tensor.matmul(pb[:, piece_bank(bn, step)], w, rows, start=True, stop=True).then_inc(piece_sum, 1)
                        if bp is not None:
                            if step == 0:
                                pe.wait_ge(nq_ready, h * B + bp + 1)
                                pe.wait_ge(k_copied, h * B + bp + 1)
                            else:
                                pe.wait_ge(nq_decayed, h * PS * B + PS * bp + step)
                            if step >= 2:
                                pe.wait_ge(ks_decayed, h * LEVELS * B + LEVELS * bp + step - 1)
                            if bp or step:
                                pe.wait_ge(kept, h * PS * B + PS * bp + step)
                            for i in range(PAIRS):
                                rate, c = divmod(i, TT)
                                chunk = slice(c * P, (c + 1) * P)
                                out = products[:, rate, c * P:(c + 1) * P]
                                rhs = nq[:, bp, rate, QUERY, chunk]
                                if step:
                                    rhs = right(nq[:, bp, rate, :, chunk], 1 << (step - 1))
                                    out = out.rearrange("p (w s h) -> p w s h", w=2, h=1 << (step - 1))
                                mm = nc.tensor.matmul(out, ks[:, bp, rate, chunk], rhs, start=True, stop=True)
                            mm.then_inc(product, 1)
                        if bi is not None:
                            hs = 1 << lv
                            pe.wait_ge(kept, h * PS * B + PS * bi + lv + 2)
                            if lv or bi:
                                pe.wait_ge(xy_grown, h * IS * B + IS * bi + lv)
                            pe.sem_inc(passed, 1)
                            for i in range(PAIRS):
                                if hs >= 32:
                                    for lo, hi, col in halves(hs):
                                        mm = nc.tensor.matmul(pb[hi, BANK_W, i * HALF + col:i * HALF + col + hs],
                                                              apt[lo, bi % 3, i, NEG_K, hi], x_inv[lo, i, lo],
                                                              start=True, stop=True)
                                    continue
                                x = x_inv[:, i:i + 1] if lv else ident[:].unsqueeze(1)
                                mm = nc.tensor.matmul(
                                    compact(pb[:, BANK_W:BANK_W + 1, i * HALF:(i + 1) * HALF], hs)[:, 0],
                                    apt[:, bi % 3, i, NEG_K], left(x, hs)[:, 0], start=True, stop=True)
                            mm.then_inc(w_sum, 1)
                        if bs is not None:
                            c = step // 2
                            n = TT * bs + c
                            chunk = slice(c * P, (c + 1) * P)
                            if step % 2 == 0:
                                if c == 0:
                                    pe.wait_ge(nq_decayed, h * PS * B + PS * (bs + 1))
                                    pe.wait_ge(ks_decayed, h * LEVELS * B + LEVELS * (bs + 1))
                                if n:
                                    pe.wait_ge(u_ready, h * TT * B + n)
                                    pe.wait_ge(o_kept, h * TT * B + n)
                                pe.wait_ge(piece_used, h * 6 * B + (6 * B if bn is None else 6 * bn + min(step + 1, 6)))
                                for rate in (SLOW, FAST):
                                    mm = nc.tensor.transpose(pb[:, BANK_N, rate * P:(rate + 1) * P],
                                                             ks[:, bs, rate, chunk], ident[:])
                                mm.then_inc(kt_sum, 1)
                                if c:
                                    pe.wait_ge(state_ready, h * ((TT - 1) * B) + (TT - 1) * bs + c)
                                else:
                                    pe.wait_ge(bv_ready, h * B + bs + 1)
                                for rate in (SLOW, FAST):
                                    out = pb[:, BANK_RU, rate * P:(rate + 1) * P]
                                    mm = nc.tensor.matmul(out, bv[:, bs, rate, chunk], ident[:], start=True, stop=(c == 0))
                                    if c:
                                        mm = nc.tensor.matmul(out, nq[:, bs, rate, NEG_K, chunk], state[:, rate],
                                                              start=False, stop=True)
                                mm.then_inc(r_sum, 1)
                            else:
                                pe.wait_ge(u_ready, h * TT * B + n + 1)
                                pe.wait_ge(kt_ready, h * TT * B + n + 1)
                                pe.wait_ge(piece_used, h * 6 * B + (6 * B if bn is None else 6 * bn + min(step + 1, 6)))
                                out = pb[:, BANK_N, 0:P]
                                for rate in (SLOW, FAST):
                                    mm = nc.tensor.matmul(out, u_sb[:, rate], apt[:, bs % 3, rate * TT + c, QUERY],
                                                          start=(rate == SLOW), stop=(rate == FAST and c == 0))
                                if c:
                                    for rate in (SLOW, FAST):
                                        mm = nc.tensor.matmul(out, state[:, rate], nq[:, bs, rate, QUERY, chunk],
                                                              start=False, stop=(rate == FAST))
                                mm.then_inc(o_sum, 1)
                                for rate in (SLOW, FAST):
                                    mm = nc.tensor.matmul(pb[:, BANK_S, rate * P:(rate + 1) * P], kt_sb[:, rate],
                                                          u_sb[:, rate], start=True, stop=True)
                                mm.then_inc(s_sum, 1)
                        if bp is None and bs is not None:
                            project(h + 1, step)
                        if bi is not None and lv:
                            hs = 1 << lv
                            pe.wait_ge(w_ready, h * IW * B + IW * bi + lv)
                            pe.sem_inc(passed, 1)
                            if lv < IS - 1:
                                for i in range(PAIRS):
                                    if hs >= 32:
                                        for lo, hi, col in halves(hs):
                                            nc.tensor.matmul(pb[hi, BANK_X, i * HALF + col:i * HALF + col + hs],
                                                             y_inv[hi, bi % 2, i, hi], w_sb[hi, i, lo],
                                                             start=True, stop=True)
                                        continue
                                    nc.tensor.matmul(
                                        compact(pb[:, BANK_X:BANK_X + 1, i * HALF:(i + 1) * HALF], hs)[:, 0],
                                        y_inv[:, bi % 2, i], left(w_sb[:, i:i + 1], hs)[:, 0], start=True, stop=True)
                            for i in range(PAIRS):
                                if hs >= 32:
                                    for lo, hi, col in halves(hs):
                                        mm = nc.tensor.matmul(pb[lo, BANK_Y, i * HALF + col:i * HALF + col + hs],
                                                              w_sb[hi, i, lo], y_inv[hi, bi % 2, i, hi],
                                                              start=True, stop=True)
                                    continue
                                mm = nc.tensor.matmul(
                                    compact(pb[:, BANK_Y:BANK_Y + 1, i * HALF:(i + 1) * HALF], hs)[:, 0],
                                    w_sb[:, i], right(y_inv[:, bi % 2, i:i + 1], hs)[:, 0], start=True, stop=True)
                            mm.then_inc(xy_sum, 1)
                        if bs is not None and step % 2 == 0:
                            c = step // 2
                            n = TT * bs + c
                            pe.wait_ge(r_ready, h * TT * B + n + 1)
                            if c == 0:
                                pe.wait_ge(xy_grown, h * IS * B + IS * (bs + 1))
                            for rate in (SLOW, FAST):
                                mm = nc.tensor.matmul(pb[:, BANK_RU, 256 + rate * P:256 + (rate + 1) * P],
                                                      y_inv[:, bs % 2, rate * TT + c], r_sb[:, rate],
                                                      start=True, stop=True)
                            mm.then_inc(u_sum, 1)

                    pe.wait_ge(g2_in, 16 * (h + 1))
                    for b in range(B):
                        nc.tensor.matmul(pb[:, GATE_BANKS[b]], g2[:], g_t[:, b * T:(b + 1) * T],
                                         start=True, stop=True).then_inc(gate_sum, 1)
                    for b in range(B):
                        pe.wait_ge(o_squared, h * B + b + 1)
                        mm = nc.tensor.matmul(pb[32 * b:32 * b + 32, BANK_N], mean_w[:], work[:, b], start=True, stop=True)
                    mm.then_inc(o_mean, 1)
                    project(h + 1, 8)
                    project(h + 1, 9)
                    pe.wait_ge(o_rroot, h + 1)
                    for b in range(B):
                        if b:
                            pe.wait_ge(gate_ready, h * B + b)
                        q = slice(32 * b, 32 * b + 32)
                        nc.tensor.matmul(pb[:, ROW_BANKS[b]], sel[q, :], work[q, 5],
                                         start=True, stop=True).then_inc(rroot_rows, 1)
                    pe.drain().then_inc(rounds, 1)

            @block.scalar
            def _(act):
                def tap(g, t):
                    i = ORDER[t][1]
                    act.wait_ge(projected, g * TILES + t + 1)
                    if t >= 2:
                        act.wait_ge(silued, g * TILES + t - 1)
                    nc.scalar.activation(work[:, CONV + t % 2], pb[:, PROJ[t]], ACT.Copy,
                                         scale=taps[:, 4 * i + 3:4 * i + 4]).then_inc(tapped, 1)

                def silu(g, t):
                    b, i = ORDER[t]
                    act.wait_ge(convolved, g * TILES + t + 1)
                    nc.scalar.activation((ks[:, b, 0], bv[:, b, 0], nq[:, b, 0, QUERY])[i], work[:, CONV + t % 2],
                                         ACT.Silu).then_inc(silued, 1)

                act.wait_ge(taps_ready, 1)
                for t in range(AHEAD):
                    tap(0, t)
                    if t >= 1:
                        silu(0, t - 1)
                silu(0, AHEAD - 1)
                act.drain().then_inc(rounds, 1)
                with act.Fori(0, H) as h:
                    act.wait_ge(rounds, 5 * h + 5)
                    act.wait_ge(cur_ready, h + 1)
                    for b in range(B):
                        act.wait_ge(vhat, h * B + b + 1)
                        if b >= 2:
                            act.wait_ge(stats, h * B + b - 1)
                        nc.scalar.activation(work[:, VH2 + b % 2], pb[:, b % 2], ACT.Square).then_inc(vh_squared, 1)
                        act.wait_ge(silued, h * TILES + 2 * b + 2)
                        nc.scalar.activation(work[:, V2 + b % 2], bv[:, b, 0], ACT.Square)
                        nc.scalar.activation(work[:, K2 + b % 2], ks[:, b, 0], ACT.Square)
                        act.wait_ge(err_ready, h * B + b + 1)
                        nc.scalar.activation(work[:, ERR + b % 2], work[:, ERR + b % 2], ACT.Square).then_inc(squared, 1)
                    act.wait_ge(stats, h * B + B)
                    for n, dst in enumerate((EN, VN, VHN, KN)):
                        last = nc.scalar.activation(work[:, dst], pb[:, 2 + n], ACT.Sqrt)
                    last.then_inc(rooted, 1)
                    act.drain()
                    nc.scalar.activation(work[:, L1P], work[:, EN], ACT.Ln, bias=1.0).then_inc(l1p_ready, 1)
                    tap(h, 10)
                    tap(h, 11)
                    act.wait_ge(feat_ready, h + 1)
                    nc.scalar.activation(work[:, HID1], work[:, FEAT], ACT.Silu,
                                                          bias=cur[:, C_BIAS1:C_BIAS1 + 1]).then_inc(hid1_ready, 1)
                    act.wait_ge(hid2_sum, h + 1)
                    nc.scalar.activation(hf[:], pb[:, 1], ACT.Silu, bias=small[:, 5:6]).then_inc(hf_ready, 1)
                    silu(h, 10)
                    silu(h, 11)
                    act.wait_ge(taps_ready, h + 2)
                    act.sem_inc(passed, 1)

                    for bn, bp, bi, lv, bs, step in slots():
                        if bn is not None and 1 <= step <= 5:
                            act.wait_ge(piece_sum, h * 6 * B + 6 * bn + step + 1)
                            if bn == 0 and step == 1:
                                act.wait_ge(piece_used, h * 6 * B + 1)
                            if step == P_BETA_SLOW and bn:
                                act.wait_ge(nq_ready, h * B + bn)
                                act.wait_ge(bv_ready, h * B + bn)
                            if step == P_AMP_SLOW and bn >= 2:
                                act.wait_ge(nq_decayed, h * PS * B + PS * (bn - 1))
                                act.wait_ge(ks_decayed, h * LEVELS * B + LEVELS * (bn - 1))
                            dst = gates[:, step - 1] if step <= P_LAMBDA else e1[:, bn % 2, step - P_AMP_SLOW]
                            nc.scalar.activation(dst, pb[:, piece_bank(bn, step)], ACT.Sigmoid,
                                                                  bias=b_out[:, step - 1:step]).then_inc(piece_used, 1)
                        if bn is not None and step == 6:
                            act.drain()
                            nc.scalar.activation(e1[:, bn % 2], e1[:, bn % 2], ACT.Exp,
                                                                scale=cur[:, C_DECAY:C_DECAY + 1]).then_inc(e1_ready, 1)
                        if bi is not None and lv:
                            act.wait_ge(w_sum, h * IS * B + IS * bi + lv + 1)
                            if bi or lv > 1:
                                act.wait_ge(xy_sum, h * IW * B + IW * bi + lv - 1)
                            else:
                                act.wait_ge(cleared, 1)
                            nc.scalar.copy(left(w_sb[:], 1 << lv),
                                                         compact(pb[:, BANK_W].rearrange("p (i t) -> p i t", i=PAIRS),
                                                                 1 << lv)).then_inc(w_ready, 1)
                        if bs is not None:
                            c = step // 2
                            n = TT * bs + c
                            if step % 2 == 0:
                                act.wait_ge(kt_sum, h * TT * B + n + 1)
                                if n:
                                    act.wait_ge(s_sum, h * TT * B + n)
                                nc.scalar.copy(kt_sb[:], pb[:, BANK_N, 0:256].rearrange(
                                    "p (r t) -> p r t", r=2)).then_inc(kt_ready, 1)
                                act.wait_ge(r_sum, h * TT * B + n + 1)
                                nc.scalar.copy(r_sb[:], pb[:, BANK_RU, 0:256].rearrange(
                                    "p (r t) -> p r t", r=2)).then_inc(r_ready, 1)
                                act.wait_ge(u_sum, h * TT * B + n + 1)
                                nc.scalar.copy(u_sb[:], pb[:, BANK_RU, 256:512].rearrange(
                                    "p (r t) -> p r t", r=2)).then_inc(u_ready, 1)
                            else:
                                if n == 0:
                                    act.wait_ge(o_stored, 16 * h + 1)
                                act.wait_ge(o_sum, h * TT * B + n + 1)
                                nc.scalar.copy(o_t[:, bs, c * P:(c + 1) * P],
                                                            pb[:, BANK_N, 0:P]).then_inc(o_kept, 1)
                        if bp is None and bs is not None:
                            tap(h + 1, step)
                            if step:
                                silu(h + 1, step - 1)
                    act.wait_ge(s_sum, h * TT * B + TT * B)
                    act.sem_inc(passed, 1)
                    act.drain()
                    for b in range(B):
                        nc.scalar.activation(work[:, b], o_t[:, b], ACT.Square).then_inc(o_squared, 1)
                    silu(h + 1, 7)
                    act.wait_ge(o_mean, h + 1)
                    nc.scalar.activation(work[:, 4], pb[:, BANK_N], ACT.Sqrt, bias=eps_col[:]).then_inc(o_root, 1)
                    for b in range(B):
                        act.wait_ge(gate_sum, h * B + b + 1)
                        nc.scalar.activation(work[:, 6 + b], pb[:, GATE_BANKS[b]], ACT.Sigmoid,
                                             bias=cur[:, C_G2B:C_G2B + 1]).then_inc(gate_ready, 1)
                    tap(h + 1, 8)
                    tap(h + 1, 9)
                    silu(h + 1, 8)
                    silu(h + 1, 9)
                    act.drain().then_inc(rounds, 1)

            @block.vector
            def _(dve):
                nc.vector.memset(w_sb[:], 0.0)
                dve.drain().then_inc(cleared, 1)
                def convolve(g, t):
                    i = ORDER[t][1]
                    dve.wait_ge(tapped, g * TILES + t + 1)
                    acc = work[:, CONV + t % 2]
                    for s in range(1, 4):
                        last = nc.vector.scalar_tensor_tensor(
                            acc[:, s:T], pb[:, PROJ[t], 0:T - s], taps[:, 4 * i + 3 - s:4 * i + 4 - s],
                            acc[:, s:T], ALU.mult, ALU.add)
                        if s < 3:
                            dve.drain()
                    last.then_inc(convolved, 1)

                nc.vector.tensor_copy(taps[:], head_cols[:, 0, 0:12]).then_inc(taps_ready, 1)
                dve.drain()
                for t in range(AHEAD):
                    convolve(0, t)
                dve.drain().then_inc(rounds, 1)
                with dve.Fori(0, H) as h:
                    dve.wait_ge(rounds, 5 * h + 5)
                    nc.vector.tensor_copy(cur[:].unsqueeze(1), head_cols[:, bass.ds(h, 1), :]).then_inc(cur_ready, 1)
                    dve.drain()
                    for b in range(B):
                        dve.wait_ge(vh_squared, h * B + b + 1)
                        dve.wait_ge(silued, h * TILES + 2 * b + 2)
                        if b >= 2:
                            dve.wait_ge(stats, h * B + b - 1)
                        nc.vector.tensor_tensor(work[:, ERR + b % 2], bv[:, b, 0], pb[:, b % 2], ALU.subtract)
                        nc.vector.tensor_tensor(work[:, V_VH + b % 2], bv[:, b, 0], pb[:, b % 2], ALU.mult).then_inc(err_ready, 1)
                    dve.wait_ge(rooted, h + 1)
                    nc.vector.tensor_scalar(work[:, KN], work[:, KN], EPS, None, ALU.add)
                    nc.vector.tensor_scalar(work[:, RV], work[:, VN], EPS, None, ALU.add)
                    nc.vector.tensor_tensor(work[:, RVV], work[:, VN], work[:, VHN], ALU.mult)
                    dve.drain()
                    nc.vector.tensor_scalar(work[:, RVV], work[:, RVV], EPS, None, ALU.add)
                    nc.vector.reciprocal(work[:, RV], work[:, RV])
                    dve.drain()
                    nc.vector.reciprocal(work[:, RVV], work[:, RVV])
                    nc.vector.tensor_tensor(work[:, RV], work[:, EN], work[:, RV], ALU.mult)
                    dve.drain()
                    nc.vector.tensor_tensor(work[:, RVV], pb[:, 6], work[:, RVV], ALU.mult)
                    nc.vector.scalar_tensor_tensor(work[:, FEAT], work[:, RV], small[:, 1:2], ent_w[:], ALU.mult, ALU.add)
                    dve.drain()
                    nc.vector.scalar_tensor_tensor(work[:, FEAT], work[:, RVV], small[:, 2:3], work[:, FEAT],
                                                   ALU.mult, ALU.add)
                    dve.drain()
                    dve.wait_ge(l1p_ready, h + 1)
                    nc.vector.scalar_tensor_tensor(
                        work[:, FEAT], work[:, L1P], small[:, 3:4], work[:, FEAT], ALU.mult, ALU.add).then_inc(feat_ready, 1)
                    nc.vector.reciprocal(rnorm[:], work[:, KN]).then_inc(rnorm_ready, 1)
                    convolve(h, 10)
                    convolve(h, 11)
                    dve.drain()
                    nc.vector.tensor_copy(taps[:].unsqueeze(1), head_cols[:, bass.ds(h + 1, 1), 0:12]).then_inc(taps_ready, 1)

                    for bn, bp, bi, lv, bs, step in slots():
                        if bn is not None:
                            if step == P_NORM:
                                dve.wait_ge(piece_sum, h * 6 * B + 6 * bn + 1)
                                nc.vector.tensor_tensor(ks[:, bn, 0], ks[:, bn, 0],
                                                                         pb[:, BANK_N], ALU.mult).then_inc(piece_used, 1)
                            if step == 4:
                                dve.wait_ge(piece_used, h * 6 * B + 6 * bn + P_LAMBDA + 1)
                                query = nq[:, bn, SLOW, QUERY]
                                nc.vector.scalar_tensor_tensor(nq[:, bn, FAST, QUERY], query, Q_SCALE,
                                                               gates[:, P_LAMBDA - 1], ALU.mult, ALU.mult)
                                dve.drain()
                                nc.vector.scalar_tensor_tensor(query, query, Q_SCALE, nq[:, bn, FAST, QUERY],
                                                               ALU.mult, ALU.subtract)
                            if step == 5:
                                for rate in (SLOW, FAST):
                                    last = nc.vector.scalar_tensor_tensor(
                                        nq[:, bn, rate, NEG_K], ks[:, bn, 0], -1.0, gates[:, P_BETA_SLOW - 1 + rate],
                                        ALU.mult, ALU.mult)
                                last.then_inc(nq_ready, 1)
                        if bp is not None:
                            dve.drain()
                            dve.wait_ge(product, h * PS * B + PS * bp + step + 1)
                            if step == 0:
                                if bp >= 3:
                                    dve.wait_ge(o_sum, h * TT * B + TT * (bp - 2))
                                else:
                                    dve.wait_ge(hf_ready, h + 1)
                                nc.vector.tensor_tensor(
                                    apt[:, bp % 3, :, QUERY], products.rearrange("p r (c t) -> p (r c) t", c=TT),
                                    spread(ident[:].unsqueeze(1), [P, PAIRS, P]), ALU.mult).then_inc(kept, 1)
                                dve.wait_ge(e1_ready, h * B + bp + 1)
                                for rate in (SLOW, FAST):
                                    last = nc.vector.tensor_tensor(
                                        nq[:, bp, rate], nq[:, bp, rate],
                                        spread(e1[:, bp % 2, rate:rate + 1], [P, 2, T]), ALU.mult)
                                last.then_inc(nq_decayed, 1)
                            else:
                                level = step - 1
                                hs = 1 << level
                                level_products = products.rearrange("p r (c w t) -> p (r c) w t", c=TT, w=2)
                                level_mask = spread(compact(mask_u[:, level:level + 1], hs), [P, PAIRS, HALF // hs, hs])
                                dve.sem_inc(passed, 1)
                                nc.vector.copy_predicated(right(apt[:, bp % 3, :, QUERY], hs), level_mask,
                                                          compact(level_products[:, :, QUERY], hs))
                                blocks = tot_of(bp, level).rearrange("p (r s two) -> p r s two", r=2, two=2)
                                for rate in (SLOW, FAST):
                                    part = right(nq[:, bp, rate], hs)
                                    last = nc.vector.tensor_tensor(
                                        part, part, spread(blocks[:, rate:rate + 1, :, 0:1], [P, 2, T // (2 * hs), hs]),
                                        ALU.mult)
                                pairs = tot_of(bp, level).rearrange("p (s two) -> p s two", two=2)
                                nc.vector.tensor_tensor(tot_of(bp, level + 1), pairs[:, :, 0],
                                                                         pairs[:, :, 1], ALU.mult).then_inc(nq_decayed, 1)
                                if level == 0:
                                    dve.wait_ge(apt_zeroed, h * B + bp + 1)
                                else:
                                    dve.wait_ge(w_sum, h * IS * B + IS * bp + level)
                                dve.sem_inc(passed, 1)
                                nc.vector.copy_predicated(right(apt[:, bp % 3, :, NEG_K], hs), level_mask,
                                                          compact(level_products[:, :, NEG_K], hs)).then_inc(kept, 1)
                        if bs is not None and step % 2 == 1 and step < PS - 1:
                            c = step // 2
                            dve.wait_ge(s_sum, h * TT * B + TT * bs + c + 1)
                            for rate in (SLOW, FAST):
                                part = pb[:, BANK_S, rate * P:(rate + 1) * P]
                                if c == 0:
                                    last = nc.vector.tensor_copy(state[:, rate], part)
                                else:
                                    i = rate * TT + c
                                    last = nc.vector.scalar_tensor_tensor(
                                        state[:, rate], state[:, rate], tot_chunk[:, bs, i:i + 1], part,
                                        ALU.mult, ALU.add)
                            last.then_inc(state_ready, 1)
                        if bi is not None and lv == 0:
                            dve.wait_ge(xy_ready, h * B + bi + 1)
                            dve.wait_ge(w_sum, h * IS * B + IS * bi + 1)
                            dve.sem_inc(passed, 1)
                            dve.drain()
                            nc.vector.copy_predicated(
                                left(x_inv[:], 1), spread(compact(mask_l[:, 0:1], 1), [P, PAIRS, HALF, 1]),
                                compact(pb[:, BANK_W].rearrange("p (i t) -> p i t", i=PAIRS), 1))
                            nc.vector.copy_predicated(
                                right(y_inv[:, bi % 2], 1), spread(compact(mask_u[:, 0:1], 1), [P, PAIRS, HALF, 1]),
                                right(apt[:, bi % 3, :, NEG_K], 1)).then_inc(xy_grown, 1)
                        if bi is not None and lv:
                            hs = 1 << lv
                            dve.wait_ge(xy_sum, h * IW * B + IW * bi + lv)
                            dve.sem_inc(passed, 1)
                            if lv < IS - 1:
                                nc.vector.copy_predicated(
                                    left(x_inv[:], hs),
                                    spread(compact(mask_l[:, lv:lv + 1], hs), [P, PAIRS, HALF // hs, hs]),
                                    compact(pb[:, BANK_X].rearrange("p (i t) -> p i t", i=PAIRS), hs))
                            nc.vector.copy_predicated(
                                right(y_inv[:, bi % 2], hs),
                                spread(compact(mask_u[:, lv:lv + 1], hs), [P, PAIRS, HALF // hs, hs]),
                                compact(pb[:, BANK_Y].rearrange("p (i t) -> p i t", i=PAIRS), hs)).then_inc(xy_grown, 1)

                        if bp is None and bs is not None:
                            convolve(h + 1, step)

                    dve.wait_ge(o_root, h + 1)
                    nc.vector.reciprocal(work[:, 5], work[:, 4]).then_inc(o_rroot, 1)
                    convolve(h + 1, 8)
                    convolve(h + 1, 9)
                    for b in range(B):
                        dve.wait_ge(rroot_rows, h * B + b + 1)
                        nc.vector.scalar_tensor_tensor(o_t[:, b], o_t[:, b], small[:, 16:17], pb[:, ROW_BANKS[b]],
                                                       ALU.mult, ALU.mult)
                        dve.drain()
                        dve.wait_ge(gate_ready, h * B + b + 1)
                        nc.vector.tensor_tensor(o_t[:, b], o_t[:, b], work[:, 6 + b], ALU.mult).then_inc(o_ready, 1)
                    dve.drain().then_inc(rounds, 1)

            @block.gpsimd
            def _(pool):
                pool.sem_inc(rounds, 1)
                with pool.Fori(0, H) as h:
                    pool.wait_ge(rounds, 5 * h + 5)
                    pool.wait_ge(hf_ready, h + 1)
                    for bn, bp, bi, lv, bs, step in slots():
                        if bn is not None and step == 0:
                            pool.wait_ge(piece_used, h * 6 * B + 6 * bn + 1)
                            pool.sem_inc(passed, 1)
                            nc.gpsimd.tensor_copy(ks[:, bn, 1], ks[:, bn, 0]).then_inc(k_copied, 1)
                        if bp is not None and step == 0:
                            if bp >= 3:
                                pool.wait_ge(w_sum, h * IS * B + IS * (bp - 2))
                                pool.sem_inc(passed, 1)
                            nc.gpsimd.memset(apt[:, bp % 3, :, NEG_K], 0.0).then_inc(apt_zeroed, 1)
                            if bp >= 2:
                                pool.wait_ge(u_sum, h * TT * B + TT * (bp - 1))
                            if bp >= 1:
                                pool.wait_ge(w_sum, h * IS * B + IS * bp)
                            pool.sem_inc(passed, 1)
                            every = spread(ident[:].unsqueeze(1), [P, PAIRS, P])
                            nc.gpsimd.tensor_copy(x_inv[:], every)
                            nc.gpsimd.tensor_copy(y_inv[:, bp % 2], every).then_inc(xy_ready, 1)
                        if bp is not None and step >= 1:
                            level = step - 1
                            hs = 1 << level
                            pool.wait_ge(product, h * PS * B + PS * bp + step + 1)
                            pool.wait_ge(nq_decayed, h * PS * B + PS * bp + step)
                            if level:
                                pool.wait_ge(ks_decayed, h * LEVELS * B + LEVELS * bp + level)
                            part = left(ks[:, bp].rearrange("p r t -> p (r t)").unsqueeze(1), hs)[:, 0]
                            blocks = tot_of(bp, level).rearrange("p (s two) -> p s two", two=2)[:, :, 1:2]
                            nc.gpsimd.tensor_tensor(part, part, spread(blocks, [P, T // hs, hs]),
                                                                     ALU.mult).then_inc(ks_decayed, 1)
                        if bn is not None and step == 4:
                            pool.wait_ge(piece_used, h * 6 * B + 6 * bn + P_BETA_FAST + 1)
                            nc.gpsimd.tensor_tensor(bv[:, bn, FAST], bv[:, bn, SLOW], gates[:, P_BETA_FAST - 1], ALU.mult)
                            pool.drain()
                            nc.gpsimd.tensor_tensor(bv[:, bn, SLOW], bv[:, bn, SLOW],
                                                                   gates[:, P_BETA_SLOW - 1], ALU.mult).then_inc(bv_ready, 1)
                    pool.drain().then_inc(rounds, 1)


def norm_deviation(act, stats, eps_col, var_ready, dev_ready, due):
    act.wait_ge(var_ready, due)
    act.activation(stats[:, :, 6:7], stats[:, :, 7:8], ACT.Sqrt, bias=eps_col[:]).then_inc(dev_ready, 1)


def norm_rows(dve, sums, stats, out, var_ready, dev_ready, due):
    dve.drain()
    for i in range(sums.shape[1]):
        dve.bn_stats(stats[:, i, 0:6], sums[:, i])
    dve.drain()
    for i in range(sums.shape[1]):
        dve.bn_aggr(stats[:, i, 8:10], stats[:, i, 0:6])
    dve.drain()
    dve.tensor_copy(stats[:, :, 7:8], stats[:, :, 9:10]).then_inc(var_ready, 1)
    dve.wait_ge(dev_ready, due)
    dve.reciprocal(stats[:, :, 6:7], stats[:, :, 6:7])
    dve.drain()
    for i in range(sums.shape[1]):
        last = dve.tensor_scalar(out[:, i], sums[:, i], stats[:, i, 8:9], stats[:, i, 6:7],
                                 ALU.subtract, ALU.mult)
    return last


def block_stage(nc, io):
    with ExitStack() as ctx:
        def sb(name, shape, dt=F32):
            return ctx.enter_context(nc.sbuf_tensor("b_" + name, shape, dt))

        def sem(name):
            return ctx.enter_context(nc.semaphore("b_" + name))

        pb = ctx.enter_context(nc.psum_tensor("b_pb", [P, 8, 512], F32))
        GROUPS, GH = 4, H // 4
        NORMS = 2
        ident = sb("ident", [P, P])
        eps_col = sb("eps_col", [P, 1])
        w_o = sb("w_o", [P, H, D])
        o_t = sb("o_t", [P, GROUPS, GH, T])
        x_in = sb("x_in", [P, TT, D])
        y_in = sb("y_in", [P, ET, T])
        sums = sb("sums", [P, TT, D])
        x1 = sb("x1", [P, TT, D])
        gated = sb("gated", [P, TT, D])
        x2 = sb("x2", [P, TT, D])
        x2_t = sb("x2_t", [P, DC, T])
        stats = sb("stats", [P, TT, 10])

        weights = sem("weights")
        o_in = [sem(f"o_in{g}") for g in range(GROUPS)]
        o_used = [sem(f"o_used{g}") for g in range(GROUPS)]
        x_loaded = sem("x_loaded")
        y_loaded = sem("y_loaded")
        x_used = sem("x_used")
        y_used = sem("y_used")
        eps_ready = sem("eps_ready")
        attn_sum = sem("attn_sum")
        var_ready = sem("var_ready")
        dev_ready = sem("dev_ready")
        x1_ready = sem("x1_ready")
        silu_ready = sem("silu_ready")
        gated_ready = sem("gated_ready")
        turned = sem("turned")
        x2_ready = sem("x2_ready")
        x2_turned = sem("x2_turned")
        x2_t_ready = sem("x2_t_ready")
        x2_stored = sem("x2_stored")
        x2_t_stored = sem("x2_t_stored")

        with nc.Block() as block:

            @block.sync
            def _(sp):
                sp.dma_start(ident[:], io["ident"]).then_inc(weights, 16)
                sp.dma_start(w_o[:], io["w_o"]).then_inc(weights, 16)
                for s in (*o_used, x_used, y_used, x2_t_ready, x2_stored, x2_t_stored):
                    sp.sem_inc(s, 1)
                with sp.Fori(0, B) as b:
                    for g in range(GROUPS):
                        sp.wait_ge(o_used[g], b + 1)
                        sp.dma_start(
                            o_t[:, g], io["attn_o"][g * GH:(g + 1) * GH, :, bass.ds(b * T, T)].rearrange("h p t -> p h t")).then_inc(o_in[g], 16)
                    sp.wait_ge(x_used, b + 1)
                    sp.dma_start(x_in[:], io["x_rows"][b]).then_inc(x_loaded, 16)
                    sp.wait_ge(y_used, b + 1)
                    sp.dma_start(y_in[:], io["y_ssm"][b].rearrange("e p t -> p e t")).then_inc(y_loaded, 16)
                sp.wait_ge(x2_stored, 16 * B + 1)
                sp.wait_ge(x2_t_stored, 16 * B + 1)

            @block.tensor
            def _(pe):
                pe.wait_ge(weights, 32)

                def project(b, groups):
                    for g in groups:
                        pe.wait_ge(o_in[g], 16 * (b + 1))
                        for k in range(GH):
                            for tt in range(TT):
                                first, last = g + k == 0, g * GH + k == H - 1
                                mm = nc.tensor.matmul(pb[:, tt], o_t[:, g, k, tt * P:(tt + 1) * P],
                                                      w_o[:, g * GH + k], start=first, stop=last)
                        mm.then_inc(o_used[g], 1)

                def turn_gated(b):
                    pe.wait_ge(gated_ready, b + 1)
                    pe.wait_ge(x2_t_ready, b + 1)
                    for lt in range(TT):
                        for et in range(ET):
                            mm = nc.tensor.transpose(pb[:, 4 + lt, et * P:(et + 1) * P],
                                                     gated[:, et, lt * P:(lt + 1) * P], ident[:])
                    mm.then_inc(turned, 1)

                def turn_x2(b):
                    pe.wait_ge(x2_ready, b + 1)
                    for k in range(DC):
                        for lt in range(TT):
                            mm = nc.tensor.transpose(pb[:, 4 + k, lt * P:(lt + 1) * P],
                                                     x2[:, lt, k * P:(k + 1) * P], ident[:])
                    mm.then_inc(x2_turned, 1)

                project(0, range(GROUPS))
                pe.drain().then_inc(attn_sum, 1)
                with pe.Fori(0, B - 1) as b:
                    pe.wait_ge(x_used, b + 2)
                    project(b + 1, range(0, GROUPS // 2))
                    turn_gated(b)
                    project(b + 1, range(GROUPS // 2, GROUPS))
                    pe.drain().then_inc(attn_sum, 1)
                    turn_x2(b)
                turn_gated(B - 1)
                turn_x2(B - 1)

            @block.scalar
            def _(act):
                act.wait_ge(eps_ready, 1)
                with act.Fori(0, B) as b:
                    norm_deviation(act, stats, eps_col, var_ready, dev_ready, NORMS * b + 1)
                    act.wait_ge(x1_ready, b + 1)
                    nc.scalar.activation(gated[:], x1[:], ACT.Silu).then_inc(silu_ready, 1)
                    norm_deviation(act, stats, eps_col, var_ready, dev_ready, NORMS * b + 2)
                    act.wait_ge(x2_ready, b + 1)
                    act.dma_start(io["x2_rows"][b], x2[:]).then_inc(x2_stored, 16)
                    act.wait_ge(x2_turned, b + 1)
                    act.wait_ge(x2_t_stored, 16 * b + 1)
                    nc.scalar.copy(x2_t[:], pb[:, 4:4 + DC]).then_inc(x2_t_ready, 1)
                    act.wait_ge(x2_t_ready, b + 2)
                    act.dma_start(io["x2_t"][b], x2_t[:]).then_inc(x2_t_stored, 16)

            @block.vector
            def _(dve):
                nc.vector.memset(eps_col[:], NORM_EPS).then_inc(eps_ready, 1)
                with dve.Fori(0, B) as b:
                    dve.wait_ge(x_loaded, 16 * (b + 1))
                    dve.wait_ge(attn_sum, b + 1)
                    nc.vector.tensor_tensor(sums[:], x_in[:], pb[:, 0:TT], ALU.add).then_inc(x_used, 1)
                    norm_rows(dve, sums, stats, x1, var_ready, dev_ready, NORMS * b + 1).then_inc(x1_ready, 1)
                    dve.wait_ge(silu_ready, b + 1)
                    dve.wait_ge(y_loaded, 16 * (b + 1))
                    nc.vector.tensor_tensor(gated[:], y_in[:], gated[:], ALU.mult)
                    dve.drain().then_inc(y_used, 1)
                    dve.drain().then_inc(gated_ready, 1)
                    dve.wait_ge(x2_stored, 16 * b + 1)
                    dve.wait_ge(turned, b + 1)
                    nc.vector.tensor_tensor(sums[:], x1[:], pb[:, 4:8], ALU.add)
                    norm_rows(dve, sums, stats, x2, var_ready, dev_ready, NORMS * b + 2).then_inc(x2_ready, 1)
                    dve.drain()


SECOND = (1, 2, 3, 4, 5, 6, 0)


def mlp_stage(nc, io):
    with ExitStack() as ctx:
        def sb(name, shape, dt=F32):
            return ctx.enter_context(nc.sbuf_tensor("f_" + name, shape, dt))

        def sem(name):
            return ctx.enter_context(nc.semaphore("f_" + name))

        pb = ctx.enter_context(nc.psum_tensor("f_pb", [P, 8, 512], F32))
        ident = sb("ident", [P, P])
        eps_col = sb("eps_col", [P, 1])
        signs = sb("signs", [P, 2])
        before = sb("before", [P, E, E])
        w_gu = sb("w_gu", [P, 2, DC, DFF])
        w_d = sb("w_d", [P, FC, D])
        w_r = sb("w_r", [P, DC, E])
        a_gu = sb("a_gu", [P, 2, 2, DC, P])
        b_gu = sb("b_gu", [P, 2, 2, DFF])
        a_d = sb("a_d", [P, FC, E, 2 * R])
        b_d = sb("b_d", [P, D])
        x2_t = sb("x2_t", [P, DC, T])
        rank_rows = sb("rank_rows", [P, 2, 2, T])
        probs = sb("probs", [P, 8, TT, E])
        compare = sb("compare", [P, 2, TT, E * E])
        e_w = sb("e_w", [P, TT, P])
        e_w_t = sb("e_w_t", [P, T])
        gate = sb("gate", [P, 3, T])
        h_base = sb("h_base", [P, FC, T])
        h_lora = sb("h_lora", [P, 4, T])
        x2 = sb("x2", [P, TT, D])
        outs = sb("outs", [P, TT, D])
        down = sb("down", [P, T])
        stats = sb("stats", [P, TT, 10])
        DOWN, SCORES = 6, 7
        NORMS = 1

        items = []
        for first in range(0, FC, 3):
            group = range(first, min(first + 3, FC))
            for e in range(-1, E):
                items += [(e, c, c - first) for c in group]
        number = {(e, c): n for n, (e, c, _) in enumerate(items)}
        last_in = {}
        held = {}
        for n, (e, c, j) in enumerate(items):
            last_in[n] = held.get(j)
            held[j] = n
        lora_items = [n for n, (e, c, j) in enumerate(items) if e >= 0]
        NI, NL, LAG, RING = len(items), len(lora_items), 2, 4

        first_weights = sem("first_weights")
        base_weights = sem("base_weights")
        lora_weights = sem("lora_weights")
        last_weights = sem("last_weights")
        x2_t_in = sem("x2_t_in")
        x2_in = sem("x2_in")
        x2_t_used = sem("x2_t_used")
        eps_ready = sem("eps_ready")
        scores = sem("scores")
        shifted = sem("shifted")
        exped = sem("exped")
        e_w_ready = sem("e_w_ready")
        e_w_turned = sem("e_w_turned")
        e_w_t_ready = sem("e_w_t_ready")
        rank_sum = sem("rank_sum")
        rank_ready = sem("rank_ready")
        item_sum = sem("item_sum")
        gate_ready = sem("gate_ready")
        h_ready = sem("h_ready")
        down_sum = sem("down_sum")
        down_ready = sem("down_ready")
        out_sum = sem("out_sum")
        var_ready = sem("var_ready")
        dev_ready = sem("dev_ready")
        out_ready = sem("out_ready")
        stored = sem("stored")
        added = sem("added")
        passed = sem("passed")

        with nc.Block() as block:

            @block.sync
            def _(sp):
                sp.sem_inc(added, 1)
                sp.sem_inc(stored, 1)
                for dst, src in ((w_r, "w_r"), (a_gu, "a_gu"), (signs, "signs"), (ident, "ident"), (before, "before")):
                    sp.dma_start(dst[:], io[src]).then_inc(first_weights, 16)
                sp.dma_start(x2_t[:], io["x2_t"][0]).then_inc(x2_t_in, 16)
                sp.dma_start(x2[:], io["x2_rows"][0]).then_inc(x2_in, 16)
                for at in range(0, FC * P, 3 * P):
                    cols = slice(at, min(at + 3 * P, FC * P))
                    loaded = base_weights if at == 0 else last_weights
                    sp.dma_start(w_gu[:, :, :, cols], io["w_gu"][:, :, :, cols]).then_inc(loaded, 16)
                    if at == 0:
                        for dst, src in ((b_gu, "b_gu"), (a_d, "a_d")):
                            sp.dma_start(dst[:], io[src]).then_inc(lora_weights, 16)
                for dst, src in ((w_d, "w_d"), (b_d, "b_d")):
                    sp.dma_start(dst[:], io[src]).then_inc(last_weights, 16)
                with sp.Fori(1, B) as b:
                    sp.wait_ge(x2_t_used, b)
                    sp.dma_start(x2_t[:], io["x2_t"][b]).then_inc(x2_t_in, 16)
                    sp.wait_ge(added, b + 1)
                    sp.dma_start(x2[:], io["x2_rows"][b]).then_inc(x2_in, 16)
                    sp.wait_ge(out_ready, b)
                    sp.dma_start(io["out"][b - 1], outs[:]).then_inc(stored, 16)
                sp.wait_ge(out_ready, B)
                sp.dma_start(io["out"][B - 1], outs[:]).then_inc(stored, 16)
                sp.wait_ge(stored, 16 * B + 1)

            @block.tensor
            def _(pe):
                pe.wait_ge(first_weights, 16 * 5)
                with pe.Fori(0, B) as b:
                    pe.wait_ge(x2_t_in, 16 * (b + 1))
                    for tt in range(TT):
                        for k in range(DC):
                            mm = nc.tensor.matmul(pb[:, SCORES, tt * E:(tt + 1) * E], x2_t[:, k, tt * P:(tt + 1) * P],
                                                  w_r[:, k], start=(k == 0), stop=(k == DC - 1))
                    mm.then_inc(scores, 1)
                    pe.wait_ge(added, b + 1)
                    for n in range(4):
                        for k in range(DC):
                            mm = nc.tensor.matmul(pb[:, n], a_gu[:, n // 2, n % 2, k], x2_t[:, k],
                                                  start=(k == 0), stop=(k == DC - 1))
                        mm.then_inc(rank_sum, 1)
                    pe.wait_ge(rank_ready, b * 4 + 4)

                    def down_project(m):
                        n = lora_items[m]
                        e, c, _ = items[n]
                        pe.wait_ge(h_ready, b * NI + n + 1)
                        q = slice(32 * (e // 2), 32 * (e // 2) + 32)
                        nc.tensor.matmul(
                            pb[q, DOWN], a_d[:, c, e], h_lora[:, m % RING],
                            start=(c == 0 and e % 2 == 0), stop=(c == FC - 1 and e % 2 == 1), skip_group_check=True).then_inc(down_sum, 1)

                    m = 0
                    for n, (e, c, j) in enumerate(items):
                        if last_in[n] is not None:
                            pe.wait_ge(h_ready, b * NI + last_in[n] + 1)
                        if n == 0:
                            pe.wait_ge(base_weights, 16)
                        if n == 3:
                            pe.wait_ge(lora_weights, 16 * 2)
                        if n == number[-1, 3]:
                            pe.wait_ge(last_weights, 16 * 5)
                        cols = slice(c * P, (c + 1) * P)
                        for side in range(2):
                            out = pb[:, 2 * j + side]
                            if e < 0:
                                for k in range(DC):
                                    mm = nc.tensor.matmul(out, w_gu[:, side, k, cols], x2_t[:, k],
                                                          start=(k == 0), stop=(k == DC - 1), skip_group_check=True)
                            else:
                                arr, q = (1, 3) if e == 0 else (0, e // 2) if e % 2 else (1, e // 2 - 1)
                                q = slice(32 * q, 32 * q + 32)
                                mm = nc.tensor.matmul(out, b_gu[q, side, arr, cols], rank_rows[q, side, arr],
                                                      start=False, stop=True, skip_group_check=True)
                        mm.then_inc(item_sum, 1)
                        if n >= LAG and items[n - LAG][0] >= 0:
                            down_project(m)
                            m += 1
                        if n == 6:
                            pe.wait_ge(e_w_ready, b + 1)
                            for tt in range(TT):
                                mm = nc.tensor.matmul(pb[:, SCORES, tt * P:(tt + 1) * P], e_w[:, tt], ident[:],
                                                      start=True, stop=True)
                            mm.then_inc(e_w_turned, 1)
                    pe.drain().then_inc(x2_t_used, 1)
                    while m < NL:
                        down_project(m)
                        m += 1
                    pe.wait_ge(h_ready, b * NI + NI)
                    for tt in range(TT):
                        for c in range(FC):
                            nc.tensor.matmul(pb[:, tt], h_base[:, c, tt * P:(tt + 1) * P], w_d[:, c],
                                             start=(c == 0), stop=False)
                        if tt == 0:
                            pe.wait_ge(down_ready, b + 1)
                        mm = nc.tensor.matmul(pb[:, tt], down[:, tt * P:(tt + 1) * P], b_d[:],
                                              start=False, stop=True)
                    mm.then_inc(out_sum, 1)

            @block.scalar
            def _(act):
                act.wait_ge(first_weights, 16 * 5)
                act.wait_ge(eps_ready, 1)
                with act.Fori(0, B) as b:
                    for n in range(4):
                        act.wait_ge(rank_sum, b * 4 + n + 1)
                        nc.scalar.activation(rank_rows[:, n // 2, n % 2], pb[:, n], ACT.Copy,
                                                              scale=signs[:, n % 2:n % 2 + 1]).then_inc(rank_ready, 1)
                    act.wait_ge(shifted, b + 1)
                    nc.scalar.activation(probs[:, 1], probs[:, 0], ACT.Exp).then_inc(exped, 1)
                    for n, (e, c, j) in enumerate(items):
                        act.wait_ge(item_sum, b * NI + n + 1)
                        if n >= 3:
                            act.wait_ge(h_ready, b * NI + n - 2)
                        nc.scalar.activation(gate[:, n % 3], pb[:, 2 * j], ACT.Silu).then_inc(gate_ready, 1)
                        if n == 8:
                            act.wait_ge(e_w_turned, b + 1)
                            nc.scalar.activation(e_w_t[:], pb[:, SCORES], ACT.Copy, scale=LORA_SCALE).then_inc(e_w_t_ready, 1)
                    norm_deviation(act, stats, eps_col, var_ready, dev_ready, NORMS * b + 1)

            @block.vector
            def _(dve):
                nc.vector.memset(eps_col[:], NORM_EPS).then_inc(eps_ready, 1)
                dve.wait_ge(first_weights, 16 * 5)
                with dve.Fori(0, B) as b:
                    dve.wait_ge(scores, b + 1)
                    s = pb[:, SCORES, 0:TT * E].rearrange("p (t e) -> p t e", e=E)
                    nc.vector.tensor_reduce(probs[:, 2, :, 0], s, AX_X, ALU.max)
                    dve.drain()
                    nc.vector.tensor_tensor(probs[:, 0], s, spread(probs[:, 2, :, 0:1], [P, TT, E]),
                                                          ALU.subtract).then_inc(shifted, 1)
                    dve.wait_ge(exped, b + 1)
                    nc.vector.tensor_reduce(probs[:, 3, :, 0], probs[:, 1], AX_X, ALU.add)
                    dve.drain()
                    nc.vector.reciprocal(probs[:, 4, :, 0], probs[:, 3, :, 0])
                    dve.drain()
                    nc.vector.tensor_tensor(probs[:, 5], probs[:, 1], spread(probs[:, 4, :, 0:1], [P, TT, E]), ALU.mult)
                    dve.drain()
                    other = spread(probs[:, 5].unsqueeze(2), [P, TT, E, E])
                    own = spread(probs[:, 5].unsqueeze(3), [P, TT, E, E])
                    more = compare[:, 0].rearrange("p t (a c) -> p t a c", a=E)
                    same = compare[:, 1].rearrange("p t (a c) -> p t a c", a=E)
                    nc.vector.tensor_tensor(more, other, own, ALU.is_gt)
                    nc.vector.tensor_tensor(same, other, own, ALU.is_equal)
                    dve.drain()
                    nc.vector.tensor_tensor(compare[:, 1], compare[:, 1],
                                            spread(before[:].rearrange("p a c -> p (a c)").unsqueeze(1), [P, TT, E * E]),
                                            ALU.mult)
                    dve.drain()
                    nc.vector.tensor_tensor(more, more, same, ALU.add)
                    dve.drain()
                    nc.vector.tensor_reduce(probs[:, 6], more, AX_X, ALU.add)
                    dve.drain()
                    nc.vector.tensor_scalar(probs[:, 6], probs[:, 6], 1.5, None, ALU.is_lt)
                    dve.drain()
                    nc.vector.tensor_tensor(probs[:, 7], probs[:, 5], probs[:, 6], ALU.mult)
                    dve.drain()
                    nc.vector.tensor_copy(e_w[:].rearrange("p t (e r) -> p t e r", r=R),
                                                          spread(probs[:, 7].unsqueeze(3), [P, TT, E, R])).then_inc(e_w_ready, 1)
                    m = 0
                    for n, (e, c, j) in enumerate(items):
                        dve.wait_ge(gate_ready, b * NI + n + 1)
                        dst = h_base[:, c]
                        if e >= 0:
                            dst = h_lora[:, m % RING]
                            if m >= RING:
                                dve.wait_ge(down_sum, b * NL + m - RING + 1)
                            m += 1
                        nc.vector.tensor_tensor(dst, gate[:, n % 3], pb[:, 2 * j + 1], ALU.mult).then_inc(h_ready, 1)
                    dve.wait_ge(down_sum, b * NL + NL)
                    dve.wait_ge(e_w_t_ready, b + 1)
                    nc.vector.tensor_tensor(down[:], e_w_t[:], pb[:, DOWN], ALU.mult).then_inc(down_ready, 1)
                    dve.wait_ge(out_sum, b + 1)
                    dve.wait_ge(x2_in, 16 * (b + 1))
                    dve.wait_ge(stored, 16 * b + 1)
                    nc.vector.tensor_tensor(outs[:], x2[:], pb[:, 0:TT], ALU.add).then_inc(added, 1)
                    norm_rows(dve, outs, stats, outs, var_ready, dev_ready, NORMS * b + 1).then_inc(out_ready, 1)


def layouts(inputs, np):
    a = {k.replace("L0_", ""): np.asarray(v) for k, v in inputs.items()}

    def pack(x):
        return np.ascontiguousarray(x)

    def rows(x, n):
        return pack(x.reshape(n, P, -1).transpose(1, 0, 2))

    ident = np.eye(P, dtype=np.float32)
    out = {"ident": ident}
    out["ctx_t"] = pack(a["ctx_1024"].transpose(0, 2, 1).reshape(B, 2, P, T).transpose(0, 2, 1, 3))
    out["ssm_in_w"] = rows(a["xattn_in_proj_w"].T, 2)
    out["ssm_x_w"] = rows(a["xattn_x_proj_w"].T, ET)
    out["ssm_dt_w"] = pack(a["xattn_dt_proj_w"].T)
    out["ssm_cols"] = rows(np.concatenate([
        a["xattn_conv_w"], a["xattn_conv_b"][:, None], a["xattn_dt_proj_b"][:, None], a["xattn_D"][:, None],
        a["xattn_A_log"]], axis=1), ET)
    out["x_t"] = rows(a["x"].reshape(B * T, D).T, DC)
    out["g1"] = rows(a["attn_g1_w"], DC)
    out["unc"] = rows(a["attn_unc_w"], DC)
    out["proxy"] = pack(a["attn_proxy_w"])
    out["mlp_w2"] = pack(a["attn_mlp_w2"])
    out["w1_embed"] = pack(np.tile(a["attn_mlp_w1"][4:8], (1, B)))
    out["embed_t"] = pack(a["attn_head_embed"].T)
    out["small"] = pack(np.concatenate([
        np.tile(a["attn_mlp_w1"][0:4].T, (B, 1)),
        np.tile(np.stack([a["attn_mlp_b1"], a["attn_mlp_b2"]], 1), (B, 1)),
        np.tile(np.stack([a["attn_" + n + "_w"] for n in ("bb", "bd", "lam", "ab", "ad")], 1), (B, 1)),
        np.tile(np.stack([a["attn_" + n + "_b"] for n in ("bb", "bd", "lam", "ab", "ad")], 1), (P, 1)),
        a["attn_onorm_w"][:, None],
        np.tile(a["attn_A_log"][None, :], (P, 1)),
        a["attn_dt_bias"].reshape(H, P).T], axis=1))
    taps = [a["attn_conv_" + n + "_w"].reshape(H, P, 4) for n in "kvq"]
    out["head_cols"] = pack(np.concatenate(taps + [a["attn_g2_b"].reshape(H, P, 1)], axis=2).transpose(1, 0, 2))
    heads = np.stack([a["attn_w" + n].reshape(DC, P, H, P).transpose(2, 1, 0, 3) for n in "kvq"], axis=2)
    out["w_qkv"] = pack(np.concatenate([heads, np.zeros_like(heads[:1])]))
    out["g2"] = pack(a["attn_g2_w"].reshape(P, H, P).transpose(1, 0, 2))
    token = np.arange(P)[:, None]
    upper, lower = [], []
    for level in range(LEVELS):
        h = 1 << level
        block = (np.arange(HALF) // h)[None, :]
        upper.append((token // h == 2 * block).astype(np.int32))
        lower.append((token // h == 2 * block + 1).astype(np.int32))
    out["mask_u"] = pack(np.stack(upper, 1))
    out["mask_l"] = pack(np.stack(lower, 1))
    sel = np.zeros((P, P), np.float32)
    sel[::32] = 1.0
    out["sel"] = sel
    out["x_rows"] = pack(a["x"].reshape(B, TT, P, D).transpose(0, 2, 1, 3))
    out["w_o"] = rows(a["attn_wo"], H)
    out["w_gu"] = pack(np.stack([rows(a["ffn_W" + n].T, DC) for n in "gu"], 1))
    out["w_d"] = rows(a["ffn_Wd"].T, FC)
    out["w_r"] = rows(a["ffn_Wr"].T, DC)

    def second(x):
        return np.concatenate([x[list(SECOND)], np.zeros_like(x[:1])])

    def a_rows(x):
        return rows(x.reshape(E * R, D).T, DC)

    def b_rows(x):
        return x.transpose(0, 2, 1).reshape(E * R, -1)

    out["a_gu"] = pack(np.stack([np.stack([a_rows(a["ffn_A" + n]), a_rows(second(a["ffn_A" + n]))], 1)
                                 for n in "gu"], 1))
    out["b_gu"] = pack(np.stack([np.stack([b_rows(a["ffn_B" + n]), b_rows(second(a["ffn_B" + n]))], 1)
                                 for n in "gu"], 1))
    a_d = np.zeros((P, FC, E, 2, R), np.float32)
    for e in range(E):
        a_d[:, :, e, e % 2] = rows(a["ffn_Ad"][e].T, FC)
    out["a_d"] = pack(a_d.reshape(P, FC, E, 2 * R))
    out["b_d"] = pack(b_rows(a["ffn_Bd"]))
    signs = np.full((E, R, 2), LORA_SCALE, np.float32)
    signs[0::2, :, 0] = -LORA_SCALE
    signs[0:6:2, :, 1] = -LORA_SCALE
    out["signs"] = pack(signs.reshape(P, 2))
    out["before"] = pack(np.tile(np.tril(np.ones((E, E), np.float32), -1)[None], (P, 1, 1)))
    return out


def kernel(**inputs):
    import numpy as np
    import concourse.bacc as _bacc
    from concourse.bass_utils import run_bass_kernel_spmd as _run

    nc = _bacc.Bacc("TRN2", target_bir_lowering=False, num_devices=1)
    arrays = layouts(inputs, np)
    io = {n: nc.dram_tensor("in_" + n, a.shape, mybir.dt.from_np(a.dtype), kind="ExternalInput").ap()
          for n, a in arrays.items()}
    for name, shape in (("y_ssm", (B, ET, P, T)), ("attn_o", (H, P, B * T)), ("x2_rows", (B, P, TT, D)),
                        ("x2_t", (B, P, DC, T))):
        io[name] = nc.dram_tensor(name, shape, F32, kind="Internal").ap()
    io["out"] = nc.dram_tensor("out_0_dram", (B, P, TT, D), F32, kind="ExternalOutput").ap()
    ssm_stage(nc, io)
    attn_stage(nc, io)
    block_stage(nc, io)
    mlp_stage(nc, io)
    r = _run(nc, [{"in_" + n: a for n, a in arrays.items()}], core_ids=[0])
    out = r.results[0]["out_0_dram"]
    return np.ascontiguousarray(out.transpose(0, 2, 1, 3)).reshape(B, T, D)
```
